# Optimizing a Trainium2 kernel written in Bass

```python
import numpy as np
import jax
import jax.numpy as jnp

def _softmax(x, axis=-1):
    return jax.nn.softmax(x, axis=axis)

def _gelu(x):
    return jax.nn.gelu(x, approximate=True)

def _silu(x):
    return jax.nn.silu(x)

def _sigmoid(x):
    return jax.nn.sigmoid(x)

def _layernorm(x, axis=-1, eps=1e-05):
    m = jnp.mean(x, axis=axis, keepdims=True)
    v = jnp.var(x, axis=axis, keepdims=True)
    return (x - m) / jnp.sqrt(v + eps)

def _scatter_add(tgt, idx, src, axis=0):
    return tgt.at[idx].add(src)

def _segment_sum(src, seg, n):
    return jax.ops.segment_sum(src, seg, n)
kernel_name = 'mk_gnn_resnorm_d4_gnn_r32_8a8376'

def setup_inputs(seed: int=0):
    np.random.seed(seed)
    _w = jnp.asarray

    def _rec_inputs():
        import jax
        import jax.numpy as jnp
        _gk = jax.random.key(seed)
        x = -0.0002117 + 1 * jax.random.normal(jax.random.fold_in(_gk, 1), (3125, 256), jnp.float32)
        src = jax.random.randint(jax.random.fold_in(_gk, 2), (50000,), 0, 3125, jnp.int32)
        dst = jnp.minimum((3125 * jax.random.uniform(jax.random.fold_in(_gk, 3), (50000,)) ** 2.0).astype(jnp.int32), 99999)
        _o = jnp.argsort(dst, stable=True)
        src = src[_o]
        dst = dst[_o]
        edge_attr_64 = jax.random.uniform(jax.random.fold_in(_gk, 12), (50000, 64), jnp.float32, 0.0, 1)
        return (x, src, dst, edge_attr_64)
    x, src, dst, edge_attr_64 = _rec_inputs()

    def _L0_gnn_setup():
        import jax, jax.numpy as jnp
        import numpy as np
        N_NODES = 3125
        N_EDGES = 50000
        IN_DIM = 256
        OUT_DIM = 256
        key = jax.random.key(seed)
        k1, k2, k3 = jax.random.split(key, 3)
        x = jax.random.normal(k1, (N_NODES, IN_DIM), dtype=jnp.float32)
        limit = 0.1 * np.sqrt(6.0 / (IN_DIM + OUT_DIM))
        W = jax.random.uniform(k2, (OUT_DIM, IN_DIM), dtype=jnp.float32, minval=-limit, maxval=limit)
        b = jnp.zeros((OUT_DIM,), dtype=jnp.float32)
        edge_index = jax.random.randint(k3, (2, N_EDGES), 0, N_NODES, dtype=jnp.int64)
        return {'x': x, 'W': W, 'b': b, 'edge_index': edge_index}
    _L0_gnn_all = _L0_gnn_setup()
    _L0_gnn_in = {k: v for k, v in _L0_gnn_all.items() if k in ('W', 'b')}
    del _L0_gnn_all

    def _L1_gnn_setup():
        import jax, jax.numpy as jnp
        import numpy as np
        N_NODES = 50000
        N_EDGES = 25000
        DIM = 256
        N_LAYERS = 3
        LN_EPS = 1e-05

        def _gcn_norm(edge_index, n_nodes, dtype):
            row, col = (edge_index[0], edge_index[1])
            loop = jnp.arange(n_nodes, dtype=edge_index.dtype)
            row = jnp.concatenate([row, loop])
            col = jnp.concatenate([col, loop])
            deg = jax.ops.segment_sum(jnp.ones(row.shape[0], dtype=dtype), col, num_segments=n_nodes)
            dinv = jnp.where(deg > 0, jax.lax.rsqrt(deg), 0.0)
            norm = dinv[row] * dinv[col]
            return (row, col, norm)
        key = jax.random.key(seed)
        ks = jax.random.split(key, 6)
        x = jax.random.normal(ks[0], (N_NODES, DIM), dtype=jnp.float32)
        edge_index = jax.random.randint(ks[1], (2, N_EDGES), 0, N_NODES, dtype=jnp.int64)
        W = jax.random.normal(ks[2], (N_LAYERS, DIM, DIM), dtype=jnp.float32) * (1.0 / np.sqrt(DIM))
        b = jax.random.normal(ks[3], (N_LAYERS, DIM), dtype=jnp.float32) * 0.02
        gamma = jnp.ones((N_LAYERS, DIM), dtype=jnp.float32)
        beta = jnp.zeros((N_LAYERS, DIM), dtype=jnp.float32)
        return {'x': x, 'W': W, 'b': b, 'gamma': gamma, 'beta': beta, 'edge_index': edge_index}
    _L1_gnn_all = _L1_gnn_setup()
    _L1_gnn_in = {k: v for k, v in _L1_gnn_all.items() if k in ('W', 'b', 'gamma', 'beta')}
    del _L1_gnn_all

    def _L2_gnn_setup():
        import jax, jax.numpy as jnp
        import numpy as np
        N, E, HID, NRBF = (10000, 10000, 256, 64)
        key = jax.random.key(seed)
        ks = jax.random.split(key, 12)

        def lin(k, fin, fout):
            bound = 1.0 / np.sqrt(fin)
            kw, kb = jax.random.split(k)
            W = jax.random.uniform(kw, (fin, fout), jnp.float32, -bound, bound)
            b = jax.random.uniform(kb, (fout,), jnp.float32, -bound, bound)
            return (W, b)
        W1, b1 = lin(ks[0], NRBF, HID)
        W2, b2 = lin(ks[1], HID, HID)
        U1, c1 = lin(ks[2], 2 * HID, HID)
        U2, c2 = lin(ks[3], HID, HID)
        h = jax.random.normal(ks[4], (N, HID), jnp.float32)
        edge_index = jax.random.randint(ks[5], (2, E), 0, N, jnp.int64)
        rbf = jax.random.uniform(ks[6], (E, NRBF), jnp.float32)
        return {'h': h, 'edge_index': edge_index, 'rbf': rbf, 'W1': W1, 'b1': b1, 'W2': W2, 'b2': b2, 'U1': U1, 'c1': c1, 'U2': U2, 'c2': c2}
    _L2_gnn_all = _L2_gnn_setup()
    _L2_gnn_in = {k: v for k, v in _L2_gnn_all.items() if k in ('W1', 'b1', 'W2', 'b2', 'U1', 'c1', 'U2', 'c2')}
    del _L2_gnn_all

    def _L3_gnn_setup():
        import jax, jax.numpy as jnp
        import numpy as np
        N_NODES = 3125
        N_EDGES = 50000
        IN_DIM = 256
        HID = 64
        HEADS = 2
        OUT_DIM = 256
        NEG_SLOPE = 0.2
        key = jax.random.key(seed)
        ks = jax.random.split(key, 10)
        feat = jax.random.normal(ks[0], (N_NODES, IN_DIM), dtype=jnp.float32)
        src = jax.random.randint(ks[1], (N_EDGES,), 0, N_NODES)
        dst = jax.random.randint(ks[2], (N_EDGES,), 0, N_NODES)
        W = jax.random.normal(ks[3], (IN_DIM, HEADS * HID), dtype=jnp.float32) * 0.05
        attn_l = jax.random.normal(ks[4], (HEADS, HID), dtype=jnp.float32) * 0.05
        attn_r = jax.random.normal(ks[5], (HEADS, HID), dtype=jnp.float32) * 0.05
        gat_bias = jnp.zeros((HEADS * HID,), dtype=jnp.float32)
        lin_W = jax.random.normal(ks[6], (HEADS * HID, OUT_DIM), dtype=jnp.float32) * 0.05
        lin_b = jnp.zeros((OUT_DIM,), dtype=jnp.float32)
        return {'feat': feat, 'src': src, 'dst': dst, 'W': W, 'attn_l': attn_l, 'attn_r': attn_r, 'gat_bias': gat_bias, 'lin_W': lin_W, 'lin_b': lin_b}
    _L3_gnn_all = _L3_gnn_setup()
    _L3_gnn_in = {k: v for k, v in _L3_gnn_all.items() if k in ('W', 'attn_l', 'attn_r', 'gat_bias', 'lin_W', 'lin_b')}
    del _L3_gnn_all
    return {'x': x, 'src': src, 'dst': dst, 'edge_attr_64': edge_attr_64, 'L0_gnn_W': _L0_gnn_in['W'], 'L0_gnn_b': _L0_gnn_in['b'], 'L1_gnn_W': _L1_gnn_in['W'], 'L1_gnn_b': _L1_gnn_in['b'], 'L1_gnn_gamma': _L1_gnn_in['gamma'], 'L1_gnn_beta': _L1_gnn_in['beta'], 'L2_gnn_W1': _L2_gnn_in['W1'], 'L2_gnn_b1': _L2_gnn_in['b1'], 'L2_gnn_W2': _L2_gnn_in['W2'], 'L2_gnn_b2': _L2_gnn_in['b2'], 'L2_gnn_U1': _L2_gnn_in['U1'], 'L2_gnn_c1': _L2_gnn_in['c1'], 'L2_gnn_U2': _L2_gnn_in['U2'], 'L2_gnn_c2': _L2_gnn_in['c2'], 'L3_gnn_W': _L3_gnn_in['W'], 'L3_gnn_attn_l': _L3_gnn_in['attn_l'], 'L3_gnn_attn_r': _L3_gnn_in['attn_r'], 'L3_gnn_gat_bias': _L3_gnn_in['gat_bias'], 'L3_gnn_lin_W': _L3_gnn_in['lin_W'], 'L3_gnn_lin_b': _L3_gnn_in['lin_b']}

def reference(x, src, dst, edge_attr_64, L0_gnn_W, L0_gnn_b, L1_gnn_W, L1_gnn_b, L1_gnn_gamma, L1_gnn_beta, L2_gnn_W1, L2_gnn_b1, L2_gnn_W2, L2_gnn_b2, L2_gnn_U1, L2_gnn_c1, L2_gnn_U2, L2_gnn_c2, L3_gnn_W, L3_gnn_attn_l, L3_gnn_attn_r, L3_gnn_gat_bias, L3_gnn_lin_W, L3_gnn_lin_b):
    import jax
    import jax.numpy as jnp

    def _L0_gnn_ref(x, W, b, edge_index):
        import jax, jax.numpy as jnp
        import numpy as np
        N_NODES = 3125
        N_EDGES = 50000
        IN_DIM = 256
        OUT_DIM = 256
        num_nodes = x.shape[0]
        src, tgt = (edge_index[0], edge_index[1])
        xt = jnp.einsum('ni,oi->no', x, W) + b
        out = jax.ops.segment_sum(xt[src], tgt, num_segments=num_nodes)
        deg = jax.ops.segment_sum(jnp.ones_like(tgt, dtype=x.dtype), tgt, num_segments=num_nodes)
        out = out / (deg + 1.0)[:, None]
        return out

    def _L1_gnn_ref(x, W, b, gamma, beta, edge_index):
        import jax, jax.numpy as jnp
        import numpy as np
        N_NODES = 50000
        N_EDGES = 25000
        DIM = 256
        N_LAYERS = 3
        LN_EPS = 1e-05

        def _gcn_norm(edge_index, n_nodes, dtype):
            row, col = (edge_index[0], edge_index[1])
            loop = jnp.arange(n_nodes, dtype=edge_index.dtype)
            row = jnp.concatenate([row, loop])
            col = jnp.concatenate([col, loop])
            deg = jax.ops.segment_sum(jnp.ones(row.shape[0], dtype=dtype), col, num_segments=n_nodes)
            dinv = jnp.where(deg > 0, jax.lax.rsqrt(deg), 0.0)
            norm = dinv[row] * dinv[col]
            return (row, col, norm)
        n = x.shape[0]
        row, col, norm = _gcn_norm(edge_index, n, x.dtype)
        for i in range(N_LAYERS):
            h = x @ W[i]
            msg = h[row] * norm[:, None]
            h = jax.ops.segment_sum(msg, col, num_segments=n) + b[i]
            mu = jnp.mean(h, axis=-1, keepdims=True)
            var = jnp.mean((h - mu) ** 2, axis=-1, keepdims=True)
            h = (h - mu) * jax.lax.rsqrt(var + LN_EPS) * gamma[i] + beta[i]
            x = jax.nn.relu(h)
        return x

    def _L2_gnn_ref(h, edge_index, rbf, W1, b1, W2, b2, U1, c1, U2, c2):
        import jax, jax.numpy as jnp
        import numpy as np
        N, E, HID, NRBF = (10000, 10000, 256, 64)
        src, dst = (edge_index[0], edge_index[1])
        gate = jax.nn.sigmoid(jax.nn.silu(rbf @ W1 + b1) @ W2 + b2)
        msg = gate * h[src]
        aggr = jax.ops.segment_sum(msg, dst, num_segments=h.shape[0])
        upd = jax.nn.silu(jnp.concatenate([h, aggr], axis=-1) @ U1 + c1) @ U2 + c2
        return h + upd

    def _L3_gnn_ref(feat, src, dst, W, attn_l, attn_r, gat_bias, lin_W, lin_b):
        import jax, jax.numpy as jnp
        import numpy as np
        N_NODES = 3125
        N_EDGES = 50000
        IN_DIM = 256
        HID = 64
        HEADS = 2
        OUT_DIM = 256
        NEG_SLOPE = 0.2
        N = feat.shape[0]
        H, D = attn_l.shape
        h = (feat @ W).reshape(N, H, D)
        el = jnp.sum(h * attn_l[None], axis=-1)
        er = jnp.sum(h * attn_r[None], axis=-1)
        e = jax.nn.leaky_relu(el[src] + er[dst], NEG_SLOPE)
        m = jax.ops.segment_max(e, dst, num_segments=N)
        ee = jnp.exp(e - m[dst])
        s = jax.ops.segment_sum(ee, dst, num_segments=N)
        alpha = ee / s[dst]
        out = jax.ops.segment_sum(alpha[:, :, None] * h[src], dst, num_segments=N)
        out = out + gat_bias.reshape(1, H, D)
        out = jax.nn.relu(out.reshape(N, H * D))
        return jax.nn.relu(out @ lin_W + lin_b)
    edge_index = jnp.stack([src, dst])
    x = _layernorm(x + _L0_gnn_ref(x, L0_gnn_W, L0_gnn_b, edge_index), axis=-1)
    x = _layernorm(x + _L1_gnn_ref(x, L1_gnn_W, L1_gnn_b, L1_gnn_gamma, L1_gnn_beta, edge_index), axis=-1)
    x = _layernorm(x + _L2_gnn_ref(x, edge_index, edge_attr_64, L2_gnn_W1, L2_gnn_b1, L2_gnn_W2, L2_gnn_b2, L2_gnn_U1, L2_gnn_c1, L2_gnn_U2, L2_gnn_c2), axis=-1)
    x = _layernorm(x + _L3_gnn_ref(x, src, dst, L3_gnn_W, L3_gnn_attn_l, L3_gnn_attn_r, L3_gnn_gat_bias, L3_gnn_lin_W, L3_gnn_lin_b), axis=-1)
    return x

_drawn_inputs = setup_inputs


def setup_inputs(seed=0):
    import zlib

    import numpy as np

    out = dict(_drawn_inputs(seed))
    spreads = {'L0_gnn_b': (0.0, 0.1),
     'L1_gnn_gamma': (1.0, 0.2),
     'L1_gnn_beta': (0.0, 0.1),
     'L3_gnn_gat_bias': (0.0, 0.285),
     'L3_gnn_lin_b': (0.0, 0.1)}
    factors = {'edge_attr_64': 8.0,
     'L2_gnn_W1': 3.391,
     'L2_gnn_b1': 8.0,
     'L2_gnn_W2': 3.564,
     'L2_gnn_b2': 58.689,
     'L2_gnn_c1': 8.0,
     'L2_gnn_c2': 3.37,
     'L3_gnn_attn_l': 4.2,
     'L3_gnn_attn_r': 25.694}
    for name, (base, spread) in spreads.items():
        noise = np.random.default_rng([zlib.crc32(name.encode()), seed]).standard_normal(out[name].shape)
        drawn = base * np.exp(spread * noise) if base else spread * noise
        out[name] = jnp.asarray(drawn.astype(out[name].dtype))
    for name, factor in factors.items():
        out[name] = (out[name] * factor).astype(out[name].dtype)
    return out
```

```python
import numpy as np
import concourse.bass as bass
from concourse import mybir
from contextlib import ExitStack, nullcontext

F32, F16, BF16, I32, U32, I16, F8 = (mybir.dt.float32, mybir.dt.float16, mybir.dt.bfloat16, mybir.dt.int32,
                                     mybir.dt.uint32, mybir.dt.int16, mybir.dt.float8e4)
ALU = mybir.AluOpType
ACT = mybir.ActivationFunctionType
AX = mybir.AxisListType

N, E, D = 3125, 50000, 256
P = 125
NB = N // P
EC = E // P
ET = 128
U = 4
NT = -(-(E // ET + 1 + NB) // U) * U
EPAD = E + ET
AT = 64
BIG_DST = 4000.0
BANK = 512
FIELDS = 4
ROUND = 12582912.0


def index_tables(nc, ctx, dram, tab):
    with ExitStack() as c:
        sb = lambda n, s, d: c.enter_context(nc.sbuf_tensor(n, s, d))
        sem = lambda n: ctx.semaphore(n)
        src_i = sb("src_i", [P, EC], I32)
        dst_i = sb("dst_i", [P, EC], I32)
        dst_f = sb("dst_f", [P, EC], F32)
        row = sb("row", [P, EC, FIELDS], F32)
        tile = sb("tile", [P, EC], F32)
        below = sb("below", [P, EC], F32)
        cnt = sb("cnt", [P, NB + 1], F32)
        ones = sb("ones", [P, P], F32)
        padrow = sb("padrow", [1, FIELDS * ET], F32)
        padattr = sb("padattr", [ET, AT], F32)
        next_i = sb("next_i", [P, EC], I32)
        back = sb("back", [P, EC], F32)
        backs = sb("backs", [P, 1], F32)
        ps_start = c.enter_context(nc.psum_tensor("ps_start", [P, NB + 1], F32))
        ps_col = c.enter_context(nc.psum_tensor("ps_col", [NB, 2], F32))
        ps_t = c.enter_context(nc.psum_tensor("ps_t", [128, NT], F32))
        ps_e = c.enter_context(nc.psum_tensor("ps_e", [1, NT], F32))
        ps_tend = c.enter_context(nc.psum_tensor("ps_tend", [1, NB], F32))
        ps_back = c.enter_context(nc.psum_tensor("ps_back", [1, 1], F32))
        cntb = sb("cntb", [NB, 1], F32)
        ntb = sb("ntb", [NB, 1], F32)
        nti = sb("nti", [NB, 1], I32)
        delta = sb("delta", [NB, 1], F32)
        tendb = sb("tendb", [NB, 1], F32)
        ones25 = sb("ones25", [NB, 128], F32)
        tri25 = sb("tri25", [NB, NB], F32)
        eye25 = sb("eye25", [NB, NB], F32)
        iot = sb("iot", [NB, NT], F32)
        past = sb("past", [NB, NT], F32)
        dvals = sb("dvals", [NB, 1], F32)
        i128 = sb("i128", [1, NT], F32)
        e0f = sb("e0f", [1, NT], F32)
        ld, cst, cv, wr, hist, startp, colp, dl, tp, te = [sem("ix_" + n) for n in
            ("load", "const", "conv", "write", "hist", "startp", "colp", "delta", "tendp", "tend")]
        pa, tb, ch, tq = [sem("ix_" + n) for n in ("past", "tab", "chain", "tabp")]
        nextz, nextd, bk, bp, ck = [sem("ix_" + n) for n in ("next_zero", "next", "back", "backp", "rows")]
        with nc.Block() as block:
            @block.sync
            def _(sp):
                sp.dma_start(dst_i[:], dram["dst"].rearrange("(p c) -> p c", c=EC)).then_inc(ld, 16)
                sp.dma_start(src_i[:], dram["src"].rearrange("(p c) -> p c", c=EC)).then_inc(ld, 16)
                sp.wait_ge(nextz, 1)
                sp.dma_start(next_i[0:P - 1, :], dram["dst"][1:E - EC + 1].rearrange("(p c) -> p c", c=EC)).then_inc(nextd, 16)
                sp.dma_start(next_i[P - 1:P, 0:EC - 1], dram["dst"][E - EC + 1:E].rearrange("(p c) -> p c", p=1)).then_inc(nextd, 16)
                sp.wait_ge(cv, 1)
                sp.dma_start(dram["pairs"][0:E, :].rearrange("(p c) k -> p (c k)", c=EC),
                             row[:].rearrange("p c k -> p (c k)")).then_inc(wr, 16)
                sp.wait_ge(cst, 9)
                sp.dma_start(dram["pairs"][E:EPAD, :].rearrange("(a e) k -> a (e k)", a=1), padrow[:]).then_inc(wr, 16)
                sp.dma_start(dram["attr_s"][E:EPAD, :], padattr[:]).then_inc(wr, 16)
                sp.wait_ge(wr, 48)

            @block.gpsimd
            def _(g):
                g.memset(padattr[:], 0.0).then_inc(cst, 1)
                g.memset(ones[:], 1.0).then_inc(cst, 1)
                g.memset(ones25[:], 1.0).then_inc(cst, 1)
                g.memset(tri25[:], 1.0).then_inc(cst, 1)
                g.memset(eye25[:], 0.0).then_inc(cst, 1)
                g.memset(padrow[:], BIG_DST).then_inc(cst, 1)
                g.wait_ge(cst, 6)
                g.affine_select(out=tri25[:], in_=tri25[:], compare_op=ALU.is_ge, fill=0.0, base=0,
                                pattern=[[1, NB]], channel_multiplier=-1).then_inc(cst, 1)
                g.affine_select(out=eye25[:], in_=eye25[:], compare_op=ALU.not_equal, fill=1.0, base=0,
                                pattern=[[-1, NB]], channel_multiplier=1).then_inc(cst, 1)
                g.memset(padrow[:].rearrange("a (e k) -> a e k", k=FIELDS)[:, :, 0:1], 0.0).then_inc(cst, 1)
                g.iota(iot[:], pattern=[[1, NT]], base=0, channel_multiplier=0,
                       allow_small_or_imprecise_dtypes=True).then_inc(cst, 1)
                g.iota(i128[:], pattern=[[ET, NT]], base=0, channel_multiplier=0,
                       allow_small_or_imprecise_dtypes=True).then_inc(cst, 1)

            @block.vector
            def _(v):
                v.memset(next_i[:], 1 << 20).then_inc(nextz, 1)
                v.wait_ge(ld, 32)
                v.tensor_copy(row[:, :, 0], src_i[:])
                v.tensor_copy(row[:, :, 1], dst_i[:]).then_inc(ck, 1)
                v.wait_ge(ck, 1)
                v.tensor_scalar(tile[:], row[:, :, 0], -float(P // 2), 1.0 / P, ALU.add, ALU.mult).then_inc(ck, 1)
                v.wait_ge(ck, 2)
                v.tensor_scalar(tile[:], tile[:], ROUND, None, ALU.add).then_inc(ck, 1)
                v.wait_ge(ck, 3)
                v.tensor_scalar(tile[:], tile[:], -ROUND, float(P), ALU.add, ALU.mult).then_inc(ck, 1)
                v.wait_ge(ck, 4)
                v.tensor_tensor(row[:, :, 2], row[:, :, 0], tile[:], ALU.subtract)
                v.tensor_tensor(row[:, :, 3], row[:, :, 1], tile[:], ALU.add).then_inc(cv, 1)
                v.tensor_copy(dst_f[:], dst_i[:]).then_inc(ch, 1)
                v.wait_ge(ch, 1)
                for b in range(NB + 1):
                    if b:
                        v.wait_ge(hist, b)
                    v.tensor_scalar(below[:], dst_f[:], float(b * P), None, ALU.is_lt, ALU.add,
                                    accum_out=cnt[:, b:b + 1]).then_inc(hist, 1)
                v.wait_ge(nextd, 32)
                v.tensor_tensor(back[:], next_i[:], dst_i[:], ALU.is_lt).then_inc(bk, 1)
                v.wait_ge(bk, 1)
                v.tensor_reduce(backs[:], back[:], op=ALU.add, axis=AX.X).then_inc(bk, 1)
                v.wait_ge(bp, 1)
                v.tensor_scalar(tab["unsorted"][:], ps_back[:], 1.0, None, ALU.min)
                v.wait_ge(colp, 1)
                v.tensor_copy(dvals[:], ps_col[:, 0:1]).then_inc(ch, 1)
                v.wait_ge(ch, 2)
                v.tensor_tensor(cntb[:], ps_col[:, 1:2], dvals[:], ALU.subtract).then_inc(ch, 1)
                v.wait_ge(ch, 3)
                v.tensor_scalar(ntb[:], cntb[:], 63.5, 1.0 / ET, ALU.add, ALU.mult).then_inc(ch, 1)
                v.wait_ge(ch, 4)
                v.tensor_scalar(tendb[:], ntb[:], 8388608.0, None, ALU.add).then_inc(ch, 1)
                v.wait_ge(ch, 5)
                v.tensor_scalar(ntb[:], tendb[:], 8388608.0, 1.0, ALU.subtract, ALU.max).then_inc(ch, 1)
                v.wait_ge(ch, 6)
                v.tensor_scalar(delta[:], ntb[:], -float(ET), None, ALU.mult).then_inc(ch, 1)
                v.wait_ge(ch, 7)
                v.tensor_tensor(delta[:], delta[:], cntb[:], ALU.add).then_inc(dl, 1)
                v.wait_ge(tp, 1)
                v.tensor_copy(tab["tend"][:], ps_tend[:])
                v.memset(tab["tbeg"][:, 0:1], 0)
                v.tensor_copy(tab["tbeg"][:, 1:NB], ps_tend[:, 0:NB - 1])
                v.tensor_copy(tendb[:], ps_col[:, 0:1]).then_inc(ch, 1)
                v.wait_ge(ch, 8)
                v.wait_ge(cst, 11)
                v.tensor_scalar(past[:], iot[:], tendb[:], None, ALU.is_ge).then_inc(pa, 1)
                v.wait_ge(tq, 2)
                v.tensor_copy(tab["bucket"][:], ps_t[0:1, :])
                v.tensor_scalar(tab["first"][:], ps_t[:], float(P), None, ALU.mult)
                v.tensor_tensor(e0f[:], ps_e[:], i128[:], ALU.add).then_inc(ch, 1)
                v.wait_ge(ch, 9)
                v.tensor_scalar(tab["e0"][:], e0f[:], float(E), None, ALU.min).then_inc(tb, 1)
                v.wait_ge(tb, 1)

            @block.tensor
            def _(t):
                t.wait_ge(cst, 11)
                t.wait_ge(hist, NB + 1)
                t.wait_ge(bk, 2)
                nc.tensor.matmul(ps_back[:], backs[:], ones[:, 0:1], start=True, stop=True).then_inc(bp, 1)
                nc.tensor.matmul(ps_col[:, 0:1], cnt[:, 0:NB], ones[:, 0:1], start=True, stop=True)
                nc.tensor.matmul(ps_col[:, 1:2], cnt[:, 1:NB + 1], ones[:, 0:1], start=True, stop=True).then_inc(colp, 1)
                t.wait_ge(dl, 1)
                nc.tensor.matmul(ps_tend[:], ntb[:], tri25[:], start=True, stop=True)
                nc.tensor.matmul(ps_col[:, 0:1], tri25[:], ntb[:], start=True, stop=True).then_inc(tp, 1)
                t.wait_ge(pa, 1)
                nc.tensor.matmul(ps_t[:], ones25[:], past[:], start=True, stop=True).then_inc(tq, 1)
                nc.tensor.matmul(ps_e[:], delta[:], past[:], start=True, stop=True).then_inc(tq, 1)


class Semaphores:

    def __init__(self, nc):
        self.nc, self.held = nc, []

    def semaphore(self, name):
        self.held.append(self.nc.alloc_semaphore(name=name))
        return self.held[-1]

    def release(self):
        self.nc.all_engine_barrier()
        self.nc.clear_and_free_semaphores(self.held)
        self.nc.all_engine_barrier()


MOV = 4
GROUPS = [(g, min(MOV, NB - g)) for g in range(0, NB, MOV)]
NG = len(GROUPS)
UB = 16
OHR = 4


CAP = 15.0


def count_edges(nc, own, dram, tab, again):
    def chosen(eng):
        if not again:
            return nullcontext()
        return eng.If(eng.value_load(tab["dense"][0:1, 0:1], min_val=0, max_val=1) != 0)

    with ExitStack() as c:
        sb = lambda n, s, d=F32: c.enter_context(nc.sbuf_tensor(f"ct{again}_{n}", s, d))
        sem = lambda n: own.semaphore(f"ct{again}_{n}")
        X, counts = tab["X"], tab["counts"]
        parts = [t[:].bitcast(BF16).rearrange("p (b f) -> p b f", f=D) for t in tab["parts"][0:3]]
        iota = sb("iota", [ET, N], I16)
        oh_s = sb("oh_s", [ET, OHR, P], BF16)
        oh_k = sb("oh_k", [ET, OHR, N], BF16)
        zero = sb("zero", [ET, BANK], BF16)
        edge = sb("edge", [ET, UB, FIELDS])
        valid = sb("valid", [ET, UB])
        over = sb("over", [P, 2 * NB])
        over_sum = sb("over_sum", [P, 1])
        minus_cap = sb("minus_cap", [P, 1])
        by_lane = sb("by_lane", [P, NB, P])
        ones = sb("ones", [P, 1])
        if again:
            exact = sb("exact", [P, 2, MOV, P])
            beyond = sb("beyond", [P, 2, MOV, P])
        else:
            rest = sb("rest", [P, 2, D])
            tree = sb("tree", [P, NB // 2, P])
            junk = sb("junk", [P, NB - NB // 2, P], BF16)
        acc = c.enter_context(nc.psum_tensor(f"ct{again}_acc", [P, NG, BANK], F32))
        ps_end = c.enter_context(nc.psum_tensor(f"ct{again}_end", [P, NB + 1], F32))
        edge_in = [sem(f"edge{j}") for j in range(UB)]
        const, onehot, pe_done, validd, x_in, part, restd, attr_copied, treed, laned, overd, endd = map(sem, (
            "const", "onehot", "pe", "valid", "x_in", "part", "rest", "attr_copied", "tree", "laned", "over", "end"))
        exactd, clipped, beyondd = map(sem, ("exact", "clipped", "beyond"))
        beyond_out = [sem("beyond_out0"), sem("beyond_out1")]
        bank_sum = [sem(f"sum{g}") for g in range(NG)]
        bank_out = [sem(f"bank{g}") for g in range(NG)]
        NCONST = 5

        def load_edges(sp):
            def load(t, j, first):
                e0 = sp.value_load(tab["e0"][0:1, bass.ds(t, 1)], min_val=0, max_val=E)
                if not first:
                    sp.wait_ge(onehot, t - (UB - 1))
                sp.dma_start(edge[:, j, :], dram["pairs"][bass.ds(e0, ET), :]).then_inc(edge_in[j], 16)
            for j in range(UB):
                load(j, j, True)
            if not again:
                sp.dma_start(X[:], dram["x"].rearrange("(b p) f -> p b f", p=P)).then_inc(x_in, 16)
            with sp.Fori(1, NT // UB) as i:
                for j in range(UB):
                    load(i * UB + j, j, False)

        def onehot_rows(v):
            v.wait_ge(const, NCONST)

            def onehots(t, j, i, first):
                v.wait_ge(edge_in[j], i * 16 + 16)
                if not first:
                    v.wait_ge(pe_done, t - (OHR - 1))
                r = j % OHR
                begins = tab["first"][:, bass.ds(t, 1)]
                v.tensor_scalar(valid[:, j:j + 1], edge[:, j, 1:2], begins, P - 0.5, ALU.subtract, ALU.is_le).then_inc(validd, 1)
                v.tensor_scalar(oh_k[:, r, :], iota[:], begins, edge[:, j, 3:4], ALU.add, ALU.is_equal)
                v.wait_ge(validd, t + 1)
                v.tensor_scalar(oh_s[:, r, :], iota[:, 0:P], edge[:, j, 2:3], valid[:, j:j + 1], ALU.is_equal,
                                ALU.mult).then_inc(onehot, 1)
            for j in range(UB):
                onehots(j, j, 0, j < OHR)
            with v.Fori(1, NT // UB) as i:
                for j in range(UB):
                    onehots(i * UB + j, j, i, False)
            if not again:
                v.wait_ge(overd, 2 * NB)
                v.tensor_reduce(over_sum[:], over[:], op=ALU.add, axis=AX.X).then_inc(overd, 1)
            v.wait_ge(endd, 1)
            if not again:
                v.tensor_scalar(tab["dense"][:], ps_end[0:1, NB:NB + 1], 1.0, None, ALU.min)
            v.tensor_copy(tab["deg"][:], ps_end[:, 0:NB])

        def count(pe):
            pe.wait_ge(const, NCONST)

            def product(g, k, lhs, rhs, start, stop):
                return nc.tensor.matmul(acc[0:P, g, 0:k * P], lhs, rhs, start=start, stop=stop)

            end = pe.value_load(tab["tend"][0:1, NB - 1:NB], min_val=NB, max_val=NT - 1)
            with pe.Fori(0, NB) as b:
                lo = pe.value_load(tab["tbeg"][0:1, bass.ds(b, 1)], min_val=0, max_val=NT - 2)
                hi = pe.value_load(tab["tend"][0:1, bass.ds(b, 1)], min_val=1, max_val=NT - 1)
                def tile(t, begin, end_):
                    pe.wait_ge(onehot, t + 1)
                    r = t % OHR
                    for g, (s0, k) in enumerate(GROUPS):
                        if begin:
                            pe.wait_ge(bank_out[g], b + 1)
                        last = product(g, k, oh_s[:, bass.ds(r, 1), :].rearrange("p a n -> p (a n)"),
                                       oh_k[:, bass.ds(r, 1), s0 * P:(s0 + k) * P].rearrange("p a n -> p (a n)"),
                                       begin, end_)
                        if end_:
                            last.then_inc(bank_sum[g], 1)
                    if end_:
                        pe.wait_ge(bank_sum[NG - 1], b + 1)
                        pe.sem_inc(pe_done, 1)
                    else:
                        last.then_inc(pe_done, 1)

                with pe.If(hi == lo + 1):
                    tile(lo, True, True)
                with pe.If(hi > lo + 1):
                    tile(lo, True, False)
                    with pe.If(hi > lo + 2):
                        with pe.Fori(lo + 1, hi - 1) as t:
                            tile(t, False, False)
                    tile(hi - 1, False, True)
            pe.wait_ge(const, NCONST)
            pe.wait_ge(pe_done, end)
            with pe.Fori(end, NT) as t:
                pe.wait_ge(onehot, t + 1)
                pe.sem_inc(pe_done, 1)
            pe.wait_ge(laned, NB * NB if again else NB)
            for b in range(NB):
                m = nc.tensor.matmul(ps_end[:, b:b + 1], by_lane[:, b, :], ones[:], start=True, stop=True)
            if not again:
                pe.wait_ge(overd, 2 * NB + 1)
                m = nc.tensor.matmul(ps_end[0:1, NB:NB + 1], over_sum[:], ones[:], start=True, stop=True)
            m.then_inc(endd, 1)

        def constants(g):
            g.iota(iota[:], pattern=[[1, N]], base=0, channel_multiplier=0).then_inc(const, 1)
            g.memset(zero[:], 0.0).then_inc(const, 1)
            g.memset(ones[:], 1.0).then_inc(const, 1)
            g.memset(minus_cap[:], -CAP).then_inc(const, 1)
            g.memset(by_lane[:], 0.0).then_inc(const, 1)

        def sum_tiles(g):
            g.wait_ge(const, NCONST)
            n = [0]

            def link(ins):
                n[0] += 1
                ins.then_inc(treed, 1)
                g.wait_ge(treed, n[0])

            for b in range(NB):
                for i in range(NG):
                    g.wait_ge(bank_out[i], b + 2)
                link(g.tensor_tensor(tree[:], counts[:, b, 0:12, 0:P], counts[:, b, 12:24, 0:P], ALU.add))
                for w in (6, 3):
                    link(g.tensor_tensor(tree[:, 0:w, :], tree[:, 0:w, :], tree[:, w:2 * w, :], ALU.add))
                link(g.tensor_tensor(tree[:, 0, :], tree[:, 0, :], tree[:, 1, :], ALU.add))
                link(g.tensor_tensor(tree[:, 2, :], tree[:, 2, :], counts[:, b, 24, 0:P], ALU.add))
                g.tensor_tensor(by_lane[:, b, :], tree[:, 0, :], tree[:, 2, :], ALU.add).then_inc(laned, 1)
                g.wait_ge(laned, b + 1)

        def clip_and_store(g):
            g.wait_ge(const, NCONST)
            for b in range(NB):
                for i, (s0, k) in enumerate(GROUPS):
                    m = b * NG + i
                    q = m % 2
                    g.wait_ge(exactd, m + 1)
                    need(g, beyond_out[q], 16 * (m // 2))
                    g.tensor_scalar(beyond[:, q, 0:k, :], exact[:, q, 0:k, :], -CAP, 0.0, ALU.add, ALU.max).then_inc(beyondd, 1)
                    g.wait_ge(beyondd, m + 1)
                    g.tensor_tensor(counts[:, b, s0:s0 + k, 0:P], exact[:, q, 0:k, :], beyond[:, q, 0:k, :],
                                    ALU.subtract, saturate=False)
                    for j in range(k):
                        step = g.tensor_tensor(by_lane[:, b, :], by_lane[:, b, :], exact[:, q, j, :], ALU.add)
                        step.then_inc(laned, 1)
                        g.wait_ge(laned, b * NB + s0 + j + 1)
                    g.sem_inc(clipped, 1)
                    g.dma_start(dram["beyond"][b, :, s0 * P:(s0 + k) * P],
                                beyond[:, q, 0:k, :].rearrange("p k d -> p (k d)")).then_inc(beyond_out[q], 16)
            for q in range(2):
                g.wait_ge(beyond_out[q], 16 * ((NB * NG + 1 - q) // 2))

        with nc.Block() as block:
            @block.sync
            def _(sp):
                with chosen(sp):
                    load_edges(sp)

            @block.gpsimd
            def _(g):
                with chosen(g):
                    constants(g)
                    if again:
                        clip_and_store(g)
                if again:
                    return
                unsorted = g.value_load(tab["unsorted"][0:1, 0:1], min_val=0, max_val=1)
                with g.If(unsorted == 0):
                    g.dma_start(dram["attr_s"][0:E, :].rearrange("(a e) f -> a (e f)", a=400),
                                dram["edge_attr_64"].rearrange("(a e) f -> a (e f)", a=400)).then_inc(attr_copied, 16)
                    g.wait_ge(attr_copied, 16)
                for b in range(NB):
                    g.wait_ge(part, 3 * b + 1)
                    g.tensor_tensor(rest[:, 0, :], X[:, b, :], parts[0][:, b, :], ALU.subtract).then_inc(restd, 1)
                    g.wait_ge(part, 3 * b + 2)
                    g.wait_ge(restd, 2 * b + 1)
                    g.tensor_tensor(rest[:, 1, :], rest[:, 0, :], parts[1][:, b, :], ALU.subtract).then_inc(restd, 1)
                sum_tiles(g)

            @block.vector
            def _(v):
                with chosen(v):
                    onehot_rows(v)

            @block.tensor
            def _(pe):
                with chosen(pe):
                    count(pe)

            @block.scalar
            def _(a):
                with chosen(a):
                    for g in range(NG):
                        a.sem_inc(bank_out[g], 1)
                    if not again:
                        a.wait_ge(x_in, 16)
                        a.wait_ge(const, NCONST)
                        for b in range(NB):
                            a.copy(parts[0][:, b, :], X[:, b, :]).then_inc(part, 1)
                            for n in (1, 2):
                                a.wait_ge(restd, 2 * b + n)
                                a.copy(parts[n][:, b, :], rest[:, n - 1, :]).then_inc(part, 1)
                    for b in range(NB):
                        for g, (s0, k) in enumerate(GROUPS):
                            m = b * NG + g
                            a.wait_ge(bank_sum[g], b + 1)
                            sums = acc[0:P, g, 0:k * P].rearrange("p (k d) -> p k d", d=P)
                            if again:
                                need(a, clipped, m - 1)
                                a.copy(exact[:, m % 2, 0:k, :], sums).then_inc(exactd, 1)
                                a.wait_ge(exactd, m + 1)
                                a.sem_inc(bank_out[g], 1)
                            else:
                                a.copy(counts[:, b, s0:s0 + k, 0:P], sums, saturate=True).then_inc(bank_out[g], 1)
                        if not again:
                            for g in range(NG):
                                a.wait_ge(bank_out[g], b + 2)
                            for half, tiles in enumerate((slice(0, NB // 2), slice(NB // 2, NB))):
                                m = 2 * b + half
                                need(a, overd, m)
                                a.activation(junk[:, 0:tiles.stop - tiles.start, :], counts[:, b, tiles, 0:P], ACT.Relu,
                                             bias=minus_cap[:], accum_out=over[:, m:m + 1]).then_inc(overd, 1)


def node_scales(nc, ctx, dram, tab, rows):
    sem = lambda n: ctx.semaphore("ns_" + n)
    loaded, ch, rooted, split = map(sem, ("loaded", "chain", "rooted", "split"))
    with ExitStack() as c, nc.Block() as block:
        sb = lambda n, s, d: c.enter_context(nc.sbuf_tensor(n, s, d))
        absg = sb("absg", [P, 2, D], F32)
        absb = sb("absb", [P, 2, D], F32)
        colg = sb("colg", [128, 2, 2], F32)
        colb = sb("colb", [128, 2, 2], F32)
        root = sb("root", [P, NB], F32)
        deg1 = sb("deg1", [P, NB], F32)

        @block.sync
        def _(sp):
            for n in ("b", "gamma", "beta"):
                for l in range(3):
                    sp.dma_start(rows[n][:, l, :], dram["L1_gnn_" + n][l].partition_broadcast(P)).then_inc(loaded, 16)
            with nc.allow_non_contiguous_dma(reason="512 numbers, once"):
                for l in range(2):
                    sp.dma_start(colg[:, l, :], dram["L1_gnn_gamma"][l].rearrange("(h p) -> p h", h=2)).then_inc(loaded, 16)
                    sp.dma_start(colb[:, l, :], dram["L1_gnn_beta"][l].rearrange("(h p) -> p h", h=2)).then_inc(loaded, 16)

        @block.scalar
        def _(a):
            a.wait_ge(ch, 1)
            a.activation(root[:], deg1[:], ACT.Sqrt).then_inc(rooted, 1)

        @block.vector
        def _(v):
            n = [0]

            def link(ins):
                n[0] += 1
                ins.then_inc(ch, 1)
                v.wait_ge(ch, n[0])

            link(v.tensor_scalar(deg1[:], tab["deg"][:], 1.0, None, ALU.add))
            link(v.reciprocal(tab["mean"][:], deg1[:]))
            link(v.tensor_tensor(tab["degmean"][:], tab["mean"][:], tab["deg"][:], ALU.mult))
            v.wait_ge(rooted, 1)
            link(v.reciprocal(tab["dinv"][:], root[:]))
            link(v.tensor_scalar(tab["dinv_x"][:], tab["dinv"][:], 128.0, None, ALU.mult))
            v.wait_ge(loaded, 16 * 13)
            for g_, b_, out in ((rows["gamma"][:, 0:2, :], rows["beta"][:, 0:2, :], None),
                                (colg[:], colb[:], tab["unscale"])):
                ag, ab = (absg[:], absb[:]) if out is None else (colg[:], colb[:])
                link(v.scalar_tensor_tensor(ag, g_, -1.0, g_, ALU.mult, ALU.max))
                link(v.scalar_tensor_tensor(ab, b_, -1.0, b_, ALU.mult, ALU.max))
                link(v.scalar_tensor_tensor(ag, ag, 16.0, ab, ALU.mult, ALU.add))
                link(v.tensor_scalar(out[:] if out is not None else ag, ag, 1.0 / 2048, 1e-30, ALU.mult, ALU.max))
            link(v.reciprocal(absb[:], absg[:]))
            link(v.tensor_tensor(rows["gamma"][:, 0:2, :], rows["gamma"][:, 0:2, :], absb[:], ALU.mult))
            link(v.tensor_tensor(rows["beta"][:, 0:2, :], rows["beta"][:, 0:2, :], absb[:], ALU.mult))


def conv_layer(nc, ctx, dram, tab, rows, L):
    with ExitStack() as c:
        sb = lambda n, s, d: c.enter_context(nc.sbuf_tensor(f"{n}_{L}", s, d))
        sem = lambda n: ctx.semaphore(f"l{L}_{n}")
        Q = tab["parts"]
        if L == 0:
            parts = [t[:].bitcast(BF16).rearrange("p (b f) -> p b f", f=D) for t in Q[0:3]]
            nxt = Q[3:5]
        else:
            parts, nxt = (Q[3:5], Q[0:2]) if L % 2 else (Q[0:2], Q[3:5])
            parts = [t[:].rearrange("p (b f) -> p b f", f=D) for t in parts]
        nxt = [t[:].rearrange("p (b f) -> p b f", f=D) for t in nxt]
        C, X = tab["counts"], tab["X"]
        last_layer = L == 3
        W = sb("W", [128, 2, D], F32)
        yt = sb("yt", [128, 2, 2, MOV * P], F32)
        a_ = sb("a", [P, MOV, D], F32)
        st = sb("st", [P, MOV, 6], F32)
        mv = sb("mv", [P, MOV, 2], F32)
        rs = sb("rs", [P, MOV], F32)
        nm = sb("nm", [P, MOV], F32)
        eps = sb("eps", [P, 1], F32)
        if L:
            tmp = sb("tmp", [P, MOV, D], F32)
        beyond = sb("beyond", [P, MOV, P], F32)
        whole = sb("whole", [P, MOV, P], F32)
        digits = sb("digits", [P, 2, MOV, P], F16 if L else BF16)
        pb = lambda n, s: c.enter_context(nc.psum_tensor(f"{n}_{L}", s, F32))
        py = pb("py", [128, 2, 2, BANK])
        po = pb("po", [P, 2, MOV, D])
        w_in, summed, y_out, projected, o_out = map(sem, ("w_in", "summed", "y_out", "projected", "o_out"))
        vch, stats, rooted, centred, affine, last_stats, relued, high, low, stored, epsd = map(sem, (
            "vchain", "stats", "rooted", "centred", "affine", "last_stats", "relued", "high", "low", "stored", "eps"))
        pch = sem("pchain")
        beyond_in, digit_steps, digits_done, digits_used, digits_seen = map(sem, (
            "beyond_in", "digit_steps", "digits", "digits_used", "digits_seen"))

        def if_dense(eng):
            return eng.If(eng.value_load(tab["dense"][0:1, 0:1], min_val=0, max_val=1) != 0)

        with nc.Block() as block:
            if L == 0:
                wt = sb("wt", [128, 2, D], F32)
                b0 = sb("b0", [P, D], F32)
                eye = sb("eye", [128, 128], F32)
                eyed, turned = sem("eye"), sem("turned")

            @block.sync
            def _(sp):
                if L == 0:
                    sp.dma_start(wt[:], dram["L0_gnn_W"].rearrange("(h p) i -> p h i", p=128)).then_inc(w_in, 16)
                    sp.dma_start(b0[:], dram["L0_gnn_b"].partition_broadcast(P)).then_inc(w_in, 16)
                else:
                    sp.dma_start(W[:], dram["L1_gnn_W"][L - 1].rearrange("(h p) o -> p h o", p=128)).then_inc(w_in, 16)
                with if_dense(sp):
                    for g, (s0, k) in enumerate(GROUPS):
                        with sp.Fori(0, NB) as i:
                            sp.wait_ge(digits_done, i + (g * NB + 1))
                            sp.dma_start(beyond[:, 0:k, :], dram["beyond"][s0:s0 + k, :, bass.ds(i * P, P)]
                                         .rearrange("b p d -> p b d")).then_inc(beyond_in, 16)
                if last_layer:
                    sp.wait_ge(low, NG)
                    sp.dma_start(dram["table"].rearrange("(b p) f -> p b f", p=P), X[:]).then_inc(stored, 16)
                    sp.wait_ge(stored, 16)

            @block.tensor
            def _(pe):
                if L == 0:
                    pe.wait_ge(eyed, 2)
                    pe.wait_ge(w_in, 32)
                    for i in range(2):
                        for o in range(2):
                            last = nc.tensor.transpose(py[:, i, o, 0:128], wt[:, o, i * 128:(i + 1) * 128], eye[:])
                    last.then_inc(turned, 1)
                    pe.wait_ge(y_out, 1)
                else:
                    pe.wait_ge(w_in, 16)
                base = 1 if L == 0 else 0

                def sums(g):
                    s0, k = GROUPS[g]
                    if g >= 2:
                        pe.wait_ge(y_out, base + 2 * (g - 1))

                    def step(i, first, last):
                        for h in range(2):
                            for n, part in enumerate(parts):
                                m = nc.tensor.matmul(
                                    py[:, g % 2, h, 0:k * P],
                                    part[:, i, h * 128:(h + 1) * 128],
                                    C[:, s0:s0 + k, i, 0:P],
                                    start=first and n == 0, stop=last and n == len(parts) - 1)
                            if last:
                                m.then_inc(summed, 1)
                    def beyond_step(i):
                        pe.wait_ge(digits_done, i + (g * NB + 2))
                        for h in range(2):
                            for n, part in enumerate(parts):
                                for d in range(2):
                                    m = nc.tensor.matmul(
                                        py[:, g % 2, h, 0:k * P],
                                        part[:, bass.ds(i, 1), h * 128:(h + 1) * 128].rearrange("p a f -> p (a f)"),
                                        digits[:, d, 0:k, :].rearrange("p k d -> p (k d)"),
                                        start=False, stop=False)
                        m.then_inc(digits_used, 1)

                    step(0, True, False)
                    for i in range(1, NB - 1):
                        step(i, False, False)
                    with if_dense(pe):
                        with pe.Fori(0, NB) as i:
                            beyond_step(i)
                    step(NB - 1, False, True)

                def project(g):
                    s0, k = GROUPS[g]
                    pe.wait_ge(y_out, base + 2 * (g + 1))
                    if g >= 2:
                        pe.wait_ge(o_out, g - 1)
                    for j in range(k):
                        for h in range(2):
                            m = nc.tensor.matmul(po[:, g % 2, j, :], yt[:, g % 2, h, j * P:(j + 1) * P], W[:, h, :],
                                                 start=h == 0, stop=h == 1)
                    m.then_inc(projected, 1)

                sums(0)
                for g in range(1, NG):
                    sums(g)
                    project(g - 1)
                project(NG - 1)

            @block.gpsimd
            def _(g_):
                g_.memset(eps[:], 1e-5).then_inc(epsd, 1)
                if L == 0:
                    g_.memset(eye[:], 0.0).then_inc(eyed, 1)
                    g_.wait_ge(eyed, 1)
                    g_.affine_select(out=eye[:], in_=eye[:], compare_op=ALU.not_equal, fill=1.0, base=0,
                                     pattern=[[-1, 128]], channel_multiplier=1).then_inc(eyed, 1)

                def digits_of(g):
                    s0, k = GROUPS[g]
                    with if_dense(g_):
                        if g == 0:
                            g_.sem_inc(digits_done, 1)
                            g_.sem_inc(digits_used, 1)
                        with g_.Fori(0, NB) as i:
                            n = i + g * NB
                            g_.wait_ge(beyond_in, n * 16 + 16)
                            g_.sem_inc(digits_seen, 1)
                            g_.tensor_scalar(whole[:, 0:k, :], beyond[:, 0:k, :], 1.0 / 256, ROUND, ALU.mult,
                                             ALU.add).then_inc(digit_steps, 1)
                            g_.wait_ge(digit_steps, n * 2 + 1)
                            g_.sem_inc(digits_seen, 1)
                            g_.wait_ge(digits_used, n + 1)
                            g_.sem_inc(digits_seen, 1)
                            g_.tensor_scalar(digits[:, 0, 0:k, :], whole[:, 0:k, :], -ROUND, 256.0, ALU.add,
                                             ALU.mult).then_inc(digit_steps, 1)
                            g_.wait_ge(digit_steps, n * 2 + 2)
                            g_.tensor_tensor(digits[:, 1, 0:k, :], beyond[:, 0:k, :], digits[:, 0, 0:k, :],
                                             ALU.subtract).then_inc(digits_done, 1)
                            g_.wait_ge(digits_done, n + 2)

                digits_of(0)
                for g, (s0, k) in enumerate(GROUPS):
                    if g + 1 < NG:
                        digits_of(g + 1)
                    if L == 0:
                        continue
                    g_.wait_ge(centred, g + 1)
                    for n, name, op in ((0, "gamma", ALU.mult), (1, "beta", ALU.add)):
                        if n:
                            g_.wait_ge(pch, g + 1)
                        m = g_.tensor_tensor(tmp[:, 0:k, :], tmp[:, 0:k, :],
                                             rows[name][:, L - 1:L, :].broadcast_to((P, k, D)), op)
                        m.then_inc(affine if n else pch, 1)

            @block.scalar
            def _(a):
                if L == 0:
                    a.wait_ge(turned, 1)
                    a.copy(W[:].rearrange("p i (o q) -> p i o q", o=2), py[:, :, :, 0:128]).then_inc(y_out, 1)
                a.wait_ge(epsd, 1)

                def take(g):
                    s0, k = GROUPS[g]
                    for h in range(2):
                        a.wait_ge(summed, 2 * g + h + 1)
                        if g >= 2 and h == 0:
                            a.wait_ge(projected, g - 1)
                        scale = {0: 1.0, 1: 1.0 / 128}.get(L)
                        if scale is None:
                            scale = tab["unscale"][:, L - 2, h:h + 1]
                        a.activation(yt[:, g % 2, h, 0:k * P], py[:, g % 2, h, 0:k * P], ACT.Copy,
                                     scale=scale).then_inc(y_out, 1)

                def normalize(n, g, k, out, src):
                    a.wait_ge(stats if n == 0 else last_stats, 2 * g + 1)
                    a.activation(rs[:, 0:k], mv[:, 0:k, 1], ACT.Sqrt, bias=eps[:]).then_inc(rooted, 1)
                    a.wait_ge(stats if n == 0 else last_stats, 2 * g + 2)
                    for j in range(k):
                        m = a.activation(out[:, j, :], src[:, j, :], ACT.Identity, bias=nm[:, j:j + 1],
                                         scale=rs[:, j:j + 1])
                    return m

                def finish(g):
                    s0, k = GROUPS[g]
                    if L == 0:
                        normalize(0, g, k, X[:, s0:s0 + k, :], a_).then_inc(centred, 1)
                        a.wait_ge(centred, g + 1)
                    else:
                        normalize(0, g, k, tmp, a_).then_inc(centred, 1)
                        if not last_layer:
                            a.wait_ge(affine, g + 1)
                    if last_layer:
                        normalize(1, g, k, X[:, s0:s0 + k, :], a_).then_inc(low, 1)
                        return
                    if g:
                        a.wait_ge(low, g)
                    for j in range(k):
                        if L == 0:
                            m = a.activation(a_[:, j, :], X[:, s0 + j, :], ACT.Copy, scale=tab["dinv_x"][:, s0 + j:s0 + j + 1])
                        else:
                            m = a.activation(a_[:, j, :], tmp[:, j, :], ACT.Relu, scale=tab["dinv"][:, s0 + j:s0 + j + 1])
                    m.then_inc(relued, 1)
                    a.wait_ge(relued, g + 1)
                    a.copy(nxt[0][:, s0:s0 + k, :], a_[:, 0:k, :]).then_inc(high, 1)

                take(0)
                for g in range(NG):
                    if g + 1 < NG:
                        take(g + 1)
                    finish(g)

            @block.vector
            def _(v):
                n = [0]

                def link(ins):
                    n[0] += 1
                    ins.then_inc(vch, 1)
                    v.wait_ge(vch, n[0])

                def moments(g, k, sem_, src):
                    for j in range(k):
                        m = v.bn_stats(st[:, j, :], src[:, j, :])
                    link(m)
                    for j in range(k):
                        m = v.bn_aggr(mv[:, j, :], st[:, j, :])
                    m.then_inc(sem_, 1)
                    return m

                if L == 0:
                    v.wait_ge(w_in, 32)
                count = [0]
                for g, (s0, k) in enumerate(GROUPS):
                    v.wait_ge(projected, g + 1)
                    if g:
                        v.wait_ge(low, g)
                    for j in range(k):
                        t = s0 + j
                        if L == 0:
                            m = v.scalar_tensor_tensor(a_[:, j, :], po[:, g % 2, j, :], tab["mean"][:, t:t + 1],
                                                       X[:, t, :], ALU.mult, ALU.add)
                        else:
                            m = v.scalar_tensor_tensor(a_[:, j, :], po[:, g % 2, j, :], tab["dinv"][:, t:t + 1],
                                                       rows["b"][:, L - 1, :], ALU.mult, ALU.add)
                    m.then_inc(o_out, 1)
                    v.wait_ge(o_out, g + 1)
                    if L == 0:
                        for j in range(k):
                            t = s0 + j
                            m = v.scalar_tensor_tensor(a_[:, j, :], b0[:], tab["degmean"][:, t:t + 1],
                                                       a_[:, j, :], ALU.mult, ALU.add)
                        link(m)
                    for pass_ in range(2 if last_layer else 1):
                        s_ = stats if pass_ == 0 else last_stats
                        if pass_:
                            v.wait_ge(affine, g + 1)
                            link(v.scalar_tensor_tensor(a_[:, 0:k, :], tmp[:, 0:k, :], 0.0, X[:, s0:s0 + k, :],
                                                        ALU.max, ALU.add))
                        moments(g, k, s_, a_)
                        count[0] += 1
                        v.wait_ge(rooted, count[0])
                        link(v.reciprocal(rs[:, 0:k], rs[:, 0:k]))
                        v.scalar_tensor_tensor(nm[:, 0:k], mv[:, 0:k, 0], -1.0, rs[:, 0:k], ALU.mult, ALU.mult).then_inc(s_, 1)
                    if not last_layer:
                        v.wait_ge(high, g + 1)
                        v.tensor_tensor(nxt[1][:, s0:s0 + k, :], a_[:, 0:k, :], nxt[0][:, s0:s0 + k, :],
                                        ALU.subtract).then_inc(low, 1)


def self_loops(nc, ctx, tab, add):
    sem = lambda n: ctx.semaphore(f"sl{add}_{n}")
    eyed = sem("eye")
    C = tab["counts"]
    with ExitStack() as c, nc.Block() as block:
        eye = c.enter_context(nc.sbuf_tensor(f"eye_sl{add}", [P, P], F32))

        @block.gpsimd
        def _(g):
            g.memset(eye[:], 0.0).then_inc(eyed, 1)
            g.wait_ge(eyed, 1)
            g.affine_select(out=eye[:], in_=eye[:], compare_op=ALU.not_equal, fill=1.0, base=0,
                            pattern=[[-1, P]], channel_multiplier=1).then_inc(eyed, 1)

        @block.vector
        def _(v):
            v.wait_ge(eyed, 2)
            for b in range(NB):
                v.tensor_tensor(C[:, b, b, 0:P], C[:, b, b, 0:P], eye[:], ALU.add if add else ALU.subtract, saturate=False)


def need(eng, sem, value):
    if not isinstance(value, int) or value > 0:
        eng.wait_ge(sem, value)


def skewed(eng, n, stages):
    leads = [lead for lead, _ in stages]
    begin, end = 2 - min(leads), n - max(leads)
    end -= (end - begin) % 2

    def plain(s):
        for lead, fn in stages:
            if 0 <= s + lead < n:
                fn(s + lead, (s + lead) % 2, (s + lead) // 2)
    for s in range(-max(leads), begin):
        plain(s)
    with eng.Fori(0, (end - begin) // 2) as i:
        for k in range(2):
            for lead, fn in stages:
                g = begin + k + lead
                fn(i * 2 + g, g % 2, i + g // 2)
    for s in range(end, n - min(leads)):
        plain(s)


EG = 4
NEG = NT // EG


def gated_messages(nc, ctx, dram, tab):
    with ExitStack() as c:
        sb = lambda n, s, d: c.enter_context(nc.sbuf_tensor("gm_" + n, s, d))
        pb = lambda n, s: c.enter_context(nc.psum_tensor("gm_" + n, s, F32))
        sem = lambda n: ctx.semaphore("gm_" + n)
        W1 = sb("W1", [2 * AT, D], F32)
        W2 = sb("W2", [128, 2, D], F32)
        b1 = sb("b1", [128, 2], F32)
        b2f = sb("b2f", [3, D], F32)
        b2r = sb("b2r", [3, D], F32)
        b2h = sb("b2h", [3, D], BF16)
        b2p = sb("b2p", [3, D], BF16)
        eye3 = sb("eye3", [3, 3], F32)
        ones = sb("ones", [3, ET], BF16)
        eye = sb("eye", [ET, ET], F32)
        iota = sb("iota", [ET, P], F32)
        edge = sb("edge", [ET, NT, 2], F32)
        slot = sb("slot", [ET, 2, EG], U32)
        attr = sb("attr", [ET, 2, EG, AT], F32)
        attr_t = sb("attr_t", [2 * AT, 2, EG // 2 * ET], F32)
        sg = sb("sg", [128, 2, 2, EG // 2 * ET], F32)
        hid = sb("hid", [128, 2, 2, 2, EG // 2 * ET], F32)
        gate = sb("gate", [ET, 2, EG, D], F32)
        hs = sb("hs", [ET, 2, EG, D], F32)
        msg = gate
        high = sb("high", [ET, 2, EG, D], F16)
        low = sb("low", [ET, 2, EG, D], F16)
        oh = sb("oh", [ET, 2, EG, P], F16)
        aggr = tab["aggr"]
        pt = pb("pt", [2 * AT, 2, BANK])
        ph = pb("ph", [128, 2, 2, EG // 2 * ET])
        pg = pb("pg", [ET, EG, D])
        pa = pb("pa", [P, EG, D])
        loaded, const, chain = map(sem, ("loaded", "const", "chain"))
        attr_in = [sem("attr_in0"), sem("attr_in1")]
        gathered = [sem("gathered0"), sem("gathered1")]
        turned, attr_t_done, first_done, sig1, hid_done, second_done, gated, onehot, msg_done, summed, added, slots = map(
            sem, ("turned", "attr_t", "first", "sig1", "hid", "second", "gated", "onehot", "msg", "summed", "added", "slots"))
        slots_seen, highd, lowd = map(sem, ("slots_seen", "high", "low"))
        NLOAD = 6
        NCONST = 7
        with nc.Block() as block:
            @block.sync
            def _(sp):
                for i in range(2):
                    sp.dma_start(W1[i * AT:(i + 1) * AT, :], dram["L2_gnn_W1"]).then_inc(loaded, 16)
                sp.dma_start(W2[:], dram["L2_gnn_W2"].rearrange("(h p) o -> p h o", p=128)).then_inc(loaded, 16)
                sp.dma_start(b2f[:], dram["L2_gnn_b2"].partition_broadcast(3)).then_inc(loaded, 16)
                with nc.allow_non_contiguous_dma(reason="256 numbers, once"):
                    sp.dma_start(b1[:, 0:1], dram["L2_gnn_b1"][0:128].rearrange("(p a) -> p a", a=1)).then_inc(loaded, 16)
                    sp.dma_start(b1[:, 1:2], dram["L2_gnn_b1"][128:256].rearrange("(p a) -> p a", a=1)).then_inc(loaded, 16)

                def load(g, q, h):
                    need(sp, turned, g - 1)
                    for j in range(EG):
                        e0 = sp.value_load(tab["e0"][0:1, bass.ds(g * EG + j, 1)], min_val=0, max_val=E)
                        sp.dma_start(attr[:, q, j, :], dram["attr_s"][bass.ds(e0, ET), :]).then_inc(attr_in[q], 16)
                        sp.dma_start(edge[:, bass.ds(g * EG + j, 1), :].rearrange("p a k -> p (a k)"),
                                     dram["pairs"][bass.ds(e0, ET), 0:2]).then_inc(attr_in[q], 16)
                skewed(sp, NEG, [(0, load)])

            @block.gpsimd
            def _(p):
                p.memset(ones[:], 1.0).then_inc(const, 1)
                p.memset(eye[:], 0.0).then_inc(const, 1)
                p.memset(aggr[:], 0.0).then_inc(const, 1)
                p.memset(eye3[:], 0.0).then_inc(const, 1)
                p.wait_ge(const, 4)
                p.affine_select(out=eye3[:], in_=eye3[:], compare_op=ALU.not_equal, fill=1.0, base=0,
                                pattern=[[-1, 3]], channel_multiplier=1).then_inc(const, 1)
                p.affine_select(out=eye[:], in_=eye[:], compare_op=ALU.not_equal, fill=1.0, base=0,
                                pattern=[[-1, ET]], channel_multiplier=1).then_inc(const, 1)
                p.iota(iota[:], pattern=[[1, P]], base=0, channel_multiplier=0,
                       allow_small_or_imprecise_dtypes=True).then_inc(const, 1)
                p.wait_ge(const, NCONST)

                def gather(g, q, h):
                    need(p, msg_done, g - 1)
                    p.wait_ge(attr_in[q], (h + 1) * (32 * EG))
                    p.tensor_copy(slot[:, q, :], edge[:, bass.ts(g, EG), 0]).then_inc(slots, 1)
                    p.wait_ge(slots, g + 1)
                    p.sem_inc(slots_seen, 1)
                    for j in range(EG):
                        p.indirect_dma_start(out=hs[:, q, j, :], out_offset=None, in_=dram["table"],
                                             in_offset=bass.IndirectOffsetOnAxis(ap=slot[:, q, j:j + 1], axis=0)
                                             ).then_inc(gathered[q], 16)

                def lower(g, q, h):
                    p.wait_ge(highd, g + 1)
                    need(p, summed, g - 1)
                    p.tensor_tensor(low[:, q, :, :], msg[:, q, :, :], high[:, q, :, :], ALU.subtract).then_inc(lowd, 1)
                skewed(p, NEG, [(1, gather), (-1, lower)])

            @block.tensor
            def _(pe):
                pe.wait_ge(loaded, 16 * NLOAD)
                pe.wait_ge(const, NCONST)
                pe.wait_ge(chain, 10)

                def turn(g, q, h):
                    pe.wait_ge(attr_in[q], (h + 1) * (32 * EG))
                    need(pe, attr_t_done, g - 1)
                    for j in range(EG // 2):
                        m = nc.tensor.transpose(pt[:, q, j * ET:(j + 1) * ET],
                                                attr[:, q, 2 * j:2 * j + 2, :].rearrange("p a f -> p (a f)"), eye[:])
                    m.then_inc(turned, 1)

                def first(g, q, h):
                    pe.wait_ge(attr_t_done, g + 1)
                    need(pe, hid_done, g)
                    for i in range(2):
                        for r in range(2):
                            half = slice(r * AT, (r + 1) * AT)
                            m = nc.tensor.matmul(ph[:, r, i, :], W1[half, i * 128:(i + 1) * 128], attr_t[half, q, :],
                                                 start=True, stop=True)
                        m.then_inc(first_done, 1)

                def second(g, q, h):
                    pe.wait_ge(hid_done, g + 1)
                    need(pe, gated, g)
                    for j in range(EG):
                        for i in range(2):
                            nc.tensor.matmul(pg[:, j, :], hid[:, q, j % 2, i, j // 2 * ET:(j // 2 + 1) * ET], W2[:, i, :],
                                             start=i == 0, stop=False)
                        m = nc.tensor.matmul(pg[:, j, :], ones[:], b2p[:], start=False, stop=True)
                    m.then_inc(second_done, 1)

                def add_up(g, q, h):
                    pe.wait_ge(lowd, g + 1)
                    pe.wait_ge(onehot, g + 1)
                    need(pe, added, g * EG)
                    for j in range(EG):
                        nc.tensor.matmul(pa[:, j, :], oh[:, q, j, :], high[:, q, j, :], start=True, stop=False)
                        m = nc.tensor.matmul(pa[:, j, :], oh[:, q, j, :], low[:, q, j, :], start=False, stop=True)
                    m.then_inc(summed, 1)
                skewed(pe, NEG, [(2, turn), (1, first), (0, second), (-2, add_up)])

            @block.scalar
            def _(a):
                a.wait_ge(loaded, 16 * NLOAD)

                def take(g, q, h):
                    a.wait_ge(turned, g + 1)
                    need(a, first_done, (g - 1) * 2)
                    a.copy(attr_t[:, q, :], pt[:, q, 0:EG // 2 * ET]).then_inc(attr_t_done, 1)

                def sigmoid1(g, q, h):
                    need(a, hid_done, g)
                    for i in range(2):
                        a.wait_ge(first_done, g * 2 + 2)
                        a.activation(sg[:, :, i, :], ph[:, :, i, :], ACT.Sigmoid, bias=b1[:, i:i + 1]).then_inc(sig1, 1)

                def sigmoid2(g, q, h):
                    a.wait_ge(second_done, g + 1)
                    need(a, lowd, g - 1)
                    a.activation(gate[:, q, :, :], pg[:], ACT.Sigmoid).then_inc(gated, 1)

                def upper(g, q, h):
                    a.wait_ge(msg_done, g + 1)
                    need(a, summed, g - 1)
                    a.copy(high[:, q, :, :], msg[:, q, :, :]).then_inc(highd, 1)
                skewed(a, NEG, [(-1, upper), (2, take), (1, sigmoid1), (0, sigmoid2)])

            @block.vector
            def _(v):
                v.wait_ge(const, NCONST)
                v.wait_ge(loaded, 16 * NLOAD)
                n = [0]

                def link(ins):
                    n[0] += 1
                    ins.then_inc(chain, 1)
                    v.wait_ge(chain, n[0])
                link(v.tensor_copy(b2h[:], b2f[:]))
                link(v.tensor_scalar(b2p[:], b2h[:], eye3[:, 0:1], None, ALU.mult))
                for part in (1, 2):
                    link(v.tensor_tensor(b2f[:], b2f[:], b2h[:], ALU.subtract))
                    link(v.tensor_copy(b2h[:], b2f[:]))
                    link(v.tensor_scalar(b2r[:], b2h[:], eye3[:, part:part + 1], None, ALU.mult))
                    link(v.tensor_tensor(b2p[:], b2p[:], b2r[:], ALU.add))

                def hidden(g, q, h):
                    v.wait_ge(sig1, g * 2 + 2)
                    need(v, second_done, g - 1)
                    for i in range(2):
                        m = v.scalar_tensor_tensor(hid[:, q, :, i, :], ph[:, :, i, :], b1[:, i:i + 1], sg[:, :, i, :],
                                                   ALU.add, ALU.mult)
                    m.then_inc(hid_done, 1)

                def onehots(g, q, h):
                    need(v, summed, g - 1)
                    v.wait_ge(attr_in[q], (h + 1) * (32 * EG))
                    for j in range(EG):
                        t = g * EG + j
                        m = v.tensor_scalar(oh[:, q, j, :], iota[:], tab["first"][:, bass.ds(t, 1)],
                                            edge[:, bass.ds(t, 1), 1], ALU.add, ALU.is_equal)
                    m.then_inc(onehot, 1)

                def message(g, q, h):
                    v.wait_ge(gated, g + 1)
                    v.wait_ge(gathered[q], (h + 1) * (16 * EG))
                    v.scalar_tensor_tensor(msg[:, q, :, :], gate[:, q, :, :], 128.0, hs[:, q, :, :], ALU.mult,
                                           ALU.mult).then_inc(msg_done, 1)

                def add(g, q, h):
                    v.wait_ge(summed, g + 1)
                    for j in range(EG):
                        b = v.value_load(tab["bucket"][0:1, bass.ds(g * EG + j, 1)], min_val=0, max_val=NB)
                        need(v, added, g * EG + j)
                        s = aggr[:, bass.ds(b, 1), :].rearrange("p a f -> p (a f)")
                        v.scalar_tensor_tensor(s, pa[:, j, :], 1.0 / 128, s, ALU.mult, ALU.add).then_inc(added, 1)
                skewed(v, NEG, [(1, hidden), (0, message), (-1, onehots), (-2, add)])
                v.wait_ge(added, NT)


def layer_norm(v, a, link, stats_sem, root_sem, counts, z, out, st, mv, rs, nm, k, side):
    n = counts[side]
    counts[side] += 1
    if side == "v":
        for j in range(k):
            m = v.bn_stats(st[:, j, :], z[:, j, :])
        link(m)
        for j in range(k):
            m = v.bn_aggr(mv[:, j, :], st[:, j, :])
        m.then_inc(stats_sem, 1)
        v.wait_ge(root_sem, n + 1)
        link(v.reciprocal(rs[:, 0:k], rs[:, 0:k]))
        v.scalar_tensor_tensor(nm[:, 0:k], mv[:, 0:k, 0], -1.0, rs[:, 0:k], ALU.mult, ALU.mult).then_inc(stats_sem, 1)
        return None
    eps = counts["eps"]
    a.wait_ge(stats_sem, 2 * n + 1)
    a.activation(rs[:, 0:k], mv[:, 0:k, 1], ACT.Sqrt, bias=eps).then_inc(root_sem, 1)
    a.wait_ge(stats_sem, 2 * n + 2)
    for j in range(k):
        m = a.activation(out[:, j, :], z[:, j, :], ACT.Identity, bias=nm[:, j:j + 1], scale=rs[:, j:j + 1])
    return m


def update_nodes(nc, ctx, dram, tab):
    with ExitStack() as c:
        sb = lambda n, s, d=F32: c.enter_context(nc.sbuf_tensor("un_" + n, s, d))
        pb = lambda n, s: c.enter_context(nc.psum_tensor("un_" + n, s, F32))
        sem = lambda n: ctx.semaphore("un_" + n)
        X, aggr = tab["X"], tab["aggr"]
        U1 = sb("U1", [128, 4, D])
        U2 = sb("U2", [128, 2, D])
        c1 = sb("c1", [128, 2])
        c2 = sb("c2", [P, D])
        W3 = sb("W3", [128, 2, 128])
        al = sb("al", [P, 2, 128])
        eye = sb("eye", [P, P])
        cat = sb("cat", [128, 4, MOV * P])
        sg = sb("sg", [128, 2, MOV * P])
        hid = sb("hid", [128, 2, MOV * P])
        z = sb("z", [P, MOV, D])
        st, mv, rs, nm = sb("st", [P, MOV, 6]), sb("mv", [P, MOV, 2]), sb("rs", [P, MOV]), sb("nm", [P, MOV])
        eps = sb("eps", [P, 1])
        xt = sb("xt", [128, 2, MOV * P])
        prod = sb("prod", [P, 2, MOV, 128])
        pt = pb("pt", [128, 4, BANK])
        ph = pb("ph", [128, 2, BANK])
        po = pb("po", [P, MOV, D])
        names = ("loaded", "const", "turned", "cat", "first", "sig", "hid", "second", "z", "chain", "stats",
                 "root", "normed", "xturned", "xt", "heads", "heads_out", "logits")
        loaded, const, turned, catd, first, sig, hidd, second, zd, ch, stats, root, normed, xturned, xtd, heads, heads_out, \
            logits = map(sem, names)
        with nc.Block() as block:
            @block.sync
            def _(sp):
                sp.dma_start(U1[:], dram["L2_gnn_U1"].rearrange("(h p) o -> p h o", p=128)).then_inc(loaded, 16)
                sp.dma_start(U2[:], dram["L2_gnn_U2"].rearrange("(h p) o -> p h o", p=128)).then_inc(loaded, 16)
                sp.dma_start(W3[:], dram["L3_gnn_W"].rearrange("(h p) o -> p h o", p=128)).then_inc(loaded, 16)
                sp.dma_start(c2[:], dram["L2_gnn_c2"].partition_broadcast(P)).then_inc(loaded, 16)
                for i, n in enumerate(("l", "r")):
                    sp.dma_start(al[:, i, :], dram["L3_gnn_attn_" + n].rearrange("h d -> (h d)")
                                 .partition_broadcast(P)).then_inc(loaded, 16)
                with nc.allow_non_contiguous_dma(reason="256 numbers, once"):
                    for i in range(2):
                        sp.dma_start(c1[:, i:i + 1], dram["L2_gnn_c1"][128 * i:128 * (i + 1)]
                                     .rearrange("(p a) -> p a", a=1)).then_inc(loaded, 16)

            @block.gpsimd
            def _(p):
                p.memset(eps[:], 1e-5).then_inc(const, 1)
                p.memset(eye[:], 0.0).then_inc(const, 1)
                p.memset(tab["heads"][:], 1.0).then_inc(const, 1)
                p.wait_ge(const, 3)
                p.affine_select(out=eye[:], in_=eye[:], compare_op=ALU.not_equal, fill=1.0, base=0,
                                pattern=[[-1, P]], channel_multiplier=1).then_inc(const, 1)

            @block.tensor
            def _(pe):
                pe.wait_ge(loaded, 16 * 8)
                pe.wait_ge(const, 4)

                def turn(g):
                    s0, k = GROUPS[g]
                    need(pe, xtd, g - 1)
                    for i in range(4):
                        for j in range(k):
                            src = (X if i < 2 else aggr)[:, s0 + j, (i % 2) * 128:(i % 2 + 1) * 128]
                            m = nc.tensor.transpose(pt[:, i, j * P:(j + 1) * P], src, eye[:])
                    m.then_inc(turned, 1)

                def first_product(g):
                    s0, k = GROUPS[g]
                    pe.wait_ge(catd, g + 1)
                    need(pe, hidd, g)
                    for o in range(2):
                        for i in range(4):
                            m = nc.tensor.matmul(ph[:, o, 0:k * P], U1[:, i, o * 128:(o + 1) * 128], cat[:, i, 0:k * P],
                                                 start=i == 0, stop=i == 3)
                        m.then_inc(first, 1)

                def second_product(g):
                    s0, k = GROUPS[g]
                    pe.wait_ge(hidd, g + 1)
                    need(pe, heads_out, g)
                    for j in range(k):
                        for i in range(2):
                            m = nc.tensor.matmul(po[:, j, :], hid[:, i, j * P:(j + 1) * P], U2[:, i, :],
                                                 start=i == 0, stop=i == 1)
                    m.then_inc(second, 1)

                def heads_of(g):
                    s0, k = GROUPS[g]
                    pe.wait_ge(normed, g + 1)
                    pe.wait_ge(catd, min(g + 2, NG))
                    for i in range(2):
                        for j in range(k):
                            m = nc.tensor.transpose(pt[:, i, j * P:(j + 1) * P], X[:, s0 + j, i * 128:(i + 1) * 128], eye[:])
                    m.then_inc(xturned, 1)
                    pe.wait_ge(xtd, g + 1)
                    for j in range(k):
                        for i in range(2):
                            m = nc.tensor.matmul(po[:, j, 0:128], xt[:, i, j * P:(j + 1) * P], W3[:, i, :],
                                                 start=i == 0, stop=i == 1)
                    m.then_inc(heads, 1)
                for g in range(NG + 1):
                    if g < NG:
                        turn(g)
                    if g:
                        second_product(g - 1)
                    if g < NG:
                        first_product(g)
                    if g:
                        heads_of(g - 1)

            counts = {"v": 0, "a": 0, "eps": eps[:]}

            @block.scalar
            def _(a):
                a.wait_ge(loaded, 16 * 8)
                a.wait_ge(const, 4)
                for g in range(NG + 1):
                    if g < NG:
                        k = GROUPS[g][1]
                        a.wait_ge(turned, g + 1)
                        a.copy(cat[:, :, 0:k * P], pt[:, :, 0:k * P]).then_inc(catd, 1)
                    if g:
                        s0, k = GROUPS[g - 1]
                        layer_norm(None, a, None, stats, root, counts, z, X[:, s0:s0 + k, :], st, mv, rs, nm, k,
                                   "a").then_inc(normed, 1)
                    if g < NG:
                        k = GROUPS[g][1]
                        for o in range(2):
                            a.wait_ge(first, 2 * g + o + 1)
                            a.activation(sg[:, o, 0:k * P], ph[:, o, 0:k * P], ACT.Sigmoid, bias=c1[:, o:o + 1]).then_inc(sig, 1)
                    if g:
                        k = GROUPS[g - 1][1]
                        a.wait_ge(xturned, g)
                        a.copy(xt[:, :, 0:k * P], pt[:, 0:2, 0:k * P]).then_inc(xtd, 1)

            @block.vector
            def _(v):
                v.wait_ge(loaded, 16 * 8)
                v.wait_ge(const, 4)
                n = [0]

                def link(ins):
                    n[0] += 1
                    ins.then_inc(ch, 1)
                    v.wait_ge(ch, n[0])

                def normalize(g):
                    s0, k = GROUPS[g]
                    v.wait_ge(second, g + 1)
                    link(v.tensor_tensor(z[:, 0:k, :], po[:, 0:k, :],
                                         c2[:].rearrange("p (a f) -> p a f", a=1).broadcast_to((P, k, D)), ALU.add))
                    link(v.scalar_tensor_tensor(z[:, 0:k, :], X[:, s0:s0 + k, :], 2.0, z[:, 0:k, :], ALU.mult, ALU.add))
                    layer_norm(v, None, link, stats, root, counts, z, None, st, mv, rs, nm, k, "v")

                def hidden(g):
                    k = GROUPS[g][1]
                    v.wait_ge(sig, 2 * g + 2)
                    for o in range(2):
                        m = v.scalar_tensor_tensor(hid[:, o, 0:k * P], ph[:, o, 0:k * P], c1[:, o:o + 1],
                                                   sg[:, o, 0:k * P], ALU.add, ALU.mult)
                    m.then_inc(hidd, 1)

                def logits_of(g):
                    s0, k = GROUPS[g]
                    v.wait_ge(heads, g + 1)
                    v.tensor_copy(tab["heads"][:, s0:s0 + k, :, 0:64],
                                  po[:, 0:k, 0:128].rearrange("p k (h d) -> p k h d", h=2))
                    for i in range(2):
                        m = v.tensor_tensor(prod[:, i, 0:k, :], po[:, 0:k, 0:128],
                                            al[:, i:i + 1, :].broadcast_to((P, k, 128)), ALU.mult)
                    m.then_inc(heads_out, 1)
                    v.wait_ge(heads_out, g + 1)
                    for i in range(2):
                        link(v.tensor_reduce(tab["logit"][:, i, s0:s0 + k, :],
                                             prod[:, i, 0:k, :].rearrange("p k (h d) -> p k h d", h=2),
                                             op=ALU.add, axis=AX.X))
                for g in range(NG + 1):
                    if g:
                        normalize(g - 1)
                    if g < NG:
                        hidden(g)
                    if g:
                        logits_of(g - 1)


BIG = 1e30
LEAK = 0.2


EB = 4
AHEAD = 3
STEPS = 2 * NB


def attention(nc, ctx, dram, tab):
    with ExitStack() as c:
        sb = lambda n, s, d=F32: c.enter_context(nc.sbuf_tensor("at_" + n, s, d))
        sem = lambda n: ctx.semaphore("at_" + n)
        C, X, logit, H = tab["counts"], tab["X"], tab["logit"], tab["heads"]
        eye = sb("eye", [128, 128])
        eps = sb("eps", [P, 1])
        minus_half = sb("minus_half", [P, 1])
        el_low = sb("el_low", [P, NB, 2])
        el_rest = sb("el_rest", [P, NB, 2])
        bg = sb("bg", [P, 128])
        bl = sb("bl", [P, D])
        LW = sb("LW", [128, D])
        masks = sb("masks", [P, EB, MOV * P])
        best = sb("best", [P, 2, MOV * P])
        top = sb("top", [P, MOV, 2])
        m_ = sb("m", [P, MOV, 2])
        r = sb("r", [P, 2, 2, MOV, 2])
        rows = sb("rows", [P, 2, 2, MOV * P])
        rect = sb("rect", [P, EB, MOV * P])
        leaky = sb("leaky", [P, EB, MOV * P])
        e = sb("e", [P, EB, MOV * P])
        w = sb("w", [P, EB, MOV * P])
        num = sb("num", [65, 2, MOV * P])
        o = sb("o", [P, MOV, 128])
        rec = sb("rec", [P, MOV, 2, 1])
        ot = sb("ot", [128, MOV * P])
        z = sb("z", [P, MOV, D])
        y = sb("y", [P, MOV, D])
        beyond = sb("beyond", [P, MOV, P])
        x_rect, x_leaky, x_e, x_w = (sb(n, [P, MOV * P]) for n in ("x_rect", "x_leaky", "x_e", "x_w"))
        st, mv, rs, nm = sb("st", [P, MOV, 6]), sb("mv", [P, MOV, 2]), sb("rs", [P, MOV]), sb("nm", [P, MOV])
        pb = lambda n, s: c.enter_context(nc.psum_tensor("at_" + n, s, F32))
        prow = pb("prow", [P, 2, MOV, 128])
        pn = pb("pn", [65, 2, BANK])
        pot = pb("pot", [P, MOV, 128])
        pot2 = pb("pot2", [128, MOV, 128])
        pl = pb("pl", [P, MOV, D])
        loaded, const, chain = sem("loaded"), sem("const"), sem("chain")
        masked, bestd, best_turned, rd, rowed, row_out = map(sem, (
            "masked", "best", "best_turned", "r", "rowed", "row_out"))
        rectd_v = sem("rect_v")
        rectd, leaked, exps, weighed, used = map(sem, ("rect", "leaky", "exps", "weighed", "used"))
        numd, nturned, nturn_used, od, oturned, otd, lin, lin_used, stats, root, normed, stored = map(sem, (
            "num", "nturned", "nturn_used", "o", "oturned", "ot", "lin", "lin_used", "stats", "root", "normed", "stored"))
        beyond_in, x_rectd, x_leaked, x_exps, x_weighed, x_used = map(sem, (
            "beyond_in", "x_rect", "x_leaky", "x_exps", "x_weighed", "x_used"))
        counts = {"v": 0, "a": 0, "eps": eps[:]}
        NCONST = 4

        def by_vector(u):
            return u % 5 in (1, 3)

        def count_by(u, vector):
            return sum(by_vector(w) == vector for w in range(u))

        def mask_at(s):
            return [i for i in range(NB) if i * 5 // 3 == s]

        def if_dense(eng):
            return eng.If(eng.value_load(tab["dense"][0:1, 0:1], min_val=0, max_val=1) != 0)

        def group_steps():
            for g in range(NG + 1):
                for s in range(STEPS):
                    yield g, s, s // NB, s % NB

        with nc.Block() as block:
            @block.sync
            def _(sp):
                sp.dma_start(bg[:], dram["L3_gnn_gat_bias"].partition_broadcast(P)).then_inc(loaded, 16)
                sp.dma_start(bl[:], dram["L3_gnn_lin_b"].partition_broadcast(P)).then_inc(loaded, 16)
                sp.dma_start(LW[:], dram["L3_gnn_lin_W"]).then_inc(loaded, 16)
                with if_dense(sp):
                    sp.sem_inc(x_weighed, 1)
                    for n in range(2 * NG):
                        s0, k = GROUPS[n // 2]
                        with sp.Fori(0, NB) as i:
                            sp.wait_ge(x_weighed, i + (n * NB + 1))
                            sp.dma_start(beyond[:, 0:k, :], dram["beyond"][s0:s0 + k, :, bass.ds(i * P, P)]
                                         .rearrange("b p d -> p b d")).then_inc(beyond_in, 16)

            @block.gpsimd
            def _(p):
                p.memset(eps[:], 1e-5).then_inc(const, 1)
                p.memset(minus_half[:], -BIG / 2).then_inc(const, 1)
                p.memset(eye[:], 0.0).then_inc(const, 1)
                p.wait_ge(const, 3)
                p.affine_select(out=eye[:], in_=eye[:], compare_op=ALU.not_equal, fill=1.0, base=0,
                                pattern=[[-1, 128]], channel_multiplier=1).then_inc(const, 1)

                def sum_parts(n, i, k):
                    u = NB * n + i
                    q = u % EB
                    if i == 0:
                        p.wait_ge(row_out, n + 1)
                    if by_vector(u):
                        p.wait_ge(rectd_v, count_by(u + 1, True))
                    else:
                        p.wait_ge(rectd, count_by(u + 1, False))
                    need(p, exps, u - EB + 1)
                    p.tensor_tensor(leaky[:, q, 0:k * P], rect[:, q, 0:k * P], rows[:, n % 2, 1, 0:k * P],
                                    ALU.add).then_inc(leaked, 1)

                def beyond_cap(n, k):
                    with if_dense(p):
                        with p.Fori(0, NB) as i:
                            p.wait_ge(x_rectd, i + (NB * n + 1))
                            p.tensor_tensor(x_leaky[:, 0:k * P], x_rect[:, 0:k * P], rows[:, n % 2, 1, 0:k * P],
                                            ALU.add).then_inc(x_leaked, 1)
                for g, s, h, i in group_steps():
                    if g < NG:
                        sum_parts(2 * g + h, i, GROUPS[g][1])
                        if i == NB - 1:
                            beyond_cap(2 * g + h, GROUPS[g][1])
                    if g and s == 45:
                        s0, k = GROUPS[g - 1]
                        p.wait_ge(normed, g)
                        p.dma_start(dram["out"][s0 * P:(s0 + k) * P, :].rearrange("(b p) f -> p b f", p=P),
                                    y[:, 0:k, :]).then_inc(stored, 16)
                p.wait_ge(stored, 16 * NG)

            @block.tensor
            def _(pe):
                pe.wait_ge(loaded, 48)
                pe.wait_ge(const, NCONST)

                def turn_best(g):
                    s0, k = GROUPS[g]
                    pe.wait_ge(bestd, 2 * NB * (g + 1))
                    need(pe, row_out, 2 * g)
                    for h in range(2):
                        for j in range(k):
                            m = nc.tensor.transpose(prow[:, h, j, 0:P], best[:, h, j * P:(j + 1) * P], eye[0:P, 0:P])
                    m.then_inc(best_turned, 1)

                def row(n):
                    g, h = n // 2, n % 2
                    s0, k = GROUPS[g]
                    pe.wait_ge(rd, g + 1)
                    need(pe, row_out, n)
                    for i in range(2):
                        for j in range(k):
                            m = nc.tensor.transpose(prow[:, i, j, 0:P],
                                                    r[:, g % 2, i, j, h:h + 1].broadcast_to((P, P)), eye[0:P, 0:P])
                    m.then_inc(rowed, 1)

                def product(n, i, k, first, last):
                    u = NB * n + i
                    pe.wait_ge(weighed, u + 1)
                    nc.tensor.matmul(pn[:, n % 2, 0:k * P], H[:, i, n % 2, :], w[:, u % EB, 0:k * P],
                                     start=first, stop=last).then_inc(used, 1)

                def beyond_cap(n, k):
                    with if_dense(pe):
                        for i in range(NB):
                            pe.wait_ge(x_weighed, NB * n + i + 2)
                            nc.tensor.matmul(pn[:, n % 2, 0:k * P], H[:, i, n % 2, :], x_w[:, 0:k * P],
                                             start=False, stop=False).then_inc(x_used, 1)

                turn_best(0)
                row(0)
                for g, s, h, i in group_steps():
                    n = 2 * g + h
                    if g < NG:
                        k = GROUPS[g][1]
                        if i == 0:
                            need(pe, numd, n - 1)
                        if i == NB - 1:
                            beyond_cap(n, k)
                        product(n, i, k, i == 0, i == NB - 1)
                        if s == 14:
                            row(2 * g + 1)
                        if g + 1 < NG and s == 41:
                            turn_best(g + 1)
                        if g + 1 < NG and s == 44:
                            row(2 * g + 2)
                        if s == 33:
                            pe.wait_ge(numd, n)
                            need(pe, nturn_used, 2 * g)
                            for j in range(k):
                                m = nc.tensor.transpose(pot[:, j, 0:65], num[:, 0, j * P:(j + 1) * P], eye[0:65, 0:65])
                            m.then_inc(nturned, 1)
                    if g:
                        k = GROUPS[g - 1][1]
                        if s == 8:
                            pe.wait_ge(numd, 2 * g)
                            pe.wait_ge(nturn_used, 2 * g - 1)
                            for j in range(k):
                                m = nc.tensor.transpose(pot[:, j, 0:65], num[:, 1, j * P:(j + 1) * P], eye[0:65, 0:65])
                            m.then_inc(nturned, 1)
                        if s == 17:
                            pe.wait_ge(od, g)
                            for j in range(k):
                                m = nc.tensor.transpose(pot2[:, j, 0:P], o[:, j, :], eye[0:P, 0:P])
                            m.then_inc(oturned, 1)
                        if s == 24:
                            pe.wait_ge(otd, g)
                            need(pe, lin_used, g - 1)
                            for j in range(k):
                                m = nc.tensor.matmul(pl[:, j, :], ot[:, j * P:(j + 1) * P], LW[:], start=True, stop=True)
                            m.then_inc(lin, 1)

            @block.scalar
            def _(a):
                a.wait_ge(const, NCONST)

                def mask(g, i):
                    s0, k = GROUPS[g]
                    u = NB * g + i
                    need(a, bestd, 2 * (u - EB + 1))
                    a.activation(masks[:, u % EB, 0:k * P].rearrange("p (k d) -> p k d", d=P), C[:, s0:s0 + k, i, 0:P],
                                 ACT.Identity, bias=minus_half[:], scale=BIG).then_inc(masked, 1)

                def row(n):
                    k = GROUPS[n // 2][1]
                    a.wait_ge(rowed, n + 1)
                    need(a, leaked, NB * (n - 1))
                    a.copy(rows[:, n % 2, :, 0:k * P].rearrange("p i (k d) -> p i k d", d=P),
                           prow[:, :, 0:k, 0:P]).then_inc(row_out, 1)

                def rectify(u):
                    n, i = u // NB, u % NB
                    k, h, q = GROUPS[n // 2][1], n % 2, u % EB
                    if i == 0:
                        a.wait_ge(row_out, n + 1)
                    if by_vector(u):
                        return
                    need(a, leaked, u - EB + 1)
                    a.activation(rect[:, q, 0:k * P], rows[:, n % 2, 0, 0:k * P], ACT.Relu,
                                 bias=el_rest[:, i, h:h + 1]).then_inc(rectd, 1)

                def exp(u):
                    n, i = u // NB, u % NB
                    k, h, q = GROUPS[n // 2][1], n % 2, u % EB
                    a.wait_ge(leaked, u + 1)
                    need(a, weighed, u - EB + 1)
                    a.activation(e[:, q, 0:k * P], leaky[:, q, 0:k * P], ACT.Exp, bias=el_low[:, i, h:h + 1]).then_inc(exps, 1)

                def beyond_cap(n, k):
                    h = n % 2
                    with if_dense(a):
                        with a.Fori(0, NB) as i:
                            a.wait_ge(x_weighed, i + (NB * n + 1))
                            a.activation(x_rect[:, 0:k * P], rows[:, n % 2, 0, 0:k * P], ACT.Relu,
                                         bias=el_rest[:, bass.ds(i, 1), h]).then_inc(x_rectd, 1)
                            a.wait_ge(x_leaked, i + (NB * n + 1))
                            a.activation(x_e[:, 0:k * P], x_leaky[:, 0:k * P], ACT.Exp,
                                         bias=el_low[:, bass.ds(i, 1), h]).then_inc(x_exps, 1)

                for i in range(NB):
                    mask(0, i)
                row(0)
                a.wait_ge(chain, 2)
                for u in range(AHEAD):
                    rectify(u)
                for g, s, h, i in group_steps():
                    n = 2 * g + h
                    u = NB * n + i
                    if g < NG:
                        k = GROUPS[g][1]
                        if u + AHEAD < 2 * NB * NG:
                            rectify(u + AHEAD)
                        exp(u)
                        if i == NB - 1:
                            beyond_cap(n, k)
                        if g + 1 < NG:
                            for i_ in mask_at(s):
                                mask(g + 1, i_)
                        if s == 20:
                            row(2 * g + 1)
                        if g + 1 < NG and s == 46:
                            row(2 * g + 2)
                        if s == 32:
                            a.wait_ge(used, NB * n)
                            need(a, nturned, 2 * g - 1)
                            a.copy(num[:, 0, 0:k * P], pn[:, 0, 0:k * P]).then_inc(numd, 1)
                    if g:
                        k = GROUPS[g - 1][1]
                        if s == 7:
                            a.wait_ge(used, NB * 2 * g)
                            need(a, nturned, 2 * g - 2)
                            a.copy(num[:, 1, 0:k * P], pn[:, 1, 0:k * P]).then_inc(numd, 1)
                        if s == 23:
                            a.wait_ge(oturned, g)
                            need(a, lin, g - 1)
                            a.copy(ot[:, 0:k * P].rearrange("p (k d) -> p k d", d=P), pot2[:, 0:k, 0:P]).then_inc(otd, 1)
                        if s == 36:
                            a.wait_ge(stats, 2 * g - 1)
                            a.activation(rs[:, 0:k], mv[:, 0:k, 1], ACT.Sqrt, bias=eps[:]).then_inc(root, 1)
                        if s == 40:
                            a.wait_ge(stats, 2 * g)
                            need(a, stored, 16 * (g - 1))
                            for j in range(k):
                                m = a.activation(y[:, j, :], z[:, j, :], ACT.Identity, bias=nm[:, j:j + 1],
                                                 scale=rs[:, j:j + 1])
                            m.then_inc(normed, 1)

            @block.vector
            def _(v):
                v.wait_ge(loaded, 48)
                v.wait_ge(const, NCONST)
                n_ = [0]

                def link(ins):
                    n_[0] += 1
                    ins.then_inc(chain, 1)
                    v.wait_ge(chain, n_[0])
                link(v.tensor_scalar(el_low[:], logit[:, 0, :, :], LEAK, None, ALU.mult))
                link(v.tensor_scalar(el_rest[:], logit[:, 0, :, :], 1 - LEAK, None, ALU.mult))

                def take_best(g, i):
                    k = GROUPS[g][1]
                    u = NB * g + i
                    v.wait_ge(masked, u + 1)
                    if i == 0:
                        need(v, best_turned, g)
                    for h in range(2):
                        b = best[:, h, 0:k * P]
                        t = masks[:, u % EB, 0:k * P]
                        if i == 0:
                            ins = v.tensor_scalar(b, t, logit[:, 0, i, h:h + 1], None, ALU.min)
                        else:
                            v.wait_ge(bestd, 2 * (u - 1) + h + 1)
                            ins = v.scalar_tensor_tensor(b, t, logit[:, 0, i, h:h + 1], b, ALU.min, ALU.max)
                        ins.then_inc(bestd, 1)

                def take_top(g):
                    s0, k = GROUPS[g]
                    er = logit[:, 1, s0:s0 + k, :]
                    v.wait_ge(best_turned, g + 1)
                    need(v, rowed, 2 * (g - 1))
                    link(v.tensor_reduce(top[:, 0:k, :].rearrange("p k h -> p h k"), prow[:, :, 0:k, 0:P], op=ALU.max,
                                         axis=AX.X))
                    m = m_[:, 0:k, :]
                    link(v.tensor_tensor(m, top[:, 0:k, :], er, ALU.add))
                    link(v.scalar_tensor_tensor(m, m, LEAK, m, ALU.mult, ALU.max))
                    link(v.tensor_scalar(top[:, 0:k, :], top[:, 0:k, :], -BIG / 4, BIG, ALU.is_lt, ALU.mult))
                    link(v.tensor_tensor(m, m, top[:, 0:k, :], ALU.add))
                    v.tensor_scalar(r[:, g % 2, 0, 0:k, :], er, 1 - LEAK, None, ALU.mult)
                    v.scalar_tensor_tensor(r[:, g % 2, 1, 0:k, :], er, LEAK, m, ALU.mult, ALU.subtract).then_inc(rd, 1)
                    v.wait_ge(rd, g + 1)

                def rectify(u):
                    if not by_vector(u):
                        return
                    n, i = u // NB, u % NB
                    k, h, q = GROUPS[n // 2][1], n % 2, u % EB
                    v.wait_ge(row_out, n + 1)
                    need(v, leaked, u - EB + 1)
                    v.tensor_scalar(rect[:, q, 0:k * P], rows[:, n % 2, 0, 0:k * P], el_rest[:, i, h:h + 1], 0.0, ALU.add,
                                    ALU.max).then_inc(rectd_v, 1)

                def weigh(n, i):
                    s0, k = GROUPS[n // 2]
                    u = NB * n + i
                    q = u % EB
                    v.wait_ge(exps, u + 1)
                    need(v, used, u - EB + 1)
                    v.scalar_tensor_tensor(w[:, q, 0:k * P].rearrange("p (k d) -> p k d", d=P),
                                           e[:, q, 0:k * P].rearrange("p (k d) -> p k d", d=P), 1.0,
                                           C[:, s0:s0 + k, i, 0:P], ALU.min, ALU.mult).then_inc(weighed, 1)

                def beyond_cap(n, k):
                    with if_dense(v):
                        if n == 0:
                            v.sem_inc(x_used, 1)
                        with v.Fori(0, NB) as i:
                            v.wait_ge(beyond_in, i * 16 + 16 * (NB * n + 1))
                            v.wait_ge(x_exps, i + (NB * n + 1))
                            v.wait_ge(x_used, i + (NB * n + 1))
                            v.scalar_tensor_tensor(x_w[:, 0:k * P], x_e[:, 0:k * P], 1.0,
                                                   beyond[:, 0:k, :].rearrange("p k d -> p (k d)"), ALU.min,
                                                   ALU.mult).then_inc(x_weighed, 1)

                def divide(g, h):
                    k = GROUPS[g][1]
                    v.wait_ge(nturned, 2 * g + h + 1)
                    link(v.tensor_scalar(rec[:, 0:k, h, :], pot[:, 0:k, 64:65], 1e-20, None, ALU.max))
                    link(v.reciprocal(rec[:, 0:k, h, :], rec[:, 0:k, h, :]))
                    if h == 0:
                        need(v, oturned, g)
                    v.tensor_tensor(o[:, 0:k, h * 64:(h + 1) * 64], pot[:, 0:k, 0:64],
                                    rec[:, 0:k, h, :].broadcast_to((P, k, 64)), ALU.mult).then_inc(nturn_used, 1)

                for i in range(NB):
                    take_best(0, i)
                take_top(0)
                for u in range(AHEAD):
                    rectify(u)
                for g, s, h, i in group_steps():
                    n = 2 * g + h
                    if g < NG:
                        k = GROUPS[g][1]
                        if NB * n + i + AHEAD < 2 * NB * NG:
                            rectify(NB * n + i + AHEAD)
                        weigh(n, i)
                        if i == NB - 1:
                            beyond_cap(n, k)
                        if g + 1 < NG:
                            for i_ in mask_at(s):
                                take_best(g + 1, i_)
                            if s == 43:
                                take_top(g + 1)
                        if s == 39:
                            divide(g, 0)
                    if g:
                        s0, k = GROUPS[g - 1]
                        if s == 14:
                            divide(g - 1, 1)
                            v.wait_ge(nturn_used, 2 * g)
                            link(v.tensor_tensor(o[:, 0:k, :], o[:, 0:k, :],
                                                 bg[:].rearrange("p (a f) -> p a f", a=1).broadcast_to((P, k, 128)), ALU.add))
                            v.tensor_scalar(o[:, 0:k, :], o[:, 0:k, :], 0.0, None, ALU.max).then_inc(od, 1)
                        if s == 30:
                            v.wait_ge(lin, g)
                            need(v, normed, g - 1)
                            v.tensor_tensor(z[:, 0:k, :], pl[:, 0:k, :],
                                            bl[:].rearrange("p (a f) -> p a f", a=1).broadcast_to((P, k, D)),
                                            ALU.add).then_inc(lin_used, 1)
                            v.wait_ge(lin_used, g)
                            link(v.scalar_tensor_tensor(z[:, 0:k, :], z[:, 0:k, :], 0.0, X[:, s0:s0 + k, :], ALU.max, ALU.add))
                            for j in range(k):
                                m = v.bn_stats(st[:, j, :], z[:, j, :])
                            link(m)
                            for j in range(k):
                                m = v.bn_aggr(mv[:, j, :], st[:, j, :])
                            m.then_inc(stats, 1)
                        if s == 38:
                            v.wait_ge(root, g)
                            link(v.reciprocal(rs[:, 0:k], rs[:, 0:k]))
                            v.scalar_tensor_tensor(nm[:, 0:k], mv[:, 0:k, 0], -1.0, rs[:, 0:k], ALU.mult,
                                                   ALU.mult).then_inc(stats, 1)


def sort_edges(nc, own, dram, tab):
    sem = lambda n: own.semaphore("so_" + n)
    loaded, const, ranked, place, counted, turn, attr_in, slots, slots_seen, scattered = map(sem, (
        "loaded", "const", "ranked", "place", "counted", "turn", "attr_in", "slots", "slots_seen", "scattered"))
    LINKS = 6
    with ExitStack() as c, nc.Block() as block:
        sb = lambda n, s, d=F32: c.enter_context(nc.sbuf_tensor("so_" + n, s, d))
        dst_i = sb("dst_i", [P, EC], I32)
        dst, row = sb("dst", [P, EC]), sb("row", [P, EC, FIELDS])
        inb, rank, term, pos = (sb(n, [P, EC]) for n in ("inb", "rank", "term", "pos"))
        pos_i = sb("pos_i", [P, EC], U32)
        edge1 = sb("edge1", [P, EC])
        bound = sb("bound", [P, NB + 1])
        before, ones = sb("before", [P, P]), sb("ones", [P, P])
        off, base = sb("off", [P, 1]), sb("base", [P, 1])
        slot, row_slot, attr_slot = sb("slot", [P, 1], U32), sb("row_slot", [P, FIELDS]), sb("attr_slot", [P, AT])
        ps = c.enter_context(nc.psum_tensor("so_ps", [P, 2], F32))
        attr = dram["edge_attr_64"].rearrange("(p c) f -> p c f", c=EC)

        @block.sync
        def _(sp):
            unsorted = sp.value_load(tab["unsorted"][0:1, 0:1], min_val=0, max_val=1)
            with sp.If(unsorted != 0):
                sp.dma_start(dst_i[:], dram["dst"].rearrange("(p c) -> p c", c=EC)).then_inc(loaded, 16)
                sp.dma_start(row[:], dram["pairs"][0:E, :].rearrange("(p c) k -> p c k", c=EC)).then_inc(loaded, 16)
                sp.dma_start(attr_slot[:], attr[:, 0, :]).then_inc(attr_in, 16)
                with sp.Fori(1, EC) as col:
                    sp.wait_ge(scattered, col * 32)
                    sp.dma_start(attr_slot[:], attr[:, bass.ds(col, 1), :].rearrange("p a f -> p (a f)")).then_inc(attr_in, 16)

        @block.gpsimd
        def _(g):
            unsorted = g.value_load(tab["unsorted"][0:1, 0:1], min_val=0, max_val=1)
            with g.If(unsorted != 0):
                g.iota(bound[:], pattern=[[P, NB + 1]], base=0, channel_multiplier=0,
                       allow_small_or_imprecise_dtypes=True).then_inc(const, 1)
                g.memset(ones[:], 1.0).then_inc(const, 1)
                g.memset(before[:], 1.0).then_inc(const, 1)
                g.memset(edge1[:], 1.0).then_inc(const, 1)
                g.memset(pos[:], -1.0).then_inc(const, 1)
                g.memset(off[:], 0.0).then_inc(const, 1)
                g.wait_ge(const, 6)
                g.affine_select(out=before[:], in_=before[:], compare_op=ALU.is_gt, fill=0.0, base=0,
                                pattern=[[1, P]], channel_multiplier=-1).then_inc(const, 1)
                g.wait_ge(place, 1)
                with g.Fori(0, EC) as col:
                    g.tensor_copy(slot[:], pos_i[:, bass.ds(col, 1)]).then_inc(slots, 1)
                    g.tensor_copy(row_slot[:], row[:, bass.ds(col, 1), :].rearrange("p a k -> p (a k)")).then_inc(slots, 1)
                    g.wait_ge(slots, col * 2 + 2)
                    g.wait_ge(attr_in, col * 16 + 16)
                    g.sem_inc(slots_seen, 1)
                    for rows, out in ((row_slot, "pairs"), (attr_slot, "attr_s")):
                        g.indirect_dma_start(out=dram[out], out_offset=bass.IndirectOffsetOnAxis(ap=slot[:], axis=0),
                                             in_=rows[:], in_offset=None).then_inc(scattered, 16)
                    g.wait_ge(scattered, col * 32 + 32)
                    g.sem_inc(slots_seen, 1)

        @block.tensor
        def _(pe):
            unsorted = pe.value_load(tab["unsorted"][0:1, 0:1], min_val=0, max_val=1)
            with pe.If(unsorted != 0):
                pe.wait_ge(const, 7)
                with pe.Fori(0, NB) as b:
                    pe.wait_ge(ranked, b * LINKS + 3)
                    nc.tensor.matmul(ps[:, 0:1], before[:], rank[:, EC - 1:EC], start=True, stop=True)
                    nc.tensor.matmul(ps[:, 1:2], ones[:], rank[:, EC - 1:EC], start=True, stop=True).then_inc(counted, 1)

        @block.vector
        def _(v):
            unsorted = v.value_load(tab["unsorted"][0:1, 0:1], min_val=0, max_val=1)
            with v.If(unsorted != 0):
                v.wait_ge(loaded, 32)
                v.wait_ge(const, 7)
                v.tensor_copy(dst[:], dst_i[:]).then_inc(turn, 1)
                v.wait_ge(turn, 1)
                with v.Fori(0, NB) as b:
                    n = [0]

                    def link(ins):
                        n[0] += 1
                        ins.then_inc(ranked, 1)
                        v.wait_ge(ranked, b * LINKS + n[0])
                    link(v.tensor_scalar(term[:], dst[:], bound[:, bass.ds(b, 1)], None, ALU.is_ge))
                    link(v.scalar_tensor_tensor(inb[:], dst[:], bound[:, bass.ds(b + 1, 1)], term[:], ALU.is_lt, ALU.mult))
                    link(v.tensor_tensor_scan(rank[:], edge1[:], inb[:], 0.0, ALU.mult, ALU.add))
                    v.wait_ge(counted, b + 1)
                    link(v.tensor_tensor(base[:], ps[:, 0:1], off[:], ALU.add))
                    v.tensor_tensor(off[:], ps[:, 1:2], off[:], ALU.add)
                    link(v.scalar_tensor_tensor(term[:], rank[:], base[:], inb[:], ALU.add, ALU.mult))
                    link(v.tensor_tensor(pos[:], pos[:], term[:], ALU.add))
                v.tensor_copy(pos_i[:], pos[:]).then_inc(place, 1)


def graph_network(nc, dram):
    with ExitStack() as ctx:
        sb = lambda n, s, d=F32: ctx.enter_context(nc.sbuf_tensor(n, s, d))
        tab = dict(unsorted=sb("unsorted", [1, 1], I32),
                   tbeg=sb("tbeg", [1, NB], I32), tend=sb("tend", [1, NB], I32), bucket=sb("bucket", [1, NT], I32),
                   e0=sb("e0", [1, NT], I32), first=sb("first", [ET, NT]),
                   dense=sb("dense", [1, 1], I32), unscale=sb("unscale", [128, 2, 2]))
        for n in ("deg", "mean", "degmean", "dinv", "dinv_x"):
            tab[n] = sb(n, [P, NB])

        def phase(build, *args):
            own = Semaphores(nc)
            build(nc, own, *args)
            own.release()
        phase(index_tables, dram, tab)
        phase(sort_edges, dram, tab)
        tab["counts"] = sb("counts8", [P, NB, NB, 128], F8)
        tab["X"] = sb("X", [P, NB, D])
        with ExitStack() as c:
            tab["parts"] = [c.enter_context(nc.sbuf_tensor(f"part{i}", [P, NB * D], F16)) for i in range(3)]
            phase(count_edges, dram, tab, False)
            phase(count_edges, dram, tab, True)
            tab["parts"] += [c.enter_context(nc.sbuf_tensor(f"part{i}", [P, NB * D], F16)) for i in (3, 4)]
            rows = {n: c.enter_context(nc.sbuf_tensor("row_" + n, [P, 3, D], F32))
                    for n in ("b", "gamma", "beta")}
            phase(node_scales, dram, tab, rows)
            phase(conv_layer, dram, tab, rows, 0)
            phase(self_loops, tab, 1)
            for L in (1, 2, 3):
                phase(conv_layer, dram, tab, rows, L)
            phase(self_loops, tab, 0)
        tab["heads"] = sb("heads", [P, NB, 2, 65])
        tab["logit"] = sb("logit", [P, 2, NB, 2])
        with ExitStack() as c:
            tab["aggr"] = c.enter_context(nc.sbuf_tensor("aggr", [P, NB + 1, D], F32))
            phase(gated_messages, dram, tab)
            phase(update_nodes, dram, tab)
        phase(attention, dram, tab)


_INS = ["x", "src", "dst", "edge_attr_64", "L0_gnn_W", "L0_gnn_b", "L1_gnn_W", "L1_gnn_b", "L1_gnn_gamma",
        "L1_gnn_beta", "L2_gnn_W1", "L2_gnn_b1", "L2_gnn_W2", "L2_gnn_b2", "L2_gnn_U1", "L2_gnn_c1", "L2_gnn_U2",
        "L2_gnn_c2", "L3_gnn_W", "L3_gnn_attn_l", "L3_gnn_attn_r", "L3_gnn_gat_bias", "L3_gnn_lin_W",
        "L3_gnn_lin_b"]
_SCRATCH = [("pairs", (EPAD, FIELDS), F32), ("table", (N, D), F32),
            ("attr_s", (EPAD, AT), F32), ("beyond", (NB, P, N), F32)]


def declare(nc, arrays):
    dram = {n: nc.dram_tensor("in_" + n, a.shape, mybir.dt.from_np(a.dtype), kind="ExternalInput").ap()
            for n, a in arrays.items()}
    for n, shape, dt in _SCRATCH:
        dram[n] = nc.dram_tensor(n, shape, dt).ap()
    dram["out"] = nc.dram_tensor("out", (N, D), F32, kind="ExternalOutput").ap()
    return dram


def kernel(**inputs):
    import concourse.bacc as bacc
    from concourse.bass_utils import run_bass_kernel_spmd

    nc = bacc.Bacc("TRN2", target_bir_lowering=False, num_devices=1)
    arrays = {n: np.ascontiguousarray(inputs[n]) for n in _INS}
    graph_network(nc, declare(nc, arrays))
    r = run_bass_kernel_spmd(nc, [{"in_" + n: a for n, a in arrays.items()}], core_ids=[0])
    return r.results[0]["out"]
```

```python
import numpy as np
import concourse.bass as bass
from concourse import mybir
from contextlib import ExitStack, nullcontext

F32, F16, BF16, I32, U32, I16, F8 = (mybir.dt.float32, mybir.dt.float16, mybir.dt.bfloat16, mybir.dt.int32,
                                     mybir.dt.uint32, mybir.dt.int16, mybir.dt.float8e4)
ALU = mybir.AluOpType
ACT = mybir.ActivationFunctionType
AX = mybir.AxisListType

N, E, D = 3125, 50000, 256
P = 125
NB = N // P
EC = E // P
ET = 128
U = 4
NT = -(-(E // ET + 1 + NB) // U) * U
EPAD = E + ET
AT = 64
BIG_DST = 4000.0
BANK = 512
FIELDS = 4
ROUND = 12582912.0


def index_tables(nc, ctx, dram, tab):
    with ExitStack() as c:
        sb = lambda n, s, d: c.enter_context(nc.sbuf_tensor(n, s, d))
        sem = lambda n: ctx.semaphore(n)
        src_i = sb("src_i", [P, EC], I32)
        dst_i = sb("dst_i", [P, EC], I32)
        dst_f = sb("dst_f", [P, EC], F32)
        row = sb("row", [P, EC, FIELDS], F32)
        tile = sb("tile", [P, EC], F32)
        below = sb("below", [P, EC], F32)
        cnt = sb("cnt", [P, NB + 1], F32)
        ones = sb("ones", [P, P], F32)
        padrow = sb("padrow", [1, FIELDS * ET], F32)
        padattr = sb("padattr", [ET, AT], F32)
        next_i = sb("next_i", [P, EC], I32)
        back = sb("back", [P, EC], F32)
        backs = sb("backs", [P, 1], F32)
        ps_col = c.enter_context(nc.psum_tensor("ps_col", [NB, 2], F32))
        ps_t = c.enter_context(nc.psum_tensor("ps_t", [128, NT], F32))
        ps_e = c.enter_context(nc.psum_tensor("ps_e", [1, NT], F32))
        ps_tend = c.enter_context(nc.psum_tensor("ps_tend", [1, NB], F32))
        ps_back = c.enter_context(nc.psum_tensor("ps_back", [1, 1], F32))
        cntb = sb("cntb", [NB, 1], F32)
        ntb = sb("ntb", [NB, 1], F32)
        delta = sb("delta", [NB, 1], F32)
        tendb = sb("tendb", [NB, 1], F32)
        ones25 = sb("ones25", [NB, 128], F32)
        tri25 = sb("tri25", [NB, NB], F32)
        eye25 = sb("eye25", [NB, NB], F32)
        iot = sb("iot", [NB, NT], F32)
        past = sb("past", [NB, NT], F32)
        dvals = sb("dvals", [NB, 1], F32)
        i128 = sb("i128", [1, NT], F32)
        e0f = sb("e0f", [1, NT], F32)
        loaded, const, rows_made, written, hist_done, column_sums, deltas, tile_ends = [sem("ix_" + n) for n in (
            "loaded", "const", "rows_made", "written", "hist", "column_sums", "deltas", "tile_ends")]
        past_done, table_done, chain, tile_sums = [sem("ix_" + n) for n in ("past", "table", "chain", "tile_sums")]
        next_zeroed, next_in, backs_done, back_sum, row_steps = [sem("ix_" + n) for n in (
            "next_zeroed", "next_in", "backs", "back_sum", "row_steps")]
        with nc.Block() as block:
            @block.sync
            def _(sp):
                sp.dma_start(dst_i[:], dram["dst"].rearrange("(p c) -> p c", c=EC)).then_inc(loaded, 16)
                sp.dma_start(src_i[:], dram["src"].rearrange("(p c) -> p c", c=EC)).then_inc(loaded, 16)
                sp.wait_ge(next_zeroed, 1)
                sp.dma_start(next_i[0:P - 1, :], dram["dst"][1:E - EC + 1].rearrange("(p c) -> p c", c=EC)).then_inc(next_in, 16)
                sp.dma_start(next_i[P - 1:P, 0:EC - 1], dram["dst"][E - EC + 1:E].rearrange("(p c) -> p c", p=1)).then_inc(next_in, 16)
                sp.wait_ge(rows_made, 1)
                sp.dma_start(dram["pairs"][0:E, :].rearrange("(p c) k -> p (c k)", c=EC),
                             row[:].rearrange("p c k -> p (c k)")).then_inc(written, 16)
                sp.wait_ge(const, 9)
                sp.dma_start(dram["pairs"][E:EPAD, :].rearrange("(a e) k -> a (e k)", a=1), padrow[:]).then_inc(written, 16)
                sp.dma_start(dram["attr_s"][E:EPAD, :], padattr[:]).then_inc(written, 16)
                sp.wait_ge(written, 48)

            @block.gpsimd
            def _(g):
                g.memset(padattr[:], 0.0).then_inc(const, 1)
                g.memset(ones[:], 1.0).then_inc(const, 1)
                g.memset(ones25[:], 1.0).then_inc(const, 1)
                g.memset(tri25[:], 1.0).then_inc(const, 1)
                g.memset(eye25[:], 0.0).then_inc(const, 1)
                g.memset(padrow[:], BIG_DST).then_inc(const, 1)
                g.wait_ge(const, 6)
                g.affine_select(out=tri25[:], in_=tri25[:], compare_op=ALU.is_ge, fill=0.0, base=0,
                                pattern=[[1, NB]], channel_multiplier=-1).then_inc(const, 1)
                g.affine_select(out=eye25[:], in_=eye25[:], compare_op=ALU.not_equal, fill=1.0, base=0,
                                pattern=[[-1, NB]], channel_multiplier=1).then_inc(const, 1)
                g.memset(padrow[:].rearrange("a (e k) -> a e k", k=FIELDS)[:, :, 0:1], 0.0).then_inc(const, 1)
                g.iota(iot[:], pattern=[[1, NT]], base=0, channel_multiplier=0,
                       allow_small_or_imprecise_dtypes=True).then_inc(const, 1)
                g.iota(i128[:], pattern=[[ET, NT]], base=0, channel_multiplier=0,
                       allow_small_or_imprecise_dtypes=True).then_inc(const, 1)

            @block.vector
            def _(v):
                v.memset(next_i[:], 1 << 20).then_inc(next_zeroed, 1)
                v.wait_ge(loaded, 32)
                v.tensor_copy(row[:, :, 0], src_i[:])
                v.tensor_copy(row[:, :, 1], dst_i[:]).then_inc(row_steps, 1)
                v.wait_ge(row_steps, 1)
                v.tensor_scalar(tile[:], row[:, :, 0], -float(P // 2), 1.0 / P, ALU.add, ALU.mult).then_inc(row_steps, 1)
                v.wait_ge(row_steps, 2)
                v.tensor_scalar(tile[:], tile[:], ROUND, None, ALU.add).then_inc(row_steps, 1)
                v.wait_ge(row_steps, 3)
                v.tensor_scalar(tile[:], tile[:], -ROUND, float(P), ALU.add, ALU.mult).then_inc(row_steps, 1)
                v.wait_ge(row_steps, 4)
                v.tensor_tensor(row[:, :, 2], row[:, :, 0], tile[:], ALU.subtract)
                v.tensor_tensor(row[:, :, 3], row[:, :, 1], tile[:], ALU.add).then_inc(rows_made, 1)
                v.tensor_copy(dst_f[:], dst_i[:]).then_inc(chain, 1)
                v.wait_ge(chain, 1)
                for b in range(NB + 1):
                    if b:
                        v.wait_ge(hist_done, b)
                    v.tensor_scalar(below[:], dst_f[:], float(b * P), None, ALU.is_lt, ALU.add,
                                    accum_out=cnt[:, b:b + 1]).then_inc(hist_done, 1)
                v.wait_ge(next_in, 32)
                v.tensor_tensor(back[:], next_i[:], dst_i[:], ALU.is_lt).then_inc(backs_done, 1)
                v.wait_ge(backs_done, 1)
                v.tensor_reduce(backs[:], back[:], op=ALU.add, axis=AX.X).then_inc(backs_done, 1)
                v.wait_ge(back_sum, 1)
                v.tensor_scalar(tab["unsorted"][:], ps_back[:], 1.0, None, ALU.min)
                v.wait_ge(column_sums, 1)
                v.tensor_copy(dvals[:], ps_col[:, 0:1]).then_inc(chain, 1)
                v.wait_ge(chain, 2)
                v.tensor_tensor(cntb[:], ps_col[:, 1:2], dvals[:], ALU.subtract).then_inc(chain, 1)
                v.wait_ge(chain, 3)
                v.tensor_scalar(ntb[:], cntb[:], 63.5, 1.0 / ET, ALU.add, ALU.mult).then_inc(chain, 1)
                v.wait_ge(chain, 4)
                v.tensor_scalar(tendb[:], ntb[:], 8388608.0, None, ALU.add).then_inc(chain, 1)
                v.wait_ge(chain, 5)
                v.tensor_scalar(ntb[:], tendb[:], 8388608.0, 1.0, ALU.subtract, ALU.max).then_inc(chain, 1)
                v.wait_ge(chain, 6)
                v.tensor_scalar(delta[:], ntb[:], -float(ET), None, ALU.mult).then_inc(chain, 1)
                v.wait_ge(chain, 7)
                v.tensor_tensor(delta[:], delta[:], cntb[:], ALU.add).then_inc(deltas, 1)
                v.wait_ge(tile_ends, 1)
                v.tensor_copy(tab["tend"][:], ps_tend[:])
                v.memset(tab["tbeg"][:, 0:1], 0)
                v.tensor_copy(tab["tbeg"][:, 1:NB], ps_tend[:, 0:NB - 1])
                v.tensor_copy(tendb[:], ps_col[:, 0:1]).then_inc(chain, 1)
                v.wait_ge(chain, 8)
                v.wait_ge(const, 11)
                v.tensor_scalar(past[:], iot[:], tendb[:], None, ALU.is_ge).then_inc(past_done, 1)
                v.wait_ge(tile_sums, 2)
                v.tensor_copy(tab["bucket"][:], ps_t[0:1, :])
                v.tensor_scalar(tab["first"][:], ps_t[:], float(P), None, ALU.mult)
                v.tensor_tensor(e0f[:], ps_e[:], i128[:], ALU.add).then_inc(chain, 1)
                v.wait_ge(chain, 9)
                v.tensor_scalar(tab["e0"][:], e0f[:], float(E), None, ALU.min).then_inc(table_done, 1)
                v.wait_ge(table_done, 1)

            @block.tensor
            def _(t):
                t.wait_ge(const, 11)
                t.wait_ge(hist_done, NB + 1)
                t.wait_ge(backs_done, 2)
                nc.tensor.matmul(ps_back[:], backs[:], ones[:, 0:1], start=True, stop=True).then_inc(back_sum, 1)
                nc.tensor.matmul(ps_col[:, 0:1], cnt[:, 0:NB], ones[:, 0:1], start=True, stop=True)
                nc.tensor.matmul(ps_col[:, 1:2], cnt[:, 1:NB + 1], ones[:, 0:1], start=True, stop=True).then_inc(column_sums, 1)
                t.wait_ge(deltas, 1)
                nc.tensor.matmul(ps_tend[:], ntb[:], tri25[:], start=True, stop=True)
                nc.tensor.matmul(ps_col[:, 0:1], tri25[:], ntb[:], start=True, stop=True).then_inc(tile_ends, 1)
                t.wait_ge(past_done, 1)
                nc.tensor.matmul(ps_t[:], ones25[:], past[:], start=True, stop=True).then_inc(tile_sums, 1)
                nc.tensor.matmul(ps_e[:], delta[:], past[:], start=True, stop=True).then_inc(tile_sums, 1)


class Semaphores:

    def __init__(self, nc):
        self.nc, self.held = nc, []

    def semaphore(self, name):
        self.held.append(self.nc.alloc_semaphore(name=name))
        return self.held[-1]

    def release(self):
        self.nc.all_engine_barrier()
        self.nc.clear_and_free_semaphores(self.held)
        self.nc.all_engine_barrier()


MOV = 4
GROUPS = [(g, min(MOV, NB - g)) for g in range(0, NB, MOV)]
NG = len(GROUPS)
UB = 16
OHR = 4


CAP = 15.0


def count_edges(nc, own, dram, tab, again):
    def chosen(eng):
        if not again:
            return nullcontext()
        return eng.If(eng.value_load(tab["dense"][0:1, 0:1], min_val=0, max_val=1) != 0)

    with ExitStack() as c:
        sb = lambda n, s, d=F32: c.enter_context(nc.sbuf_tensor(f"ct{again}_{n}", s, d))
        sem = lambda n: own.semaphore(f"ct{again}_{n}")
        X, counts = tab["X"], tab["counts"]
        parts = [t[:].bitcast(BF16).rearrange("p (b f) -> p b f", f=D) for t in tab["parts"][0:3]]
        iota = sb("iota", [ET, N], I16)
        oh_s = sb("oh_s", [ET, OHR, P], BF16)
        oh_k = sb("oh_k", [ET, OHR, N], BF16)
        zero = sb("zero", [ET, BANK], BF16)
        edge = sb("edge", [ET, UB, FIELDS])
        valid = sb("valid", [ET, UB])
        over = sb("over", [P, 2 * NB])
        over_sum = sb("over_sum", [P, 1])
        minus_cap = sb("minus_cap", [P, 1])
        by_lane = sb("by_lane", [P, NB, P])
        ones = sb("ones", [P, 1])
        if again:
            exact = sb("exact", [P, 2, MOV, P])
            beyond = sb("beyond", [P, 2, MOV, P])
        else:
            rest = sb("rest", [P, 2, D])
            tree = sb("tree", [P, NB // 2, P])
            junk = sb("junk", [P, NB - NB // 2, P], BF16)
        acc = c.enter_context(nc.psum_tensor(f"ct{again}_acc", [P, NG, BANK], F32))
        ps_end = c.enter_context(nc.psum_tensor(f"ct{again}_end", [P, NB + 1], F32))
        edge_in = [sem(f"edge{j}") for j in range(UB)]
        const, onehot, pe_done, validd, x_in, part, restd, attr_copied, treed, laned, overd, endd = map(sem, (
            "const", "onehot", "pe", "valid", "x_in", "part", "rest", "attr_copied", "tree", "laned", "over", "end"))
        exactd, clipped, beyondd = map(sem, ("exact", "clipped", "beyond"))
        beyond_out = [sem("beyond_out0"), sem("beyond_out1")]
        bank_sum = [sem(f"sum{g}") for g in range(NG)]
        bank_out = [sem(f"bank{g}") for g in range(NG)]
        NCONST = 5

        def load_edges(sp):
            def load(t, j, first):
                e0 = sp.value_load(tab["e0"][0:1, bass.ds(t, 1)], min_val=0, max_val=E)
                if not first:
                    sp.wait_ge(onehot, t - (UB - 1))
                sp.dma_start(edge[:, j, :], dram["pairs"][bass.ds(e0, ET), :]).then_inc(edge_in[j], 16)
            for j in range(UB):
                load(j, j, True)
            if not again:
                sp.dma_start(X[:], dram["x"].rearrange("(b p) f -> p b f", p=P)).then_inc(x_in, 16)
            with sp.Fori(UB, NT - UB + 1, UB) as t:
                for j in range(UB):
                    load(t + j, j, False)

        def onehot_rows(v):
            v.wait_ge(const, NCONST)

            def onehots(t, j, loads, first):
                v.wait_ge(edge_in[j], loads)
                r = j % OHR
                begins = tab["first"][:, bass.ds(t, 1)]
                v.tensor_scalar(valid[:, j:j + 1], edge[:, j, 1:2], begins, P - 0.5, ALU.subtract, ALU.is_le).then_inc(validd, 1)
                if not first:
                    v.wait_ge(pe_done, t - (OHR - 1))
                v.tensor_scalar(oh_k[:, r, :], iota[:], begins, edge[:, j, 3:4], ALU.add, ALU.is_equal)
                v.wait_ge(validd, t + 1)
                v.tensor_scalar(oh_s[:, r, :], iota[:, 0:P], edge[:, j, 2:3], valid[:, j:j + 1], ALU.is_equal,
                                ALU.mult).then_inc(onehot, 1)
            for j in range(UB):
                onehots(j, j, 16, j < OHR)
            with v.Fori(UB, NT - UB + 1, UB) as t:
                for j in range(UB):
                    onehots(t + j, j, t * (16 // UB) + 16, False)
            if not again:
                v.wait_ge(overd, 2 * NB)
                v.tensor_reduce(over_sum[:], over[:], op=ALU.add, axis=AX.X).then_inc(overd, 1)
            v.wait_ge(endd, 1)
            if not again:
                v.tensor_scalar(tab["dense"][:], ps_end[0:1, NB:NB + 1], 1.0, None, ALU.min)
            v.tensor_copy(tab["deg"][:], ps_end[:, 0:NB])

        def count(pe):
            pe.wait_ge(const, NCONST)

            def product(g, k, lhs, rhs, start, stop):
                return nc.tensor.matmul(acc[0:P, g, 0:k * P], lhs, rhs, start=start, stop=stop)

            end = pe.value_load(tab["tend"][0:1, NB - 1:NB], min_val=NB, max_val=NT - 1)
            with pe.Fori(0, NB) as b:
                lo = pe.value_load(tab["tbeg"][0:1, bass.ds(b, 1)], min_val=0, max_val=NT - 2)
                hi = pe.value_load(tab["tend"][0:1, bass.ds(b, 1)], min_val=1, max_val=NT - 1)
                def tile(t, begin, end_):
                    pe.wait_ge(onehot, t + 1)
                    r = t % OHR
                    for g, (s0, k) in enumerate(GROUPS):
                        if begin:
                            pe.wait_ge(bank_out[g], b + 1)
                        last = product(g, k, oh_s[:, bass.ds(r, 1), :].rearrange("p a n -> p (a n)"),
                                       oh_k[:, bass.ds(r, 1), s0 * P:(s0 + k) * P].rearrange("p a n -> p (a n)"),
                                       begin, end_)
                        if end_:
                            last.then_inc(bank_sum[g], 1)
                    if end_:
                        pe.wait_ge(bank_sum[NG - 1], b + 1)
                        pe.sem_inc(pe_done, 1)
                    else:
                        last.then_inc(pe_done, 1)

                with pe.If(hi == lo + 1):
                    tile(lo, True, True)
                with pe.If(hi > lo + 1):
                    tile(lo, True, False)
                    with pe.If(hi > lo + 2):
                        with pe.Fori(lo + 1, hi - 1) as t:
                            tile(t, False, False)
                    tile(hi - 1, False, True)
            pe.wait_ge(const, NCONST)
            pe.wait_ge(pe_done, end)
            with pe.Fori(end, NT) as t:
                pe.wait_ge(onehot, t + 1)
                pe.sem_inc(pe_done, 1)
            pe.wait_ge(laned, NB * NB if again else NB)
            for b in range(NB):
                m = nc.tensor.matmul(ps_end[:, b:b + 1], by_lane[:, b, :], ones[:], start=True, stop=True)
            if not again:
                pe.wait_ge(overd, 2 * NB + 1)
                m = nc.tensor.matmul(ps_end[0:1, NB:NB + 1], over_sum[:], ones[:], start=True, stop=True)
            m.then_inc(endd, 1)

        def constants(g):
            g.iota(iota[:], pattern=[[1, N]], base=0, channel_multiplier=0).then_inc(const, 1)
            g.memset(zero[:], 0.0).then_inc(const, 1)
            g.memset(ones[:], 1.0).then_inc(const, 1)
            g.memset(minus_cap[:], -CAP).then_inc(const, 1)
            g.memset(by_lane[:], 0.0).then_inc(const, 1)

        def sum_tiles(g):
            g.wait_ge(const, NCONST)
            n = [0]

            def link(ins):
                n[0] += 1
                ins.then_inc(treed, 1)
                g.wait_ge(treed, n[0])

            for b in range(NB):
                for i in range(NG):
                    g.wait_ge(bank_out[i], b + 2)
                link(g.tensor_tensor(tree[:], counts[:, b, 0:12, 0:P], counts[:, b, 12:24, 0:P], ALU.add))
                for w in (6, 3):
                    link(g.tensor_tensor(tree[:, 0:w, :], tree[:, 0:w, :], tree[:, w:2 * w, :], ALU.add))
                link(g.tensor_tensor(tree[:, 0, :], tree[:, 0, :], tree[:, 1, :], ALU.add))
                link(g.tensor_tensor(tree[:, 2, :], tree[:, 2, :], counts[:, b, 24, 0:P], ALU.add))
                g.tensor_tensor(by_lane[:, b, :], tree[:, 0, :], tree[:, 2, :], ALU.add).then_inc(laned, 1)
                g.wait_ge(laned, b + 1)

        def clip_and_store(g):
            g.wait_ge(const, NCONST)
            for b in range(NB):
                for i, (s0, k) in enumerate(GROUPS):
                    m = b * NG + i
                    q = m % 2
                    g.wait_ge(exactd, m + 1)
                    need(g, beyond_out[q], 16 * (m // 2))
                    g.tensor_scalar(beyond[:, q, 0:k, :], exact[:, q, 0:k, :], -CAP, 0.0, ALU.add, ALU.max).then_inc(beyondd, 1)
                    g.wait_ge(beyondd, m + 1)
                    g.tensor_tensor(counts[:, b, s0:s0 + k, 0:P], exact[:, q, 0:k, :], beyond[:, q, 0:k, :],
                                    ALU.subtract, saturate=False)
                    for j in range(k):
                        step = g.tensor_tensor(by_lane[:, b, :], by_lane[:, b, :], exact[:, q, j, :], ALU.add)
                        step.then_inc(laned, 1)
                        g.wait_ge(laned, b * NB + s0 + j + 1)
                    g.sem_inc(clipped, 1)
                    g.dma_start(dram["beyond"][b, :, s0 * P:(s0 + k) * P],
                                beyond[:, q, 0:k, :].rearrange("p k d -> p (k d)")).then_inc(beyond_out[q], 16)
            for q in range(2):
                g.wait_ge(beyond_out[q], 16 * ((NB * NG + 1 - q) // 2))

        with nc.Block() as block:
            @block.sync
            def _(sp):
                with chosen(sp):
                    load_edges(sp)

            @block.gpsimd
            def _(g):
                with chosen(g):
                    constants(g)
                    if again:
                        clip_and_store(g)
                if again:
                    return
                unsorted = g.value_load(tab["unsorted"][0:1, 0:1], min_val=0, max_val=1)
                with g.If(unsorted == 0):
                    g.dma_start(dram["attr_s"][0:E, :].rearrange("(a e) f -> a (e f)", a=400),
                                dram["edge_attr_64"].rearrange("(a e) f -> a (e f)", a=400)).then_inc(attr_copied, 16)
                    g.wait_ge(attr_copied, 16)
                for b in range(NB):
                    g.wait_ge(part, 3 * b + 1)
                    g.tensor_tensor(rest[:, 0, :], X[:, b, :], parts[0][:, b, :], ALU.subtract).then_inc(restd, 1)
                    g.wait_ge(part, 3 * b + 2)
                    g.wait_ge(restd, 2 * b + 1)
                    g.tensor_tensor(rest[:, 1, :], rest[:, 0, :], parts[1][:, b, :], ALU.subtract).then_inc(restd, 1)
                sum_tiles(g)

            @block.vector
            def _(v):
                with chosen(v):
                    onehot_rows(v)

            @block.tensor
            def _(pe):
                with chosen(pe):
                    count(pe)

            @block.scalar
            def _(a):
                with chosen(a):
                    for g in range(NG):
                        a.sem_inc(bank_out[g], 1)
                    if not again:
                        a.wait_ge(x_in, 16)
                        a.wait_ge(const, NCONST)
                        for b in range(NB):
                            a.copy(parts[0][:, b, :], X[:, b, :]).then_inc(part, 1)
                            for n in (1, 2):
                                a.wait_ge(restd, 2 * b + n)
                                a.copy(parts[n][:, b, :], rest[:, n - 1, :]).then_inc(part, 1)
                    for b in range(NB):
                        for g, (s0, k) in enumerate(GROUPS):
                            m = b * NG + g
                            a.wait_ge(bank_sum[g], b + 1)
                            sums = acc[0:P, g, 0:k * P].rearrange("p (k d) -> p k d", d=P)
                            if again:
                                need(a, clipped, m - 1)
                                a.copy(exact[:, m % 2, 0:k, :], sums).then_inc(exactd, 1)
                                a.wait_ge(exactd, m + 1)
                                a.sem_inc(bank_out[g], 1)
                            else:
                                a.copy(counts[:, b, s0:s0 + k, 0:P], sums, saturate=True).then_inc(bank_out[g], 1)
                        if not again:
                            for g in range(NG):
                                a.wait_ge(bank_out[g], b + 2)
                            for half, tiles in enumerate((slice(0, NB // 2), slice(NB // 2, NB))):
                                m = 2 * b + half
                                need(a, overd, m)
                                a.activation(junk[:, 0:tiles.stop - tiles.start, :], counts[:, b, tiles, 0:P], ACT.Relu,
                                             bias=minus_cap[:], accum_out=over[:, m:m + 1]).then_inc(overd, 1)


def conv_layers(nc, ctx, dram, tab, rows):
    with ExitStack() as c:
        sb = lambda n, s, d: c.enter_context(nc.sbuf_tensor("cv_" + n, s, d))
        Q = tab["parts"]
        three = [t[:].bitcast(BF16).rearrange("p (b f) -> p b f", f=D) for t in Q[0:3]]
        even, odd = ([t[:].rearrange("p (b f) -> p b f", f=D) for t in pair] for pair in (Q[0:2], Q[3:5]))
        sources = [(three, odd), (odd, even), (even, odd), (odd, even)]
        C, X = tab["counts"], tab["X"]
        W = sb("W", [128, 2, D], F32)
        yt = sb("yt", [128, 2, 2, MOV * P], F32)
        a_ = sb("a", [P, MOV, D], F32)
        st = sb("st", [P, MOV, 6], F32)
        mv = sb("mv", [P, MOV, 2], F32)
        rs = sb("rs", [P, MOV], F32)
        nm = sb("nm", [P, MOV], F32)
        eps = sb("eps", [P, 1], F32)
        eye = sb("eye", [128, 128], F32)
        work = sb("work", [128, MOV, D], F32)
        tmp = work[0:P]
        wt, b0 = work[:, 0:2, :], work[0:P, 2, :]
        beyond = sb("beyond", [P, MOV, P], F32)
        whole = sb("whole", [P, MOV, P], F32)
        digits16 = sb("digits", [P, 2, MOV, P], F16)
        pb = lambda n, s: c.enter_context(nc.psum_tensor("cv_" + n, s, F32))
        py = pb("py", [128, 2, 2, BANK])
        po = pb("po", [P, 2, MOV, D])
        names = ("w_in summed y_out projected o_out vch stats rooted centred affine last_stats relued "
                 "high low stored pch beyond_in digit_steps digits_done digits_used digits_seen").split()
        signals = [{n: ctx.semaphore(f"l{L}_{n}") for n in names} for L in range(4)]
        epsd, eyed, turned, loops = map(ctx.semaphore, ("eps", "eye", "turned", "loops"))
        rows_in, scale_steps, rooted_deg = map(ctx.semaphore, ("rows_in", "scale_steps", "rooted_deg"))
        colg, colb = sb("colg", [128, 2, 2], F32), sb("colb", [128, 2, 2], F32)
        root, deg1 = sb("root", [P, NB], F32), sb("deg1", [P, NB], F32)

        def load_rows(sp):
            for n in ("b", "gamma", "beta"):
                for l in range(3):
                    sp.dma_start(rows[n][:, l, :], dram["L1_gnn_" + n][l].partition_broadcast(P)).then_inc(rows_in, 16)
            with nc.allow_non_contiguous_dma(reason="512 numbers, once"):
                for l in range(2):
                    sp.dma_start(colg[:, l, :], dram["L1_gnn_gamma"][l].rearrange("(h p) -> p h", h=2)).then_inc(rows_in, 16)
                    sp.dma_start(colb[:, l, :], dram["L1_gnn_beta"][l].rearrange("(h p) -> p h", h=2)).then_inc(rows_in, 16)

        def scales(v):
            absg, absb = a_[:, 0:2, :], a_[:, 2:4, :]
            n = [0]

            def link(ins):
                n[0] += 1
                ins.then_inc(scale_steps, 1)
                v.wait_ge(scale_steps, n[0])

            link(v.tensor_scalar(deg1[:], tab["deg"][:], 1.0, None, ALU.add))
            link(v.reciprocal(tab["mean"][:], deg1[:]))
            link(v.tensor_tensor(tab["degmean"][:], tab["mean"][:], tab["deg"][:], ALU.mult))
            v.wait_ge(rooted_deg, 1)
            link(v.reciprocal(tab["dinv"][:], root[:]))
            link(v.tensor_scalar(tab["dinv_x"][:], tab["dinv"][:], 128.0, None, ALU.mult))
            v.wait_ge(rows_in, 16 * 13)
            for g_, b_, ag, ab, out in (
                    (rows["gamma"][:, 0:2, :], rows["beta"][:, 0:2, :], absg, absb, absg),
                    (colg[:], colb[:], colg[:], colb[:], tab["unscale"][:])):
                link(v.scalar_tensor_tensor(ag, g_, -1.0, g_, ALU.mult, ALU.max))
                link(v.scalar_tensor_tensor(ab, b_, -1.0, b_, ALU.mult, ALU.max))
                link(v.scalar_tensor_tensor(ag, ag, 16.0, ab, ALU.mult, ALU.add))
                link(v.tensor_scalar(out, ag, 1.0 / 2048, 1e-30, ALU.mult, ALU.max))
            link(v.reciprocal(absb, absg))
            link(v.tensor_tensor(rows["gamma"][:, 0:2, :], rows["gamma"][:, 0:2, :], absb, ALU.mult))
            link(v.tensor_tensor(rows["beta"][:, 0:2, :], rows["beta"][:, 0:2, :], absb, ALU.mult))

        def layer(L):
            digits = digits16[:] if L else digits16[:].bitcast(BF16)
            return signals[L], signals[L - 1] if L else None, *sources[L], digits, L == 3

        def if_dense(eng):
            return eng.If(eng.value_load(tab["dense"][0:1, 0:1], min_val=0, max_val=1) != 0)

        with nc.Block() as block:
            @block.sync
            def _(sp):
                for L in range(4):
                    S, before, parts, nxt, digits, last_layer = layer(L)
                    if L == 0:
                        sp.dma_start(wt, dram["L0_gnn_W"].rearrange("(h p) i -> p h i", p=128)).then_inc(S["w_in"], 16)
                        sp.dma_start(b0, dram["L0_gnn_b"].partition_broadcast(P)).then_inc(S["w_in"], 16)
                        load_rows(sp)
                    else:
                        sp.wait_ge(before["projected"], NG)
                        sp.dma_start(W[:], dram["L1_gnn_W"][L - 1].rearrange("(h p) o -> p h o", p=128)).then_inc(S["w_in"], 16)
                    with if_dense(sp):
                        for g, (s0, k) in enumerate(GROUPS):
                            with sp.Fori(0, NB) as i:
                                sp.wait_ge(S["digits_done"], i + (g * NB + 1))
                                sp.dma_start(beyond[:, 0:k, :], dram["beyond"][s0:s0 + k, :, bass.ds(i * P, P)]
                                             .rearrange("b p d -> p b d")).then_inc(S["beyond_in"], 16)
                    if last_layer:
                        for g, (s0, k) in enumerate(GROUPS):
                            sp.wait_ge(S["low"], g + 1)
                            sp.dma_start(dram["table"][s0 * P:(s0 + k) * P, :].rearrange("(b p) f -> p b f", p=P),
                                         X[:, s0:s0 + k, :]).then_inc(S["stored"], 16)
                        sp.wait_ge(S["stored"], 16 * NG)

            @block.tensor
            def _(pe):
                for L in range(4):
                    S, before, parts, nxt, digits, last_layer = layer(L)
                    if L == 0:
                        pe.wait_ge(eyed, 2)
                        pe.wait_ge(S["w_in"], 32)
                        for i in range(2):
                            for o in range(2):
                                last = nc.tensor.transpose(py[:, i, o, 0:128], wt[:, o, i * 128:(i + 1) * 128], eye[:])
                        last.then_inc(turned, 1)
                        pe.wait_ge(S["y_out"], 1)
                    base = 1 if L == 0 else 0

                    def sums(g):
                        s0, k = GROUPS[g]
                        if g >= 2:
                            pe.wait_ge(S["y_out"], base + 2 * (g - 1))

                        def step(i, first, last):
                            if L and g == 0 and i % MOV == 0:
                                pe.wait_ge(before["low"], i // MOV + 1)
                            if L == 1 and s0 <= i < s0 + k:
                                pe.wait_ge(loops, i + 1)
                            for h in range(2):
                                for n, part in enumerate(parts):
                                    m = nc.tensor.matmul(
                                        py[:, g % 2, h, 0:k * P],
                                        part[:, i, h * 128:(h + 1) * 128],
                                        C[:, s0:s0 + k, i, 0:P],
                                        start=first and n == 0, stop=last and n == len(parts) - 1)
                                if last:
                                    m.then_inc(S["summed"], 1)

                        def beyond_step(i):
                            pe.wait_ge(S["digits_done"], i + (g * NB + 2))
                            for h in range(2):
                                for n, part in enumerate(parts):
                                    for d in range(2):
                                        m = nc.tensor.matmul(
                                            py[:, g % 2, h, 0:k * P],
                                            part[:, bass.ds(i, 1), h * 128:(h + 1) * 128].rearrange("p a f -> p (a f)"),
                                            digits[:, d, 0:k, :].rearrange("p k d -> p (k d)"),
                                            start=False, stop=False)
                            m.then_inc(S["digits_used"], 1)

                        step(0, True, False)
                        for i in range(1, NB - 1):
                            step(i, False, False)
                        with if_dense(pe):
                            if L and g == 0:
                                pe.wait_ge(before["low"], NG)
                            with pe.Fori(0, NB) as i:
                                beyond_step(i)
                        step(NB - 1, False, True)

                    def project(g):
                        s0, k = GROUPS[g]
                        pe.wait_ge(S["y_out"], base + 2 * (g + 1))
                        if L and g == 0:
                            pe.wait_ge(S["w_in"], 16)
                            pe.wait_ge(before["o_out"], NG)
                        if g >= 2:
                            pe.wait_ge(S["o_out"], g - 1)
                        for j in range(k):
                            for h in range(2):
                                m = nc.tensor.matmul(po[:, g % 2, j, :], yt[:, g % 2, h, j * P:(j + 1) * P], W[:, h, :],
                                                     start=h == 0, stop=h == 1)
                        m.then_inc(S["projected"], 1)

                    sums(0)
                    for g in range(1, NG):
                        sums(g)
                        project(g - 1)
                    project(NG - 1)

            @block.gpsimd
            def _(g_):
                for L in range(4):
                    S, before, parts, nxt, digits, last_layer = layer(L)
                    if L == 0:
                        g_.memset(eps[:], 1e-5).then_inc(epsd, 1)
                        g_.memset(eye[:], 0.0).then_inc(eyed, 1)
                        g_.wait_ge(eyed, 1)
                        g_.affine_select(out=eye[:], in_=eye[:], compare_op=ALU.not_equal, fill=1.0, base=0,
                                         pattern=[[-1, 128]], channel_multiplier=1).then_inc(eyed, 1)

                    def digits_of(g):
                        s0, k = GROUPS[g]
                        with if_dense(g_):
                            if g == 0:
                                if L:
                                    g_.wait_ge(before["digits_used"], NG * NB + 1)
                                g_.sem_inc(S["digits_done"], 1)
                                g_.sem_inc(S["digits_used"], 1)
                            with g_.Fori(0, NB) as i:
                                n = i + g * NB
                                g_.wait_ge(S["beyond_in"], n * 16 + 16)
                                g_.sem_inc(S["digits_seen"], 1)
                                g_.tensor_scalar(whole[:, 0:k, :], beyond[:, 0:k, :], 1.0 / 256, ROUND, ALU.mult,
                                                 ALU.add).then_inc(S["digit_steps"], 1)
                                g_.wait_ge(S["digit_steps"], n * 2 + 1)
                                g_.sem_inc(S["digits_seen"], 1)
                                g_.wait_ge(S["digits_used"], n + 1)
                                g_.sem_inc(S["digits_seen"], 1)
                                g_.tensor_scalar(digits[:, 0, 0:k, :], whole[:, 0:k, :], -ROUND, 256.0, ALU.add,
                                                 ALU.mult).then_inc(S["digit_steps"], 1)
                                g_.wait_ge(S["digit_steps"], n * 2 + 2)
                                g_.tensor_tensor(digits[:, 1, 0:k, :], beyond[:, 0:k, :], digits[:, 0, 0:k, :],
                                                 ALU.subtract).then_inc(S["digits_done"], 1)
                                g_.wait_ge(S["digits_done"], n + 2)

                    digits_of(0)
                    for g, (s0, k) in enumerate(GROUPS):
                        if g + 1 < NG:
                            digits_of(g + 1)
                        if L == 0:
                            continue
                        g_.wait_ge(S["centred"], g + 1)
                        for n, name, op in ((0, "gamma", ALU.mult), (1, "beta", ALU.add)):
                            if n:
                                g_.wait_ge(S["pch"], g + 1)
                            m = g_.tensor_tensor(tmp[:, 0:k, :], tmp[:, 0:k, :],
                                                 rows[name][:, L - 1:L, :].broadcast_to((P, k, D)), op)
                            m.then_inc(S["affine"] if n else S["pch"], 1)

            @block.scalar
            def _(a):
                for L in range(4):
                    S, before, parts, nxt, digits, last_layer = layer(L)
                    if L == 0:
                        a.wait_ge(turned, 1)
                        a.copy(W[:].rearrange("p i (o q) -> p i o q", o=2), py[:, :, :, 0:128]).then_inc(S["y_out"], 1)
                        a.wait_ge(scale_steps, 1)
                        a.activation(root[:], deg1[:], ACT.Sqrt).then_inc(rooted_deg, 1)
                    a.wait_ge(epsd, 1)
                    if L:
                        a.wait_ge(before["projected"], NG)

                    def take(g):
                        s0, k = GROUPS[g]
                        for h in range(2):
                            a.wait_ge(S["summed"], 2 * g + h + 1)
                            if g >= 2 and h == 0:
                                a.wait_ge(S["projected"], g - 1)
                            scale = {0: 1.0, 1: 1.0 / 128}.get(L)
                            if scale is None:
                                scale = tab["unscale"][:, L - 2, h:h + 1]
                            a.activation(yt[:, g % 2, h, 0:k * P], py[:, g % 2, h, 0:k * P], ACT.Copy,
                                         scale=scale).then_inc(S["y_out"], 1)

                    def normalize(n, g, k, out, src):
                        a.wait_ge(S["stats"] if n == 0 else S["last_stats"], 2 * g + 1)
                        a.activation(rs[:, 0:k], mv[:, 0:k, 1], ACT.Sqrt, bias=eps[:]).then_inc(S["rooted"], 1)
                        a.wait_ge(S["stats"] if n == 0 else S["last_stats"], 2 * g + 2)
                        for j in range(k):
                            m = a.activation(out[:, j, :], src[:, j, :], ACT.Identity, bias=nm[:, j:j + 1],
                                             scale=rs[:, j:j + 1])
                        return m

                    def finish(g):
                        s0, k = GROUPS[g]
                        if L == 0:
                            normalize(0, g, k, X[:, s0:s0 + k, :], a_).then_inc(S["centred"], 1)
                            a.wait_ge(S["centred"], g + 1)
                        else:
                            normalize(0, g, k, tmp, a_).then_inc(S["centred"], 1)
                            if not last_layer:
                                a.wait_ge(S["affine"], g + 1)
                        if last_layer:
                            normalize(1, g, k, X[:, s0:s0 + k, :], a_).then_inc(S["low"], 1)
                            return
                        if g:
                            a.wait_ge(S["low"], g)
                        for j in range(k):
                            if L == 0:
                                m = a.activation(a_[:, j, :], X[:, s0 + j, :], ACT.Copy, scale=tab["dinv_x"][:, s0 + j:s0 + j + 1])
                            else:
                                m = a.activation(a_[:, j, :], tmp[:, j, :], ACT.Relu, scale=tab["dinv"][:, s0 + j:s0 + j + 1])
                        m.then_inc(S["relued"], 1)
                        a.wait_ge(S["relued"], g + 1)
                        a.copy(nxt[0][:, s0:s0 + k, :], a_[:, 0:k, :]).then_inc(S["high"], 1)

                    take(0)
                    for g in range(NG):
                        if g + 1 < NG:
                            take(g + 1)
                        finish(g)

            @block.vector
            def _(v):
                for L in range(4):
                    S, before, parts, nxt, digits, last_layer = layer(L)
                    n = [0]

                    def link(ins):
                        n[0] += 1
                        ins.then_inc(S["vch"], 1)
                        v.wait_ge(S["vch"], n[0])

                    def moments(g, k, sem_, src):
                        for j in range(k):
                            m = v.bn_stats(st[:, j, :], src[:, j, :])
                        link(m)
                        for j in range(k):
                            m = v.bn_aggr(mv[:, j, :], st[:, j, :])
                        m.then_inc(sem_, 1)
                        return m

                    if L == 0:
                        scales(v)
                        v.wait_ge(S["w_in"], 32)
                    count = [0]
                    for g, (s0, k) in enumerate(GROUPS):
                        if L in (0, 3) and g == NG - 1:
                            v.wait_ge(S["summed"], 2 * NG)
                            v.wait_ge(eyed, 2)
                            for b in range(NB):
                                v.tensor_tensor(C[:, b, b, 0:P], C[:, b, b, 0:P], eye[0:P, 0:P],
                                                ALU.subtract if L else ALU.add, saturate=False).then_inc(loops, 1)
                        v.wait_ge(S["projected"], g + 1)
                        if g:
                            v.wait_ge(S["low"], g)
                        elif L:
                            v.wait_ge(before["low"], NG)
                        for j in range(k):
                            t = s0 + j
                            if L == 0:
                                m = v.scalar_tensor_tensor(a_[:, j, :], po[:, g % 2, j, :], tab["mean"][:, t:t + 1],
                                                           X[:, t, :], ALU.mult, ALU.add)
                            else:
                                m = v.scalar_tensor_tensor(a_[:, j, :], po[:, g % 2, j, :], tab["dinv"][:, t:t + 1],
                                                           rows["b"][:, L - 1, :], ALU.mult, ALU.add)
                        m.then_inc(S["o_out"], 1)
                        v.wait_ge(S["o_out"], g + 1)
                        if L == 0:
                            for j in range(k):
                                t = s0 + j
                                m = v.scalar_tensor_tensor(a_[:, j, :], b0, tab["degmean"][:, t:t + 1],
                                                           a_[:, j, :], ALU.mult, ALU.add)
                            link(m)
                        for pass_ in range(2 if last_layer else 1):
                            s_ = S["stats"] if pass_ == 0 else S["last_stats"]
                            if pass_:
                                v.wait_ge(S["affine"], g + 1)
                                link(v.scalar_tensor_tensor(a_[:, 0:k, :], tmp[:, 0:k, :], 0.0, X[:, s0:s0 + k, :],
                                                            ALU.max, ALU.add))
                            moments(g, k, s_, a_)
                            count[0] += 1
                            v.wait_ge(S["rooted"], count[0])
                            link(v.reciprocal(rs[:, 0:k], rs[:, 0:k]))
                            v.scalar_tensor_tensor(nm[:, 0:k], mv[:, 0:k, 0], -1.0, rs[:, 0:k], ALU.mult, ALU.mult).then_inc(s_, 1)
                        if not last_layer:
                            v.wait_ge(S["high"], g + 1)
                            v.tensor_tensor(nxt[1][:, s0:s0 + k, :], a_[:, 0:k, :], nxt[0][:, s0:s0 + k, :],
                                            ALU.subtract).then_inc(S["low"], 1)


def need(eng, sem, value):
    if not isinstance(value, int) or value > 0:
        eng.wait_ge(sem, value)


def skewed(eng, n, stages):
    leads = [lead for lead, _ in stages]
    begin, end = 2 - min(leads), n - max(leads)
    end -= (end - begin) % 2

    def plain(s):
        for lead, fn in stages:
            if 0 <= s + lead < n:
                fn(s + lead, (s + lead) % 2, (s + lead) // 2)
    for s in range(-max(leads), begin):
        plain(s)
    with eng.Fori(0, (end - begin) // 2) as i:
        for k in range(2):
            for lead, fn in stages:
                g = begin + k + lead
                fn(i * 2 + g, g % 2, i + g // 2)
    for s in range(end, n - min(leads)):
        plain(s)


EG = 4
NEG = NT // EG


def gated_messages(nc, ctx, dram, tab):
    with ExitStack() as c:
        sb = lambda n, s, d: c.enter_context(nc.sbuf_tensor("gm_" + n, s, d))
        pb = lambda n, s: c.enter_context(nc.psum_tensor("gm_" + n, s, F32))
        sem = lambda n: ctx.semaphore("gm_" + n)
        W1 = sb("W1", [2 * AT, D], F32)
        W2 = sb("W2", [128, 2, D], F32)
        b1 = sb("b1", [128, 2], F32)
        b2f = sb("b2f", [3, D], F32)
        b2r = sb("b2r", [3, D], F32)
        b2h = sb("b2h", [3, D], BF16)
        b2p = sb("b2p", [3, D], BF16)
        eye3 = sb("eye3", [3, 3], F32)
        ones = sb("ones", [3, ET], BF16)
        eye = sb("eye", [ET, ET], F32)
        iota = sb("iota", [ET, P], F32)
        edge = sb("edge", [ET, NT, 2], F32)
        slot = sb("slot", [ET, 2, EG], U32)
        attr = sb("attr", [ET, 2, EG, AT], F32)
        attr_t = sb("attr_t", [2 * AT, 2, EG // 2 * ET], F32)
        sg = sb("sg", [128, 2, 2, EG // 2 * ET], F32)
        hid = sb("hid", [128, 2, 2, 2, EG // 2 * ET], F32)
        gate = sb("gate", [ET, 2, EG, D], F32)
        hs = sb("hs", [ET, 2, EG, D], F32)
        msg = gate
        high = sb("high", [ET, 2, EG, D], F16)
        low = sb("low", [ET, 2, EG, D], F16)
        oh = sb("oh", [ET, 2, EG, P], F16)
        aggr = tab["aggr"]
        pt = pb("pt", [2 * AT, 2, BANK])
        ph = pb("ph", [128, 2, 2, EG // 2 * ET])
        pg = pb("pg", [ET, EG, D])
        pa = pb("pa", [P, EG, D])
        loaded, const, chain = map(sem, ("loaded", "const", "chain"))
        attr_in = [sem("attr_in0"), sem("attr_in1")]
        gathered = [sem("gathered0"), sem("gathered1")]
        turned, attr_t_done, first_done, sig1, hid_done, second_done, gated, onehot, msg_done, summed, added, slots = map(
            sem, ("turned", "attr_t", "first", "sig1", "hid", "second", "gated", "onehot", "msg", "summed", "added", "slots"))
        slots_seen, highd, lowd = map(sem, ("slots_seen", "high", "low"))
        NLOAD = 6
        NCONST = 7
        with nc.Block() as block:
            @block.sync
            def _(sp):
                for i in range(2):
                    sp.dma_start(W1[i * AT:(i + 1) * AT, :], dram["L2_gnn_W1"]).then_inc(loaded, 16)
                sp.dma_start(W2[:], dram["L2_gnn_W2"].rearrange("(h p) o -> p h o", p=128)).then_inc(loaded, 16)
                sp.dma_start(b2f[:], dram["L2_gnn_b2"].partition_broadcast(3)).then_inc(loaded, 16)
                with nc.allow_non_contiguous_dma(reason="256 numbers, once"):
                    sp.dma_start(b1[:, 0:1], dram["L2_gnn_b1"][0:128].rearrange("(p a) -> p a", a=1)).then_inc(loaded, 16)
                    sp.dma_start(b1[:, 1:2], dram["L2_gnn_b1"][128:256].rearrange("(p a) -> p a", a=1)).then_inc(loaded, 16)

                def load(g, q, h):
                    starts = [sp.value_load(tab["e0"][0:1, bass.ds(g * EG + j, 1)], min_val=0, max_val=E)
                              for j in range(EG)]
                    need(sp, turned, g - 1)
                    for j, e0 in enumerate(starts):
                        sp.dma_start(attr[:, q, j, :], dram["attr_s"][bass.ds(e0, ET), :]).then_inc(attr_in[q], 16)
                        sp.dma_start(edge[:, bass.ds(g * EG + j, 1), :].rearrange("p a k -> p (a k)"),
                                     dram["pairs"][bass.ds(e0, ET), 0:2]).then_inc(attr_in[q], 16)
                skewed(sp, NEG, [(0, load)])

            @block.gpsimd
            def _(p):
                p.memset(ones[:], 1.0).then_inc(const, 1)
                p.memset(eye[:], 0.0).then_inc(const, 1)
                p.memset(aggr[:], 0.0).then_inc(const, 1)
                p.memset(eye3[:], 0.0).then_inc(const, 1)
                p.wait_ge(const, 4)
                p.affine_select(out=eye3[:], in_=eye3[:], compare_op=ALU.not_equal, fill=1.0, base=0,
                                pattern=[[-1, 3]], channel_multiplier=1).then_inc(const, 1)
                p.affine_select(out=eye[:], in_=eye[:], compare_op=ALU.not_equal, fill=1.0, base=0,
                                pattern=[[-1, ET]], channel_multiplier=1).then_inc(const, 1)
                p.iota(iota[:], pattern=[[1, P]], base=0, channel_multiplier=0,
                       allow_small_or_imprecise_dtypes=True).then_inc(const, 1)
                p.wait_ge(const, NCONST)

                def gather(g, q, h):
                    need(p, msg_done, g - 1)
                    p.wait_ge(attr_in[q], (h + 1) * (32 * EG))
                    p.tensor_copy(slot[:, q, :], edge[:, bass.ts(g, EG), 0]).then_inc(slots, 1)
                    p.wait_ge(slots, g + 1)
                    p.sem_inc(slots_seen, 1)
                    for j in range(EG):
                        p.indirect_dma_start(out=hs[:, q, j, :], out_offset=None, in_=dram["table"],
                                             in_offset=bass.IndirectOffsetOnAxis(ap=slot[:, q, j:j + 1], axis=0)
                                             ).then_inc(gathered[q], 16)

                def lower(g, q, h):
                    p.wait_ge(highd, g + 1)
                    need(p, summed, g - 1)
                    p.tensor_tensor(low[:, q, :, :], msg[:, q, :, :], high[:, q, :, :], ALU.subtract).then_inc(lowd, 1)
                skewed(p, NEG, [(1, gather), (-1, lower)])

            @block.tensor
            def _(pe):
                pe.wait_ge(loaded, 16 * NLOAD)
                pe.wait_ge(const, NCONST)
                pe.wait_ge(chain, 10)

                def turn(g, q, h):
                    pe.wait_ge(attr_in[q], (h + 1) * (32 * EG))
                    need(pe, attr_t_done, g - 1)
                    for j in range(EG // 2):
                        m = nc.tensor.transpose(pt[:, q, j * ET:(j + 1) * ET],
                                                attr[:, q, 2 * j:2 * j + 2, :].rearrange("p a f -> p (a f)"), eye[:])
                    m.then_inc(turned, 1)

                def first(g, q, h):
                    pe.wait_ge(attr_t_done, g + 1)
                    need(pe, hid_done, g)
                    for i in range(2):
                        for r in range(2):
                            half = slice(r * AT, (r + 1) * AT)
                            m = nc.tensor.matmul(ph[:, r, i, :], W1[half, i * 128:(i + 1) * 128], attr_t[half, q, :],
                                                 start=True, stop=True)
                        m.then_inc(first_done, 1)

                def second(g, q, h):
                    pe.wait_ge(hid_done, g + 1)
                    need(pe, gated, g)
                    for j in range(EG):
                        for i in range(2):
                            nc.tensor.matmul(pg[:, j, :], hid[:, q, j % 2, i, j // 2 * ET:(j // 2 + 1) * ET], W2[:, i, :],
                                             start=i == 0, stop=False)
                        m = nc.tensor.matmul(pg[:, j, :], ones[:], b2p[:], start=False, stop=True)
                    m.then_inc(second_done, 1)

                def add_up(g, q, h):
                    pe.wait_ge(lowd, g + 1)
                    pe.wait_ge(onehot, g + 1)
                    need(pe, added, g * EG)
                    for j in range(EG):
                        nc.tensor.matmul(pa[:, j, :], oh[:, q, j, :], high[:, q, j, :], start=True, stop=False)
                        m = nc.tensor.matmul(pa[:, j, :], oh[:, q, j, :], low[:, q, j, :], start=False, stop=True)
                    m.then_inc(summed, 1)
                skewed(pe, NEG, [(2, turn), (1, first), (0, second), (-2, add_up)])

            @block.scalar
            def _(a):
                a.wait_ge(loaded, 16 * NLOAD)

                def take(g, q, h):
                    a.wait_ge(turned, g + 1)
                    need(a, first_done, (g - 1) * 2)
                    a.copy(attr_t[:, q, :], pt[:, q, 0:EG // 2 * ET]).then_inc(attr_t_done, 1)

                def sigmoid1(g, q, h):
                    need(a, hid_done, g)
                    for i in range(2):
                        a.wait_ge(first_done, g * 2 + 2)
                        a.activation(sg[:, :, i, :], ph[:, :, i, :], ACT.Sigmoid, bias=b1[:, i:i + 1]).then_inc(sig1, 1)

                def sigmoid2(g, q, h):
                    a.wait_ge(second_done, g + 1)
                    need(a, lowd, g - 1)
                    a.activation(gate[:, q, :, :], pg[:], ACT.Sigmoid).then_inc(gated, 1)

                def upper(g, q, h):
                    a.wait_ge(msg_done, g + 1)
                    need(a, summed, g - 1)
                    a.copy(high[:, q, :, :], msg[:, q, :, :]).then_inc(highd, 1)
                skewed(a, NEG, [(-1, upper), (2, take), (1, sigmoid1), (0, sigmoid2)])

            @block.vector
            def _(v):
                v.wait_ge(const, NCONST)
                v.wait_ge(loaded, 16 * NLOAD)
                n = [0]

                def link(ins):
                    n[0] += 1
                    ins.then_inc(chain, 1)
                    v.wait_ge(chain, n[0])
                link(v.tensor_copy(b2h[:], b2f[:]))
                link(v.tensor_scalar(b2p[:], b2h[:], eye3[:, 0:1], None, ALU.mult))
                for part in (1, 2):
                    link(v.tensor_tensor(b2f[:], b2f[:], b2h[:], ALU.subtract))
                    link(v.tensor_copy(b2h[:], b2f[:]))
                    link(v.tensor_scalar(b2r[:], b2h[:], eye3[:, part:part + 1], None, ALU.mult))
                    link(v.tensor_tensor(b2p[:], b2p[:], b2r[:], ALU.add))

                def hidden(g, q, h):
                    v.wait_ge(sig1, g * 2 + 2)
                    need(v, second_done, g - 1)
                    for i in range(2):
                        m = v.scalar_tensor_tensor(hid[:, q, :, i, :], ph[:, :, i, :], b1[:, i:i + 1], sg[:, :, i, :],
                                                   ALU.add, ALU.mult)
                    m.then_inc(hid_done, 1)

                def onehots(g, q, h):
                    need(v, summed, g - 1)
                    v.wait_ge(attr_in[q], (h + 1) * (32 * EG))
                    for j in range(EG):
                        t = g * EG + j
                        m = v.tensor_scalar(oh[:, q, j, :], iota[:], tab["first"][:, bass.ds(t, 1)],
                                            edge[:, bass.ds(t, 1), 1], ALU.add, ALU.is_equal)
                    m.then_inc(onehot, 1)

                def message(g, q, h):
                    v.wait_ge(gated, g + 1)
                    v.wait_ge(gathered[q], (h + 1) * (16 * EG))
                    v.scalar_tensor_tensor(msg[:, q, :, :], gate[:, q, :, :], 128.0, hs[:, q, :, :], ALU.mult,
                                           ALU.mult).then_inc(msg_done, 1)

                def add(g, q, h):
                    v.wait_ge(summed, g + 1)
                    for j in range(EG):
                        b = v.value_load(tab["bucket"][0:1, bass.ds(g * EG + j, 1)], min_val=0, max_val=NB)
                        need(v, added, g * EG + j)
                        s = aggr[:, bass.ds(b, 1), :].rearrange("p a f -> p (a f)")
                        v.scalar_tensor_tensor(s, pa[:, j, :], 1.0 / 128, s, ALU.mult, ALU.add).then_inc(added, 1)
                skewed(v, NEG, [(1, hidden), (0, message), (-1, onehots), (-2, add)])
                v.wait_ge(added, NT)


def layer_norm(v, a, link, stats_sem, root_sem, counts, z, out, st, mv, rs, nm, k, side):
    n = counts[side]
    counts[side] += 1
    if side == "v":
        for j in range(k):
            m = v.bn_stats(st[:, j, :], z[:, j, :])
        link(m)
        for j in range(k):
            m = v.bn_aggr(mv[:, j, :], st[:, j, :])
        m.then_inc(stats_sem, 1)
        v.wait_ge(root_sem, n + 1)
        link(v.reciprocal(rs[:, 0:k], rs[:, 0:k]))
        v.scalar_tensor_tensor(nm[:, 0:k], mv[:, 0:k, 0], -1.0, rs[:, 0:k], ALU.mult, ALU.mult).then_inc(stats_sem, 1)
        return None
    eps = counts["eps"]
    a.wait_ge(stats_sem, 2 * n + 1)
    a.activation(rs[:, 0:k], mv[:, 0:k, 1], ACT.Sqrt, bias=eps).then_inc(root_sem, 1)
    a.wait_ge(stats_sem, 2 * n + 2)
    for j in range(k):
        m = a.activation(out[:, j, :], z[:, j, :], ACT.Identity, bias=nm[:, j:j + 1], scale=rs[:, j:j + 1])
    return m


def update_nodes(nc, ctx, dram, tab):
    with ExitStack() as c:
        sb = lambda n, s, d=F32: c.enter_context(nc.sbuf_tensor("un_" + n, s, d))
        pb = lambda n, s: c.enter_context(nc.psum_tensor("un_" + n, s, F32))
        sem = lambda n: ctx.semaphore("un_" + n)
        X, aggr = tab["X"], tab["aggr"]
        U1 = sb("U1", [128, 4, D])
        U2 = sb("U2", [128, 2, D])
        c1 = sb("c1", [128, 2])
        c2 = sb("c2", [P, D])
        W3 = sb("W3", [128, 2, 128])
        al = sb("al", [P, 2, 128])
        eye = sb("eye", [P, P])
        cat = sb("cat", [128, 4, MOV * P])
        sg = sb("sg", [128, 2, MOV * P])
        hid = sb("hid", [128, 2, MOV * P])
        z = sb("z", [P, MOV, D])
        st, mv, rs, nm = sb("st", [P, MOV, 6]), sb("mv", [P, MOV, 2]), sb("rs", [P, MOV]), sb("nm", [P, MOV])
        eps = sb("eps", [P, 1])
        xt = sb("xt", [128, 2, MOV * P])
        prod = sb("prod", [P, 2, MOV, 128])
        pt = pb("pt", [128, 4, BANK])
        ph = pb("ph", [128, 2, BANK])
        po = pb("po", [P, MOV, D])
        names = ("loaded", "const", "turned", "cat", "first", "sig", "hid", "second", "chain", "stats",
                 "root", "normed", "xturned", "xt", "heads", "heads_out")
        loaded, const, turned, catd, first, sig, hidd, second, ch, stats, root, normed, xturned, xtd, heads, \
            heads_out = map(sem, names)
        with nc.Block() as block:
            @block.sync
            def _(sp):
                sp.dma_start(U1[:], dram["L2_gnn_U1"].rearrange("(h p) o -> p h o", p=128)).then_inc(loaded, 16)
                sp.dma_start(U2[:], dram["L2_gnn_U2"].rearrange("(h p) o -> p h o", p=128)).then_inc(loaded, 16)
                sp.dma_start(W3[:], dram["L3_gnn_W"].rearrange("(h p) o -> p h o", p=128)).then_inc(loaded, 16)
                sp.dma_start(c2[:], dram["L2_gnn_c2"].partition_broadcast(P)).then_inc(loaded, 16)
                for i, n in enumerate(("l", "r")):
                    sp.dma_start(al[:, i, :], dram["L3_gnn_attn_" + n].rearrange("h d -> (h d)")
                                 .partition_broadcast(P)).then_inc(loaded, 16)
                with nc.allow_non_contiguous_dma(reason="256 numbers, once"):
                    for i in range(2):
                        sp.dma_start(c1[:, i:i + 1], dram["L2_gnn_c1"][128 * i:128 * (i + 1)]
                                     .rearrange("(p a) -> p a", a=1)).then_inc(loaded, 16)

            @block.gpsimd
            def _(p):
                p.memset(eps[:], 1e-5).then_inc(const, 1)
                p.memset(eye[:], 0.0).then_inc(const, 1)
                p.memset(tab["heads"][:], 1.0).then_inc(const, 1)
                p.wait_ge(const, 3)
                p.affine_select(out=eye[:], in_=eye[:], compare_op=ALU.not_equal, fill=1.0, base=0,
                                pattern=[[-1, P]], channel_multiplier=1).then_inc(const, 1)

            @block.tensor
            def _(pe):
                pe.wait_ge(loaded, 16 * 8)
                pe.wait_ge(const, 4)

                def turn(g):
                    s0, k = GROUPS[g]
                    need(pe, xtd, g - 1)
                    for i in range(4):
                        for j in range(k):
                            src = (X if i < 2 else aggr)[:, s0 + j, (i % 2) * 128:(i % 2 + 1) * 128]
                            m = nc.tensor.transpose(pt[:, i, j * P:(j + 1) * P], src, eye[:])
                    m.then_inc(turned, 1)

                def first_product(g):
                    s0, k = GROUPS[g]
                    pe.wait_ge(catd, g + 1)
                    need(pe, hidd, g)
                    for o in range(2):
                        for i in range(4):
                            m = nc.tensor.matmul(ph[:, o, 0:k * P], U1[:, i, o * 128:(o + 1) * 128], cat[:, i, 0:k * P],
                                                 start=i == 0, stop=i == 3)
                        m.then_inc(first, 1)

                def second_product(g):
                    s0, k = GROUPS[g]
                    pe.wait_ge(hidd, g + 1)
                    need(pe, heads_out, g)
                    for j in range(k):
                        for i in range(2):
                            m = nc.tensor.matmul(po[:, j, :], hid[:, i, j * P:(j + 1) * P], U2[:, i, :],
                                                 start=i == 0, stop=i == 1)
                    m.then_inc(second, 1)

                def heads_of(g):
                    s0, k = GROUPS[g]
                    pe.wait_ge(normed, g + 1)
                    pe.wait_ge(catd, min(g + 2, NG))
                    for i in range(2):
                        for j in range(k):
                            m = nc.tensor.transpose(pt[:, i, j * P:(j + 1) * P], X[:, s0 + j, i * 128:(i + 1) * 128], eye[:])
                    m.then_inc(xturned, 1)
                    pe.wait_ge(xtd, g + 1)
                    for j in range(k):
                        for i in range(2):
                            m = nc.tensor.matmul(po[:, j, 0:128], xt[:, i, j * P:(j + 1) * P], W3[:, i, :],
                                                 start=i == 0, stop=i == 1)
                    m.then_inc(heads, 1)
                for g in range(NG + 1):
                    if g < NG:
                        turn(g)
                    if g:
                        second_product(g - 1)
                    if g < NG:
                        first_product(g)
                    if g:
                        heads_of(g - 1)

            counts = {"v": 0, "a": 0, "eps": eps[:]}

            @block.scalar
            def _(a):
                a.wait_ge(loaded, 16 * 8)
                a.wait_ge(const, 4)
                for g in range(NG + 1):
                    if g < NG:
                        k = GROUPS[g][1]
                        a.wait_ge(turned, g + 1)
                        a.copy(cat[:, :, 0:k * P], pt[:, :, 0:k * P]).then_inc(catd, 1)
                    if g:
                        s0, k = GROUPS[g - 1]
                        layer_norm(None, a, None, stats, root, counts, z, X[:, s0:s0 + k, :], st, mv, rs, nm, k,
                                   "a").then_inc(normed, 1)
                    if g < NG:
                        k = GROUPS[g][1]
                        for o in range(2):
                            a.wait_ge(first, 2 * g + o + 1)
                            a.activation(sg[:, o, 0:k * P], ph[:, o, 0:k * P], ACT.Sigmoid, bias=c1[:, o:o + 1]).then_inc(sig, 1)
                    if g:
                        k = GROUPS[g - 1][1]
                        a.wait_ge(xturned, g)
                        a.copy(xt[:, :, 0:k * P], pt[:, 0:2, 0:k * P]).then_inc(xtd, 1)

            @block.vector
            def _(v):
                v.wait_ge(loaded, 16 * 8)
                v.wait_ge(const, 4)
                n = [0]

                def link(ins):
                    n[0] += 1
                    ins.then_inc(ch, 1)
                    v.wait_ge(ch, n[0])

                def normalize(g):
                    s0, k = GROUPS[g]
                    v.wait_ge(second, g + 1)
                    link(v.tensor_tensor(z[:, 0:k, :], po[:, 0:k, :],
                                         c2[:].rearrange("p (a f) -> p a f", a=1).broadcast_to((P, k, D)), ALU.add))
                    link(v.scalar_tensor_tensor(z[:, 0:k, :], X[:, s0:s0 + k, :], 2.0, z[:, 0:k, :], ALU.mult, ALU.add))
                    layer_norm(v, None, link, stats, root, counts, z, None, st, mv, rs, nm, k, "v")

                def hidden(g):
                    k = GROUPS[g][1]
                    v.wait_ge(sig, 2 * g + 2)
                    for o in range(2):
                        m = v.scalar_tensor_tensor(hid[:, o, 0:k * P], ph[:, o, 0:k * P], c1[:, o:o + 1],
                                                   sg[:, o, 0:k * P], ALU.add, ALU.mult)
                    m.then_inc(hidd, 1)

                def logits_of(g):
                    s0, k = GROUPS[g]
                    v.wait_ge(heads, g + 1)
                    v.tensor_copy(tab["heads"][:, s0:s0 + k, :, 0:64],
                                  po[:, 0:k, 0:128].rearrange("p k (h d) -> p k h d", h=2))
                    for i in range(2):
                        m = v.tensor_tensor(prod[:, i, 0:k, :], po[:, 0:k, 0:128],
                                            al[:, i:i + 1, :].broadcast_to((P, k, 128)), ALU.mult)
                    m.then_inc(heads_out, 1)
                    v.wait_ge(heads_out, g + 1)
                    for i in range(2):
                        link(v.tensor_reduce(tab["logit"][:, i, s0:s0 + k, :],
                                             prod[:, i, 0:k, :].rearrange("p k (h d) -> p k h d", h=2),
                                             op=ALU.add, axis=AX.X))
                for g in range(NG + 1):
                    if g:
                        normalize(g - 1)
                    if g < NG:
                        hidden(g)
                    if g:
                        logits_of(g - 1)


BIG = 1e30
LEAK = 0.2


EB = 4
AHEAD = 3
STEPS = 2 * NB


def attention(nc, ctx, dram, tab):
    with ExitStack() as c:
        sb = lambda n, s, d=F32: c.enter_context(nc.sbuf_tensor("at_" + n, s, d))
        sem = lambda n: ctx.semaphore("at_" + n)
        C, X, logit, H = tab["counts"], tab["X"], tab["logit"], tab["heads"]
        eye = sb("eye", [128, 128])
        eps = sb("eps", [P, 1])
        minus_half = sb("minus_half", [P, 1])
        el_low = sb("el_low", [P, NB, 2])
        el_rest = sb("el_rest", [P, NB, 2])
        bg = sb("bg", [P, 128])
        bl = sb("bl", [P, D])
        LW = sb("LW", [128, D])
        masks = sb("masks", [P, EB, MOV * P])
        best = sb("best", [P, 2, MOV * P])
        top = sb("top", [P, MOV, 2])
        m_ = sb("m", [P, MOV, 2])
        r = sb("r", [P, 2, 2, MOV, 2])
        rows = sb("rows", [P, 2, 2, MOV * P])
        rect = sb("rect", [P, EB, MOV * P])
        leaky = sb("leaky", [P, EB, MOV * P])
        e = sb("e", [P, EB, MOV * P])
        w = sb("w", [P, EB, MOV * P])
        num = sb("num", [65, 2, MOV * P])
        o = sb("o", [P, MOV, 128])
        rec = sb("rec", [P, MOV, 2, 1])
        ot = sb("ot", [128, MOV * P])
        z = sb("z", [P, MOV, D])
        y = sb("y", [P, MOV, D])
        beyond = sb("beyond", [P, MOV, P])
        x_rect, x_leaky, x_e, x_w = (sb(n, [P, MOV * P]) for n in ("x_rect", "x_leaky", "x_e", "x_w"))
        st, mv, rs, nm = sb("st", [P, MOV, 6]), sb("mv", [P, MOV, 2]), sb("rs", [P, MOV]), sb("nm", [P, MOV])
        pb = lambda n, s: c.enter_context(nc.psum_tensor("at_" + n, s, F32))
        prow = pb("prow", [P, 2, MOV, 128])
        pn = pb("pn", [65, 2, BANK])
        pot = pb("pot", [P, MOV, 128])
        pot2 = pb("pot2", [128, MOV, 128])
        pl = pb("pl", [P, MOV, D])
        loaded, const, chain = sem("loaded"), sem("const"), sem("chain")
        masked, bestd, best_turned, rd, rowed, row_out = map(sem, (
            "masked", "best", "best_turned", "r", "rowed", "row_out"))
        rectd_v = sem("rect_v")
        rectd, leaked, exps, weighed, used = map(sem, ("rect", "leaky", "exps", "weighed", "used"))
        numd, nturned, nturn_used, od, oturned, otd, lin, lin_used, stats, root, normed, stored = map(sem, (
            "num", "nturned", "nturn_used", "o", "oturned", "ot", "lin", "lin_used", "stats", "root", "normed", "stored"))
        beyond_in, x_rectd, x_leaked, x_exps, x_weighed, x_used = map(sem, (
            "beyond_in", "x_rect", "x_leaky", "x_exps", "x_weighed", "x_used"))
        NCONST = 4

        def by_vector(u):
            return u % 5 in (1, 3)

        def count_by(u, vector):
            return sum(by_vector(w) == vector for w in range(u))

        def mask_at(s):
            return [i for i in range(NB) if i * 5 // 3 == s]

        def if_dense(eng):
            return eng.If(eng.value_load(tab["dense"][0:1, 0:1], min_val=0, max_val=1) != 0)

        def group_steps():
            for g in range(NG + 1):
                for s in range(STEPS):
                    yield g, s, s // NB, s % NB

        with nc.Block() as block:
            @block.sync
            def _(sp):
                sp.dma_start(bg[:], dram["L3_gnn_gat_bias"].partition_broadcast(P)).then_inc(loaded, 16)
                sp.dma_start(bl[:], dram["L3_gnn_lin_b"].partition_broadcast(P)).then_inc(loaded, 16)
                sp.dma_start(LW[:], dram["L3_gnn_lin_W"]).then_inc(loaded, 16)
                with if_dense(sp):
                    sp.sem_inc(x_weighed, 1)
                    for n in range(2 * NG):
                        s0, k = GROUPS[n // 2]
                        with sp.Fori(0, NB) as i:
                            sp.wait_ge(x_weighed, i + (n * NB + 1))
                            sp.dma_start(beyond[:, 0:k, :], dram["beyond"][s0:s0 + k, :, bass.ds(i * P, P)]
                                         .rearrange("b p d -> p b d")).then_inc(beyond_in, 16)

            @block.gpsimd
            def _(p):
                p.memset(eps[:], 1e-5).then_inc(const, 1)
                p.memset(minus_half[:], -BIG / 2).then_inc(const, 1)
                p.memset(eye[:], 0.0).then_inc(const, 1)
                p.wait_ge(const, 3)
                p.affine_select(out=eye[:], in_=eye[:], compare_op=ALU.not_equal, fill=1.0, base=0,
                                pattern=[[-1, 128]], channel_multiplier=1).then_inc(const, 1)

                def sum_parts(n, i, k):
                    u = NB * n + i
                    q = u % EB
                    if i == 0:
                        p.wait_ge(row_out, n + 1)
                    if by_vector(u):
                        p.wait_ge(rectd_v, count_by(u + 1, True))
                    else:
                        p.wait_ge(rectd, count_by(u + 1, False))
                    need(p, exps, u - EB + 1)
                    p.tensor_tensor(leaky[:, q, 0:k * P], rect[:, q, 0:k * P], rows[:, n % 2, 1, 0:k * P],
                                    ALU.add).then_inc(leaked, 1)

                def beyond_cap(n, k):
                    with if_dense(p):
                        with p.Fori(0, NB) as i:
                            p.wait_ge(x_rectd, i + (NB * n + 1))
                            p.tensor_tensor(x_leaky[:, 0:k * P], x_rect[:, 0:k * P], rows[:, n % 2, 1, 0:k * P],
                                            ALU.add).then_inc(x_leaked, 1)
                for g, s, h, i in group_steps():
                    if g < NG:
                        sum_parts(2 * g + h, i, GROUPS[g][1])
                        if i == NB - 1:
                            beyond_cap(2 * g + h, GROUPS[g][1])
                    if g and s == 45:
                        s0, k = GROUPS[g - 1]
                        p.wait_ge(normed, g)
                        p.dma_start(dram["out"][s0 * P:(s0 + k) * P, :].rearrange("(b p) f -> p b f", p=P),
                                    y[:, 0:k, :]).then_inc(stored, 16)
                p.wait_ge(stored, 16 * NG)

            @block.tensor
            def _(pe):
                pe.wait_ge(loaded, 48)
                pe.wait_ge(const, NCONST)

                def turn_best(g):
                    s0, k = GROUPS[g]
                    pe.wait_ge(bestd, 2 * NB * (g + 1))
                    need(pe, row_out, 2 * g)
                    for h in range(2):
                        for j in range(k):
                            m = nc.tensor.transpose(prow[:, h, j, 0:P], best[:, h, j * P:(j + 1) * P], eye[0:P, 0:P])
                    m.then_inc(best_turned, 1)

                def row(n):
                    g, h = n // 2, n % 2
                    s0, k = GROUPS[g]
                    pe.wait_ge(rd, g + 1)
                    need(pe, row_out, n)
                    for i in range(2):
                        for j in range(k):
                            m = nc.tensor.transpose(prow[:, i, j, 0:P],
                                                    r[:, g % 2, i, j, h:h + 1].broadcast_to((P, P)), eye[0:P, 0:P])
                    m.then_inc(rowed, 1)

                def product(n, i, k, first, last):
                    u = NB * n + i
                    pe.wait_ge(weighed, u + 1)
                    nc.tensor.matmul(pn[:, n % 2, 0:k * P], H[:, i, n % 2, :], w[:, u % EB, 0:k * P],
                                     start=first, stop=last).then_inc(used, 1)

                def beyond_cap(n, k):
                    with if_dense(pe):
                        for i in range(NB):
                            pe.wait_ge(x_weighed, NB * n + i + 2)
                            nc.tensor.matmul(pn[:, n % 2, 0:k * P], H[:, i, n % 2, :], x_w[:, 0:k * P],
                                             start=False, stop=False).then_inc(x_used, 1)

                turn_best(0)
                row(0)
                for g, s, h, i in group_steps():
                    n = 2 * g + h
                    if g < NG:
                        k = GROUPS[g][1]
                        if i == 0:
                            need(pe, numd, n - 1)
                        if i == NB - 1:
                            beyond_cap(n, k)
                        product(n, i, k, i == 0, i == NB - 1)
                        if s == 14:
                            row(2 * g + 1)
                        if g + 1 < NG and s == 41:
                            turn_best(g + 1)
                        if g + 1 < NG and s == 44:
                            row(2 * g + 2)
                        if s == 33:
                            pe.wait_ge(numd, n)
                            need(pe, nturn_used, 2 * g)
                            for j in range(k):
                                m = nc.tensor.transpose(pot[:, j, 0:65], num[:, 0, j * P:(j + 1) * P], eye[0:65, 0:65])
                            m.then_inc(nturned, 1)
                    if g:
                        k = GROUPS[g - 1][1]
                        if s == 8:
                            pe.wait_ge(numd, 2 * g)
                            pe.wait_ge(nturn_used, 2 * g - 1)
                            for j in range(k):
                                m = nc.tensor.transpose(pot[:, j, 0:65], num[:, 1, j * P:(j + 1) * P], eye[0:65, 0:65])
                            m.then_inc(nturned, 1)
                        if s == 17:
                            pe.wait_ge(od, g)
                            for j in range(k):
                                m = nc.tensor.transpose(pot2[:, j, 0:P], o[:, j, :], eye[0:P, 0:P])
                            m.then_inc(oturned, 1)
                        if s == 24:
                            pe.wait_ge(otd, g)
                            need(pe, lin_used, g - 1)
                            for j in range(k):
                                m = nc.tensor.matmul(pl[:, j, :], ot[:, j * P:(j + 1) * P], LW[:], start=True, stop=True)
                            m.then_inc(lin, 1)

            @block.scalar
            def _(a):
                a.wait_ge(const, NCONST)

                def mask(g, i):
                    s0, k = GROUPS[g]
                    u = NB * g + i
                    need(a, bestd, 2 * (u - EB + 1))
                    a.activation(masks[:, u % EB, 0:k * P].rearrange("p (k d) -> p k d", d=P), C[:, s0:s0 + k, i, 0:P],
                                 ACT.Identity, bias=minus_half[:], scale=BIG).then_inc(masked, 1)

                def row(n):
                    k = GROUPS[n // 2][1]
                    a.wait_ge(rowed, n + 1)
                    need(a, leaked, NB * (n - 1))
                    a.copy(rows[:, n % 2, :, 0:k * P].rearrange("p i (k d) -> p i k d", d=P),
                           prow[:, :, 0:k, 0:P]).then_inc(row_out, 1)

                def rectify(u):
                    n, i = u // NB, u % NB
                    k, h, q = GROUPS[n // 2][1], n % 2, u % EB
                    if i == 0:
                        a.wait_ge(row_out, n + 1)
                    if by_vector(u):
                        return
                    need(a, leaked, u - EB + 1)
                    a.activation(rect[:, q, 0:k * P], rows[:, n % 2, 0, 0:k * P], ACT.Relu,
                                 bias=el_rest[:, i, h:h + 1]).then_inc(rectd, 1)

                def exp(u):
                    n, i = u // NB, u % NB
                    k, h, q = GROUPS[n // 2][1], n % 2, u % EB
                    a.wait_ge(leaked, u + 1)
                    need(a, weighed, u - EB + 1)
                    a.activation(e[:, q, 0:k * P], leaky[:, q, 0:k * P], ACT.Exp, bias=el_low[:, i, h:h + 1]).then_inc(exps, 1)

                def beyond_cap(n, k):
                    h = n % 2
                    with if_dense(a):
                        with a.Fori(0, NB) as i:
                            a.wait_ge(x_weighed, i + (NB * n + 1))
                            a.activation(x_rect[:, 0:k * P], rows[:, n % 2, 0, 0:k * P], ACT.Relu,
                                         bias=el_rest[:, bass.ds(i, 1), h]).then_inc(x_rectd, 1)
                            a.wait_ge(x_leaked, i + (NB * n + 1))
                            a.activation(x_e[:, 0:k * P], x_leaky[:, 0:k * P], ACT.Exp,
                                         bias=el_low[:, bass.ds(i, 1), h]).then_inc(x_exps, 1)

                for i in range(NB):
                    mask(0, i)
                row(0)
                a.wait_ge(chain, 2)
                for u in range(AHEAD):
                    rectify(u)
                for g, s, h, i in group_steps():
                    n = 2 * g + h
                    u = NB * n + i
                    if g < NG:
                        k = GROUPS[g][1]
                        if u + AHEAD < 2 * NB * NG:
                            rectify(u + AHEAD)
                        exp(u)
                        if i == NB - 1:
                            beyond_cap(n, k)
                        if g + 1 < NG:
                            for i_ in mask_at(s):
                                mask(g + 1, i_)
                        if s == 20:
                            row(2 * g + 1)
                        if g + 1 < NG and s == 46:
                            row(2 * g + 2)
                        if s == 32:
                            a.wait_ge(used, NB * n)
                            need(a, nturned, 2 * g - 1)
                            a.copy(num[:, 0, 0:k * P], pn[:, 0, 0:k * P]).then_inc(numd, 1)
                    if g:
                        k = GROUPS[g - 1][1]
                        if s == 7:
                            a.wait_ge(used, NB * 2 * g)
                            need(a, nturned, 2 * g - 2)
                            a.copy(num[:, 1, 0:k * P], pn[:, 1, 0:k * P]).then_inc(numd, 1)
                        if s == 23:
                            a.wait_ge(oturned, g)
                            need(a, lin, g - 1)
                            a.copy(ot[:, 0:k * P].rearrange("p (k d) -> p k d", d=P), pot2[:, 0:k, 0:P]).then_inc(otd, 1)
                        if s == 36:
                            a.wait_ge(stats, 2 * g - 1)
                            a.activation(rs[:, 0:k], mv[:, 0:k, 1], ACT.Sqrt, bias=eps[:]).then_inc(root, 1)
                        if s == 40:
                            a.wait_ge(stats, 2 * g)
                            need(a, stored, 16 * (g - 1))
                            for j in range(k):
                                m = a.activation(y[:, j, :], z[:, j, :], ACT.Identity, bias=nm[:, j:j + 1],
                                                 scale=rs[:, j:j + 1])
                            m.then_inc(normed, 1)

            @block.vector
            def _(v):
                v.wait_ge(loaded, 48)
                v.wait_ge(const, NCONST)
                n_ = [0]

                def link(ins):
                    n_[0] += 1
                    ins.then_inc(chain, 1)
                    v.wait_ge(chain, n_[0])
                link(v.tensor_scalar(el_low[:], logit[:, 0, :, :], LEAK, None, ALU.mult))
                link(v.tensor_scalar(el_rest[:], logit[:, 0, :, :], 1 - LEAK, None, ALU.mult))

                def take_best(g, i):
                    k = GROUPS[g][1]
                    u = NB * g + i
                    v.wait_ge(masked, u + 1)
                    if i == 0:
                        need(v, best_turned, g)
                    for h in range(2):
                        b = best[:, h, 0:k * P]
                        t = masks[:, u % EB, 0:k * P]
                        if i == 0:
                            ins = v.tensor_scalar(b, t, logit[:, 0, i, h:h + 1], None, ALU.min)
                        else:
                            v.wait_ge(bestd, 2 * (u - 1) + h + 1)
                            ins = v.scalar_tensor_tensor(b, t, logit[:, 0, i, h:h + 1], b, ALU.min, ALU.max)
                        ins.then_inc(bestd, 1)

                def take_top(g):
                    s0, k = GROUPS[g]
                    er = logit[:, 1, s0:s0 + k, :]
                    v.wait_ge(best_turned, g + 1)
                    need(v, rowed, 2 * (g - 1))
                    link(v.tensor_reduce(top[:, 0:k, :].rearrange("p k h -> p h k"), prow[:, :, 0:k, 0:P], op=ALU.max,
                                         axis=AX.X))
                    m = m_[:, 0:k, :]
                    link(v.tensor_tensor(m, top[:, 0:k, :], er, ALU.add))
                    link(v.scalar_tensor_tensor(m, m, LEAK, m, ALU.mult, ALU.max))
                    link(v.tensor_scalar(top[:, 0:k, :], top[:, 0:k, :], -BIG / 4, BIG, ALU.is_lt, ALU.mult))
                    link(v.tensor_tensor(m, m, top[:, 0:k, :], ALU.add))
                    v.tensor_scalar(r[:, g % 2, 0, 0:k, :], er, 1 - LEAK, None, ALU.mult)
                    v.scalar_tensor_tensor(r[:, g % 2, 1, 0:k, :], er, LEAK, m, ALU.mult, ALU.subtract).then_inc(rd, 1)
                    v.wait_ge(rd, g + 1)

                def rectify(u):
                    if not by_vector(u):
                        return
                    n, i = u // NB, u % NB
                    k, h, q = GROUPS[n // 2][1], n % 2, u % EB
                    v.wait_ge(row_out, n + 1)
                    need(v, leaked, u - EB + 1)
                    v.tensor_scalar(rect[:, q, 0:k * P], rows[:, n % 2, 0, 0:k * P], el_rest[:, i, h:h + 1], 0.0, ALU.add,
                                    ALU.max).then_inc(rectd_v, 1)

                def weigh(n, i):
                    s0, k = GROUPS[n // 2]
                    u = NB * n + i
                    q = u % EB
                    v.wait_ge(exps, u + 1)
                    need(v, used, u - EB + 1)
                    v.scalar_tensor_tensor(w[:, q, 0:k * P].rearrange("p (k d) -> p k d", d=P),
                                           e[:, q, 0:k * P].rearrange("p (k d) -> p k d", d=P), 1.0,
                                           C[:, s0:s0 + k, i, 0:P], ALU.min, ALU.mult).then_inc(weighed, 1)

                def beyond_cap(n, k):
                    with if_dense(v):
                        if n == 0:
                            v.sem_inc(x_used, 1)
                        with v.Fori(0, NB) as i:
                            v.wait_ge(beyond_in, i * 16 + 16 * (NB * n + 1))
                            v.wait_ge(x_exps, i + (NB * n + 1))
                            v.wait_ge(x_used, i + (NB * n + 1))
                            v.scalar_tensor_tensor(x_w[:, 0:k * P], x_e[:, 0:k * P], 1.0,
                                                   beyond[:, 0:k, :].rearrange("p k d -> p (k d)"), ALU.min,
                                                   ALU.mult).then_inc(x_weighed, 1)

                def divide(g, h):
                    k = GROUPS[g][1]
                    v.wait_ge(nturned, 2 * g + h + 1)
                    link(v.tensor_scalar(rec[:, 0:k, h, :], pot[:, 0:k, 64:65], 1e-20, None, ALU.max))
                    link(v.reciprocal(rec[:, 0:k, h, :], rec[:, 0:k, h, :]))
                    if h == 0:
                        need(v, oturned, g)
                    v.tensor_tensor(o[:, 0:k, h * 64:(h + 1) * 64], pot[:, 0:k, 0:64],
                                    rec[:, 0:k, h, :].broadcast_to((P, k, 64)), ALU.mult).then_inc(nturn_used, 1)

                for i in range(NB):
                    take_best(0, i)
                take_top(0)
                for u in range(AHEAD):
                    rectify(u)
                for g, s, h, i in group_steps():
                    n = 2 * g + h
                    if g < NG:
                        k = GROUPS[g][1]
                        if NB * n + i + AHEAD < 2 * NB * NG:
                            rectify(NB * n + i + AHEAD)
                        weigh(n, i)
                        if i == NB - 1:
                            beyond_cap(n, k)
                        if g + 1 < NG:
                            for i_ in mask_at(s):
                                take_best(g + 1, i_)
                            if s == 43:
                                take_top(g + 1)
                        if s == 39:
                            divide(g, 0)
                    if g:
                        s0, k = GROUPS[g - 1]
                        if s == 14:
                            divide(g - 1, 1)
                            v.wait_ge(nturn_used, 2 * g)
                            link(v.tensor_tensor(o[:, 0:k, :], o[:, 0:k, :],
                                                 bg[:].rearrange("p (a f) -> p a f", a=1).broadcast_to((P, k, 128)), ALU.add))
                            v.tensor_scalar(o[:, 0:k, :], o[:, 0:k, :], 0.0, None, ALU.max).then_inc(od, 1)
                        if s == 30:
                            v.wait_ge(lin, g)
                            need(v, normed, g - 1)
                            v.tensor_tensor(z[:, 0:k, :], pl[:, 0:k, :],
                                            bl[:].rearrange("p (a f) -> p a f", a=1).broadcast_to((P, k, D)),
                                            ALU.add).then_inc(lin_used, 1)
                            v.wait_ge(lin_used, g)
                            link(v.scalar_tensor_tensor(z[:, 0:k, :], z[:, 0:k, :], 0.0, X[:, s0:s0 + k, :], ALU.max, ALU.add))
                            for j in range(k):
                                m = v.bn_stats(st[:, j, :], z[:, j, :])
                            link(m)
                            for j in range(k):
                                m = v.bn_aggr(mv[:, j, :], st[:, j, :])
                            m.then_inc(stats, 1)
                        if s == 38:
                            v.wait_ge(root, g)
                            link(v.reciprocal(rs[:, 0:k], rs[:, 0:k]))
                            v.scalar_tensor_tensor(nm[:, 0:k], mv[:, 0:k, 0], -1.0, rs[:, 0:k], ALU.mult,
                                                   ALU.mult).then_inc(stats, 1)


def sort_edges(nc, own, dram, tab):
    sem = lambda n: own.semaphore("so_" + n)
    loaded, const, ranked, place, counted, turn, attr_in, slots, slots_seen, scattered = map(sem, (
        "loaded", "const", "ranked", "place", "counted", "turn", "attr_in", "slots", "slots_seen", "scattered"))
    LINKS = 6
    with ExitStack() as c, nc.Block() as block:
        sb = lambda n, s, d=F32: c.enter_context(nc.sbuf_tensor("so_" + n, s, d))
        dst_i = sb("dst_i", [P, EC], I32)
        dst, row = sb("dst", [P, EC]), sb("row", [P, EC, FIELDS])
        inb, rank, term, pos = (sb(n, [P, EC]) for n in ("inb", "rank", "term", "pos"))
        pos_i = sb("pos_i", [P, EC], U32)
        edge1 = sb("edge1", [P, EC])
        bound = sb("bound", [P, NB + 1])
        before, ones = sb("before", [P, P]), sb("ones", [P, P])
        off, base = sb("off", [P, 1]), sb("base", [P, 1])
        slot, row_slot, attr_slot = sb("slot", [P, 1], U32), sb("row_slot", [P, FIELDS]), sb("attr_slot", [P, AT])
        ps = c.enter_context(nc.psum_tensor("so_ps", [P, 2], F32))
        attr = dram["edge_attr_64"].rearrange("(p c) f -> p c f", c=EC)

        @block.sync
        def _(sp):
            unsorted = sp.value_load(tab["unsorted"][0:1, 0:1], min_val=0, max_val=1)
            with sp.If(unsorted != 0):
                sp.dma_start(dst_i[:], dram["dst"].rearrange("(p c) -> p c", c=EC)).then_inc(loaded, 16)
                sp.dma_start(row[:], dram["pairs"][0:E, :].rearrange("(p c) k -> p c k", c=EC)).then_inc(loaded, 16)
                sp.dma_start(attr_slot[:], attr[:, 0, :]).then_inc(attr_in, 16)
                with sp.Fori(1, EC) as col:
                    sp.wait_ge(scattered, col * 32)
                    sp.dma_start(attr_slot[:], attr[:, bass.ds(col, 1), :].rearrange("p a f -> p (a f)")).then_inc(attr_in, 16)

        @block.gpsimd
        def _(g):
            unsorted = g.value_load(tab["unsorted"][0:1, 0:1], min_val=0, max_val=1)
            with g.If(unsorted != 0):
                g.iota(bound[:], pattern=[[P, NB + 1]], base=0, channel_multiplier=0,
                       allow_small_or_imprecise_dtypes=True).then_inc(const, 1)
                g.memset(ones[:], 1.0).then_inc(const, 1)
                g.memset(before[:], 1.0).then_inc(const, 1)
                g.memset(edge1[:], 1.0).then_inc(const, 1)
                g.memset(pos[:], -1.0).then_inc(const, 1)
                g.memset(off[:], 0.0).then_inc(const, 1)
                g.wait_ge(const, 6)
                g.affine_select(out=before[:], in_=before[:], compare_op=ALU.is_gt, fill=0.0, base=0,
                                pattern=[[1, P]], channel_multiplier=-1).then_inc(const, 1)
                g.wait_ge(place, 1)
                with g.Fori(0, EC) as col:
                    g.tensor_copy(slot[:], pos_i[:, bass.ds(col, 1)]).then_inc(slots, 1)
                    g.tensor_copy(row_slot[:], row[:, bass.ds(col, 1), :].rearrange("p a k -> p (a k)")).then_inc(slots, 1)
                    g.wait_ge(slots, col * 2 + 2)
                    g.wait_ge(attr_in, col * 16 + 16)
                    g.sem_inc(slots_seen, 1)
                    for rows, out in ((row_slot, "pairs"), (attr_slot, "attr_s")):
                        g.indirect_dma_start(out=dram[out], out_offset=bass.IndirectOffsetOnAxis(ap=slot[:], axis=0),
                                             in_=rows[:], in_offset=None).then_inc(scattered, 16)
                    g.wait_ge(scattered, col * 32 + 32)
                    g.sem_inc(slots_seen, 1)

        @block.tensor
        def _(pe):
            unsorted = pe.value_load(tab["unsorted"][0:1, 0:1], min_val=0, max_val=1)
            with pe.If(unsorted != 0):
                pe.wait_ge(const, 7)
                with pe.Fori(0, NB) as b:
                    pe.wait_ge(ranked, b * LINKS + 3)
                    nc.tensor.matmul(ps[:, 0:1], before[:], rank[:, EC - 1:EC], start=True, stop=True)
                    nc.tensor.matmul(ps[:, 1:2], ones[:], rank[:, EC - 1:EC], start=True, stop=True).then_inc(counted, 1)

        @block.vector
        def _(v):
            unsorted = v.value_load(tab["unsorted"][0:1, 0:1], min_val=0, max_val=1)
            with v.If(unsorted != 0):
                v.wait_ge(loaded, 32)
                v.wait_ge(const, 7)
                v.tensor_copy(dst[:], dst_i[:]).then_inc(turn, 1)
                v.wait_ge(turn, 1)
                with v.Fori(0, NB) as b:
                    n = [0]

                    def link(ins):
                        n[0] += 1
                        ins.then_inc(ranked, 1)
                        v.wait_ge(ranked, b * LINKS + n[0])
                    link(v.tensor_scalar(term[:], dst[:], bound[:, bass.ds(b, 1)], None, ALU.is_ge))
                    link(v.scalar_tensor_tensor(inb[:], dst[:], bound[:, bass.ds(b + 1, 1)], term[:], ALU.is_lt, ALU.mult))
                    link(v.tensor_tensor_scan(rank[:], edge1[:], inb[:], 0.0, ALU.mult, ALU.add))
                    v.wait_ge(counted, b + 1)
                    link(v.tensor_tensor(base[:], ps[:, 0:1], off[:], ALU.add))
                    v.tensor_tensor(off[:], ps[:, 1:2], off[:], ALU.add)
                    link(v.scalar_tensor_tensor(term[:], rank[:], base[:], inb[:], ALU.add, ALU.mult))
                    link(v.tensor_tensor(pos[:], pos[:], term[:], ALU.add))
                v.tensor_copy(pos_i[:], pos[:]).then_inc(place, 1)


def graph_network(nc, dram):
    with ExitStack() as ctx:
        sb = lambda n, s, d=F32: ctx.enter_context(nc.sbuf_tensor(n, s, d))
        tab = dict(unsorted=sb("unsorted", [1, 1], I32),
                   tbeg=sb("tbeg", [1, NB], I32), tend=sb("tend", [1, NB], I32), bucket=sb("bucket", [1, NT], I32),
                   e0=sb("e0", [1, NT], I32), first=sb("first", [ET, NT]),
                   dense=sb("dense", [1, 1], I32), unscale=sb("unscale", [128, 2, 2]))
        for n in ("deg", "mean", "degmean", "dinv", "dinv_x"):
            tab[n] = sb(n, [P, NB])

        def phase(build, *args):
            own = Semaphores(nc)
            build(nc, own, *args)
            own.release()
        phase(index_tables, dram, tab)
        phase(sort_edges, dram, tab)
        tab["counts"] = sb("counts8", [P, NB, NB, 128], F8)
        tab["X"] = sb("X", [P, NB, D])
        with ExitStack() as c:
            tab["parts"] = [c.enter_context(nc.sbuf_tensor(f"part{i}", [P, NB * D], F16)) for i in range(3)]
            phase(count_edges, dram, tab, False)
            phase(count_edges, dram, tab, True)
            tab["parts"] += [c.enter_context(nc.sbuf_tensor(f"part{i}", [P, NB * D], F16)) for i in (3, 4)]
            rows = {n: c.enter_context(nc.sbuf_tensor("row_" + n, [P, 3, D], F32))
                    for n in ("b", "gamma", "beta")}
            phase(conv_layers, dram, tab, rows)
        tab["heads"] = sb("heads", [P, NB, 2, 65])
        tab["logit"] = sb("logit", [P, 2, NB, 2])
        with ExitStack() as c:
            tab["aggr"] = c.enter_context(nc.sbuf_tensor("aggr", [P, NB + 1, D], F32))
            phase(gated_messages, dram, tab)
            phase(update_nodes, dram, tab)
        phase(attention, dram, tab)


_INS = ["x", "src", "dst", "edge_attr_64", "L0_gnn_W", "L0_gnn_b", "L1_gnn_W", "L1_gnn_b", "L1_gnn_gamma",
        "L1_gnn_beta", "L2_gnn_W1", "L2_gnn_b1", "L2_gnn_W2", "L2_gnn_b2", "L2_gnn_U1", "L2_gnn_c1", "L2_gnn_U2",
        "L2_gnn_c2", "L3_gnn_W", "L3_gnn_attn_l", "L3_gnn_attn_r", "L3_gnn_gat_bias", "L3_gnn_lin_W",
        "L3_gnn_lin_b"]
_SCRATCH = [("pairs", (EPAD, FIELDS), F32), ("table", (N, D), F32),
            ("attr_s", (EPAD, AT), F32), ("beyond", (NB, P, N), F32)]


def declare(nc, arrays):
    dram = {n: nc.dram_tensor("in_" + n, a.shape, mybir.dt.from_np(a.dtype), kind="ExternalInput").ap()
            for n, a in arrays.items()}
    for n, shape, dt in _SCRATCH:
        dram[n] = nc.dram_tensor(n, shape, dt).ap()
    dram["out"] = nc.dram_tensor("out", (N, D), F32, kind="ExternalOutput").ap()
    return dram


def kernel(**inputs):
    import concourse.bacc as bacc
    from concourse.bass_utils import run_bass_kernel_spmd

    nc = bacc.Bacc("TRN2", target_bir_lowering=False, num_devices=1)
    arrays = {n: np.ascontiguousarray(inputs[n]) for n in _INS}
    graph_network(nc, declare(nc, arrays))
    r = run_bass_kernel_spmd(nc, [{"in_" + n: a for n, a in arrays.items()}], core_ids=[0])
    return r.results[0]["out"]
```
